# Optimizing a Trainium2 kernel written in Bass

```python
import numpy as np
import jax
import jax.numpy as jnp

def _softmax(x, axis=-1):
    return jax.nn.softmax(x, axis=axis)

def _gelu(x):
    return jax.nn.gelu(x, approximate=True)

def _silu(x):
    return jax.nn.silu(x)

def _sigmoid(x):
    return jax.nn.sigmoid(x)

def _layernorm(x, axis=-1, eps=1e-05):
    m = jnp.mean(x, axis=axis, keepdims=True)
    v = jnp.var(x, axis=axis, keepdims=True)
    return (x - m) / jnp.sqrt(v + eps)

def _scatter_add(tgt, idx, src, axis=0):
    return tgt.at[idx].add(src)

def _segment_sum(src, seg, n):
    return jax.ops.segment_sum(src, seg, n)
kernel_name = 'mk_seq_postln_d1_jaxref_r8_f053d9'

def setup_inputs(seed: int=0):
    np.random.seed(seed)
    _w = jnp.asarray

    def _L0_attn_setup():
        import jax, jax.numpy as jnp
        import numpy as np
        H = 16

        def _alibi_slopes(n):
            start = 2.0 ** (-2.0 ** (-(np.log2(n) - 3)))
            return np.array([start * start ** i for i in range(n)], dtype=np.float32)
        key = jax.random.key(seed)
        ks = jax.random.split(key, 6)
        B, L, C = (2, 256, 128)
        scale = 0.02
        return {'q': jax.random.normal(ks[0], (B, L, C), dtype=jnp.float32), 'Wq': jax.random.normal(ks[1], (C, C), dtype=jnp.float32) * scale, 'Wk': jax.random.normal(ks[2], (C, C), dtype=jnp.float32) * scale, 'Wv': jax.random.normal(ks[3], (C, C), dtype=jnp.float32) * scale, 'Wo': jax.random.normal(ks[4], (C, C), dtype=jnp.float32) * scale, 'bo': jax.random.normal(ks[5], (C,), dtype=jnp.float32) * scale}
    _L0_attn_in = _L0_attn_setup()

    def _L0_ffn_setup():
        import jax, jax.numpy as jnp
        import numpy as np
        DIM = 128
        DEPTH = 6
        HEADS = 16
        DIM_HEAD = 64
        WINDOW = 32
        INNER = HEADS * DIM_HEAD
        DIM_INNER = int(DIM * 4 * 2 / 3)
        QK_SCALE = 8.0

        def shift_tokens(t):
            a, s = jnp.split(t, 2, -1)
            s = jnp.pad(s, ((0, 0), (1, 0), (0, 0)))[:, :-1]
            return jnp.concatenate([a, s], -1)

        def l2norm(t):
            return t / jnp.maximum(jnp.linalg.norm(t, axis=-1, keepdims=True), 1e-12)

        def rotate_half(x):
            x1, x2 = jnp.split(x, 2, -1)
            return jnp.concatenate([-x2, x1], -1)

        def rotary_tables(n):
            half = jnp.arange(0, DIM_HEAD, 2, dtype=jnp.float32)
            inv_freq = 1.0 / 10000.0 ** (half / DIM_HEAD)
            t = jnp.arange(n, dtype=jnp.float32)
            freqs = t[:, None] * inv_freq[None, :]
            freqs = jnp.concatenate([freqs, freqs], -1)
            base_scale = (half + 0.4 * DIM_HEAD) / (1.4 * DIM_HEAD)
            power = (t - n // 2) / (WINDOW // 2)
            scale = base_scale[None, :] ** power[:, None]
            scale = jnp.concatenate([scale, scale], -1)
            return (freqs, scale)

        def local_attention(q, k, v):
            b, h, n, d = q.shape
            w = WINDOW
            nw = n // w
            bq = q.reshape(b, h, nw, w, d)
            bk = k.reshape(b, h, nw, w, d)
            bv = v.reshape(b, h, nw, w, d)

            def look(t):
                p = jnp.pad(t, ((0, 0), (0, 0), (1, 0), (0, 0), (0, 0)))
                return jnp.concatenate([p[:, :, :nw], p[:, :, 1:]], axis=3)
            bk2, bv2 = (look(bk), look(bv))
            seq = jnp.arange(n).reshape(nw, w)
            seq_p = jnp.pad(seq, ((1, 0), (0, 0)), constant_values=-1)
            jt = jnp.concatenate([seq_p[:nw], seq_p[1:]], axis=1)
            it = seq[:, :, None]
            jb = jt[:, None, :]
            mask = (it < jb) | (it > jb + w) | (jb == -1)
            sim = jnp.einsum('bhwie,bhwje->bhwij', bq, bk2) * QK_SCALE
            sim = jnp.where(mask, -jnp.finfo(sim.dtype).max, sim)
            attn = jax.nn.softmax(sim, -1)
            out = jnp.einsum('bhwij,bhwje->bhwie', attn, bv2)
            return out.reshape(b, h, n, d)

        def attn_layer(x, Wqkv, qs, ksc, Wo):
            b, n, _ = x.shape
            qkv = x @ Wqkv
            q, k, v = jnp.split(qkv, 3, -1)
            sh = lambda t: t.reshape(b, n, HEADS, DIM_HEAD).transpose(0, 2, 1, 3)
            q, k, v = (sh(q), sh(k), sh(v))
            q = l2norm(q) * qs
            k = l2norm(k) * ksc
            freqs, scale = rotary_tables(n)
            cos, sin = (jnp.cos(freqs), jnp.sin(freqs))
            q = q * cos * scale + rotate_half(q) * sin * scale
            inv = 1.0 / scale
            k = k * cos * inv + rotate_half(k) * sin * inv
            out = local_attention(q, k, v)
            out = out.transpose(0, 2, 1, 3).reshape(b, n, INNER)
            return out @ Wo

        def ffn_layer(x, g, bln, W1, b1, W2, b2):
            mu = x.mean(-1, keepdims=True)
            var = ((x - mu) ** 2).mean(-1, keepdims=True)
            xn = (x - mu) / jnp.sqrt(var + 1e-05) * g + bln
            hg = xn @ W1 + b1
            a, gate = jnp.split(hg, 2, -1)
            return a * jax.nn.gelu(gate, approximate=False) @ W2 + b2
        key = jax.random.key(seed)
        ks = jax.random.split(key, 8)
        B, N = (2, 256)
        init = lambda k, shape: jax.random.normal(k, shape, jnp.float32) * 0.02
        return {'x': jax.random.normal(ks[0], (B, N, DIM), jnp.float32), 'Wqkv': init(ks[1], (DEPTH, DIM, 3 * INNER)), 'q_scale': jnp.ones((DEPTH, DIM_HEAD), jnp.float32), 'k_scale': jnp.ones((DEPTH, DIM_HEAD), jnp.float32), 'Wo': init(ks[2], (DEPTH, INNER, DIM)), 'ln_g': jnp.ones((DEPTH, DIM), jnp.float32), 'ln_b': jnp.zeros((DEPTH, DIM), jnp.float32), 'W1': init(ks[3], (DEPTH, DIM, 2 * DIM_INNER)), 'b1': jnp.zeros((DEPTH, 2 * DIM_INNER), jnp.float32), 'W2': init(ks[4], (DEPTH, DIM_INNER, DIM)), 'b2': jnp.zeros((DEPTH, DIM), jnp.float32)}
    _L0_ffn_in = _L0_ffn_setup()
    _d = {'L0_attn_q': _L0_attn_in['q'], 'L0_attn_Wq': _L0_attn_in['Wq'], 'L0_attn_Wk': _L0_attn_in['Wk'], 'L0_attn_Wv': _L0_attn_in['Wv'], 'L0_attn_Wo': _L0_attn_in['Wo'], 'L0_attn_bo': _L0_attn_in['bo'], 'L0_ffn_Wqkv': _L0_ffn_in['Wqkv'], 'L0_ffn_q_scale': _L0_ffn_in['q_scale'], 'L0_ffn_k_scale': _L0_ffn_in['k_scale'], 'L0_ffn_Wo': _L0_ffn_in['Wo'], 'L0_ffn_ln_g': _L0_ffn_in['ln_g'], 'L0_ffn_ln_b': _L0_ffn_in['ln_b'], 'L0_ffn_W1': _L0_ffn_in['W1'], 'L0_ffn_b1': _L0_ffn_in['b1'], 'L0_ffn_W2': _L0_ffn_in['W2'], 'L0_ffn_b2': _L0_ffn_in['b2']}
    _x0 = _d['L0_attn_q']
    _d['L0_attn_q'] = jax.random.normal(jax.random.fold_in(jax.random.key(seed), 1), (4, 512, 128), dtype=_x0.dtype)
    del _x0
    return _d

def reference(L0_attn_q, L0_attn_Wq, L0_attn_Wk, L0_attn_Wv, L0_attn_Wo, L0_attn_bo, L0_ffn_Wqkv, L0_ffn_q_scale, L0_ffn_k_scale, L0_ffn_Wo, L0_ffn_ln_g, L0_ffn_ln_b, L0_ffn_W1, L0_ffn_b1, L0_ffn_W2, L0_ffn_b2):

    def _L0_attn_ref(q, Wq, Wk, Wv, Wo, bo):
        import jax, jax.numpy as jnp
        import numpy as np
        H = 16

        def _alibi_slopes(n):
            start = 2.0 ** (-2.0 ** (-(np.log2(n) - 3)))
            return np.array([start * start ** i for i in range(n)], dtype=np.float32)
        B, L, C = q.shape
        D = C // H
        inv_sqrt_d = jnp.asarray(D, q.dtype) ** (-0.5)

        def proj(x, W):
            return (x @ W.T).reshape(B, L, H, D).transpose(0, 2, 1, 3)
        qh, kh, vh = (proj(q, Wq), proj(q, Wk), proj(q, Wv))
        pos = jnp.arange(L)
        rel = jnp.abs(pos[None, :] - pos[:, None]).astype(q.dtype)
        slopes = jnp.asarray(_alibi_slopes(H), dtype=q.dtype)
        bias = (-slopes)[:, None, None] * rel
        scores = jnp.einsum('bhld,bhsd->bhls', qh, kh) * inv_sqrt_d + bias[None]
        attn = jax.nn.softmax(scores, axis=-1)
        out = jnp.einsum('bhls,bhsd->bhld', attn, vh)
        out = out.transpose(0, 2, 1, 3).reshape(B, L, C)
        return out @ Wo.T + bo

    def _L0_ffn_ref(x, Wqkv, q_scale, k_scale, Wo, ln_g, ln_b, W1, b1, W2, b2):
        import jax, jax.numpy as jnp
        import numpy as np
        DIM = 128
        DEPTH = 6
        HEADS = 16
        DIM_HEAD = 64
        WINDOW = 32
        INNER = HEADS * DIM_HEAD
        DIM_INNER = int(DIM * 4 * 2 / 3)
        QK_SCALE = 8.0

        def shift_tokens(t):
            a, s = jnp.split(t, 2, -1)
            s = jnp.pad(s, ((0, 0), (1, 0), (0, 0)))[:, :-1]
            return jnp.concatenate([a, s], -1)

        def l2norm(t):
            return t / jnp.maximum(jnp.linalg.norm(t, axis=-1, keepdims=True), 1e-12)

        def rotate_half(x):
            x1, x2 = jnp.split(x, 2, -1)
            return jnp.concatenate([-x2, x1], -1)

        def rotary_tables(n):
            half = jnp.arange(0, DIM_HEAD, 2, dtype=jnp.float32)
            inv_freq = 1.0 / 10000.0 ** (half / DIM_HEAD)
            t = jnp.arange(n, dtype=jnp.float32)
            freqs = t[:, None] * inv_freq[None, :]
            freqs = jnp.concatenate([freqs, freqs], -1)
            base_scale = (half + 0.4 * DIM_HEAD) / (1.4 * DIM_HEAD)
            power = (t - n // 2) / (WINDOW // 2)
            scale = base_scale[None, :] ** power[:, None]
            scale = jnp.concatenate([scale, scale], -1)
            return (freqs, scale)

        def local_attention(q, k, v):
            b, h, n, d = q.shape
            w = WINDOW
            nw = n // w
            bq = q.reshape(b, h, nw, w, d)
            bk = k.reshape(b, h, nw, w, d)
            bv = v.reshape(b, h, nw, w, d)

            def look(t):
                p = jnp.pad(t, ((0, 0), (0, 0), (1, 0), (0, 0), (0, 0)))
                return jnp.concatenate([p[:, :, :nw], p[:, :, 1:]], axis=3)
            bk2, bv2 = (look(bk), look(bv))
            seq = jnp.arange(n).reshape(nw, w)
            seq_p = jnp.pad(seq, ((1, 0), (0, 0)), constant_values=-1)
            jt = jnp.concatenate([seq_p[:nw], seq_p[1:]], axis=1)
            it = seq[:, :, None]
            jb = jt[:, None, :]
            mask = (it < jb) | (it > jb + w) | (jb == -1)
            sim = jnp.einsum('bhwie,bhwje->bhwij', bq, bk2) * QK_SCALE
            sim = jnp.where(mask, -jnp.finfo(sim.dtype).max, sim)
            attn = jax.nn.softmax(sim, -1)
            out = jnp.einsum('bhwij,bhwje->bhwie', attn, bv2)
            return out.reshape(b, h, n, d)

        def attn_layer(x, Wqkv, qs, ksc, Wo):
            b, n, _ = x.shape
            qkv = x @ Wqkv
            q, k, v = jnp.split(qkv, 3, -1)
            sh = lambda t: t.reshape(b, n, HEADS, DIM_HEAD).transpose(0, 2, 1, 3)
            q, k, v = (sh(q), sh(k), sh(v))
            q = l2norm(q) * qs
            k = l2norm(k) * ksc
            freqs, scale = rotary_tables(n)
            cos, sin = (jnp.cos(freqs), jnp.sin(freqs))
            q = q * cos * scale + rotate_half(q) * sin * scale
            inv = 1.0 / scale
            k = k * cos * inv + rotate_half(k) * sin * inv
            out = local_attention(q, k, v)
            out = out.transpose(0, 2, 1, 3).reshape(b, n, INNER)
            return out @ Wo

        def ffn_layer(x, g, bln, W1, b1, W2, b2):
            mu = x.mean(-1, keepdims=True)
            var = ((x - mu) ** 2).mean(-1, keepdims=True)
            xn = (x - mu) / jnp.sqrt(var + 1e-05) * g + bln
            hg = xn @ W1 + b1
            a, gate = jnp.split(hg, 2, -1)
            return a * jax.nn.gelu(gate, approximate=False) @ W2 + b2
        for i in range(DEPTH):
            x = attn_layer(shift_tokens(x), Wqkv[i], q_scale[i], k_scale[i], Wo[i]) + x
            x = ffn_layer(shift_tokens(x), ln_g[i], ln_b[i], W1[i], b1[i], W2[i], b2[i]) + x
        return x
    x = L0_attn_q
    x = _layernorm(x + _L0_attn_ref(x, L0_attn_Wq, L0_attn_Wk, L0_attn_Wv, L0_attn_Wo, L0_attn_bo), axis=-1)
    x = _layernorm(x + _L0_ffn_ref(x, L0_ffn_Wqkv, L0_ffn_q_scale, L0_ffn_k_scale, L0_ffn_Wo, L0_ffn_ln_g, L0_ffn_ln_b, L0_ffn_W1, L0_ffn_b1, L0_ffn_W2, L0_ffn_b2), axis=-1)
    return x

_drawn_inputs = setup_inputs


def setup_inputs(seed=0):
    import zlib

    import numpy as np

    out = dict(_drawn_inputs(seed))
    spreads = {'L0_ffn_q_scale': (1.0, 0.6),
     'L0_ffn_k_scale': (1.0, 0.6),
     'L0_ffn_ln_g': (1.0, 0.6),
     'L0_ffn_ln_b': (0.0, 0.8),
     'L0_ffn_b1': (0.0, 0.8),
     'L0_ffn_b2': (0.0, 0.1)}
    factors = {'L0_attn_Wq': 8.0,
     'L0_attn_Wk': 8.0,
     'L0_attn_Wv': 5.514,
     'L0_attn_Wo': 5.657,
     'L0_ffn_W1': 3.671,
     'L0_ffn_W2': 3.605}
    for name, (base, spread) in spreads.items():
        noise = np.random.default_rng([zlib.crc32(name.encode()), seed]).standard_normal(out[name].shape)
        drawn = base * np.exp(spread * noise) if base else spread * noise
        out[name] = jnp.asarray(drawn.astype(out[name].dtype))
    for name, factor in factors.items():
        out[name] = (out[name] * factor).astype(out[name].dtype)
    return out
```

```python
from contextlib import ExitStack

import numpy as np

import concourse.bass as bass
from concourse import mybir

F32 = mybir.dt.float32
BF16 = mybir.dt.bfloat16
F16 = mybir.dt.float16
U16 = mybir.dt.uint16
ALU = mybir.AluOpType
ACT = mybir.ActivationFunctionType
AX = mybir.AxisListType

P = 128
B, L, C = 4, 512, 128
TPB = L // P
TPL = B * TPB
LN_EPS = 1e-5
XW = L + 8

AH, AD = 16, 8
AROWS = 64 + 36
STEPS = 2 * 3 + 4 * 3

DEPTH = 6
TILES = DEPTH * TPL
HEADS, DH = 16, 64
INNER = HEADS * DH
PAIRS = HEADS // 2
WIN = 32
WPT = P // WIN
FF = int(C * 4 * 2 / 3)
LOADS = 7
FIRST, LAG = 4, 3



def alibi_attention(nc, args, state):
    x, eye, wqkvT, woT, bo, q_const, k_const, relu_const, slope_const = args
    x_shift, x1_tok, ident, identb, halfneg, eps = state
    with ExitStack() as ctx:
        def sb(name, shape, dt=F32):
            return ctx.enter_context(nc.sbuf_tensor(name, shape, dt))

        def sem(name):
            return ctx.enter_context(nc.semaphore(name))

        w_sb = sb("a_w", [P, 3 * C])
        wo_sb = sb("a_wo", [P, C])
        bo_sb = sb("a_bo", [P, C])
        relu_sb = sb("a_relu", [P, 2, P], F16)
        slope_sb = sb("a_slope", [P, AH, 2, P], F16)
        qT = sb("a_qT", [AROWS, AH, L], BF16)
        kT = sb("a_kT", [AROWS, AH, L], BF16)
        q_tok = sb("a_q_tok", [P, TPB, AH, 64], BF16)
        k_tok = sb("a_k_tok", [P, TPB, AH, 64], BF16)
        rest = sb("a_rest", [P, 2, TPB, C])
        v_ext = sb("a_v_ext", [P, TPB, AH, 32])
        x_in = sb("a_x_in", [P, TPB, P])
        xT = sb("a_xT", [P, TPB, P])
        negmax = sb("a_negmax", [P, TPB, 4])
        m_rest = sb("a_m_rest", [P, TPB, 4])
        m_tok = sb("a_m_tok", [P, TPB, 3, 4], BF16)
        mT = sb("a_mT", [12, L], BF16)
        prob = sb("a_prob", [P, 2, 4, L])
        oT = sb("a_oT", [P, L])
        rden = sb("a_rden", [P, TPB, 4])
        o_tok = sb("a_o_tok", [P, TPB, AH, AD])
        ocT = sb("a_ocT", [P, TPB, P])
        total = sb("a_total", [P, TPB, P])
        stats = sb("a_stats", [P, TPB, 6])
        mv = sb("a_mv", [P, TPB, 2])
        rstd = sb("a_rstd", [P, TPB])
        x1 = sb("a_x1", [P, TPB, P])
        max_bank = [ctx.enter_context(nc.psum_tensor(f"a_max{i}", [P, L], F32)) for i in range(2)]
        sT_bank = ctx.enter_context(nc.psum_tensor("a_sT", [P, 4, L], F32))
        o_bank = ctx.enter_context(nc.psum_tensor("a_o", [P, L], F32))
        misc = ctx.enter_context(nc.psum_tensor("a_misc", [P, TPB, P], F32))

        loaded, boot, k_zero, step_ok = sem("a_loaded"), sem("a_boot"), sem("a_k_zero"), sem("a_step_ok")
        xin_ok, xT_mm, xT_ok, qkv_mm, v_ok, split_ok, chain = map(
            sem, ["a_xin_ok", "a_xT_mm", "a_xT_ok", "a_qkv_mm", "a_v_ok", "a_split_ok", "a_chain"])
        turn_mm, qT_ok, kT_ok, p1_mm, max_ok, m_ok, m_mm, mT_ok, mrow_ok = map(
            sem, ["a_turn_mm", "a_qT_ok", "a_kT_ok", "a_p1_mm", "a_max_ok", "a_m_ok", "a_m_mm", "a_mT_ok", "a_mrow_ok"])
        sT_mm, exp_ok, o_mm, oT_ok, back_mm, rden_ok, o_ok, oc_mm, oc_ok, y_mm = map(
            sem, ["a_sT_mm", "a_exp_ok", "a_o_mm", "a_oT_ok", "a_back_mm", "a_rden_ok", "a_o_ok", "a_oc_mm", "a_oc_ok", "a_y_mm"])
        sum_ok, res_ok, bn_ok, mv_ok, eps_ok, rstd_ok, x1_ok, x1T_mm, xw_ok = map(
            sem, ["a_sum_ok", "a_res_ok", "a_bn_ok", "a_mv_ok", "a_eps_ok", "a_rstd_ok", "a_x1_ok", "a_x1T_mm", "a_xw_ok"])

        def upto(eng, s, b, per_batch, count):
            n = b * per_batch + count
            if isinstance(n, int) and n <= 0:
                return
            eng.wait_ge(s, n)

        def run(eng, batch):
            batch(0)
            with eng.Fori(1, B) as b:
                batch(b)

        def rows(b):
            return x1_tok[:, bass.ds(b * TPB, TPB), :]

        block = ctx.enter_context(nc.Block())

        @block.sync
        def _(sp):
            sp.dma_start(ident[:], eye).then_inc(loaded, 16)
            sp.dma_start(x1_tok[:], x.rearrange("b (t p) c -> p (b t) c", p=P)).then_inc(loaded, 16)
            sp.dma_start(w_sb[:], wqkvT).then_inc(loaded, 16)
            sp.dma_start(wo_sb[:], woT).then_inc(loaded, 16)
            sp.dma_start(bo_sb[:], bo.broadcast_to([P, C])).then_inc(loaded, 16)
            sp.dma_start(qT[64:AROWS].bitcast(U16), q_const).then_inc(loaded, 16)
            sp.dma_start(kT[64:AROWS].bitcast(U16), k_const).then_inc(loaded, 16)
            sp.dma_start(relu_sb[:].bitcast(U16), relu_const).then_inc(loaded, 16)
            sp.dma_start(slope_sb[:].bitcast(U16), slope_const).then_inc(loaded, 16)

            def batch(b):
                for g in range(4):
                    upto(sp, mT_ok, b, 4, g + 1)
                    for piece in range(3):
                        sp.dma_start(qT[48 + piece:49 + piece, 4 * g:4 * g + 4, :], mT[4 * piece:4 * piece + 4, :]
                                     ).then_inc(mrow_ok, 16)

            run(sp, batch)
            sp.wait_ge(mrow_ok, B * 4 * 3 * 16)

        @block.tensor
        def _(pe):
            def first_pass(b, g, i):
                for n in range(4):
                    h, u = 4 * g + n, 16 * g + 4 * i + n
                    upto(pe, max_ok, b, 64, u - 1)
                    out = max_bank[u % 2]
                    pe.matmul(out[:], qT[:, h, i * P:(i + 1) * P], kT[:, h, :], start=True, stop=True)
                    for piece in range(2):
                        last = pe.matmul(out[:, i * P:(i + 1) * P], relu_sb[:, 0, :], slope_sb[:, h, piece, :],
                                         start=False, stop=True, skip_group_check=True)
                    last.then_inc(p1_mm, 1)

            def turn_maxima(b, g):
                upto(pe, m_ok, b, 4, g + 1)
                if g:
                    upto(pe, o_ok, b, 4, g)
                for t in range(TPB):
                    last = pe.matmul(misc[0:12, 0:2, :].bitcast(BF16).rearrange("p a n -> p (a n)")[
                        :, t * P:(t + 1) * P],
                        m_tok[:, t].rearrange("p a h -> p (a h)"), identb[:], start=True, stop=True,
                        is_transpose=True)
                last.then_inc(m_mm, 1)

            def scores(b, g, j):
                if j == 0:
                    pe.wait_ge(mrow_ok, (b * 4 + g + 1) * 48)
                for half in range(2):
                    u = 8 * g + 2 * j + half
                    upto(pe, exp_ok, b, 32, u - 1)
                    for n in range(2):
                        h = 4 * g + 2 * half + n
                        out = sT_bank[:, 2 * half + n, :]
                        pe.matmul(out, kT[:, h, j * P:(j + 1) * P], qT[:, h, :], start=True, stop=True)
                        for piece in range(2):
                            last = pe.matmul(out[:, j * P:(j + 1) * P], relu_sb[:, 1, :], slope_sb[:, h, piece, :],
                                             start=False, stop=True, skip_group_check=True)
                    last.then_inc(sT_mm, 1)

            def weigh(b, g, j):
                upto(pe, exp_ok, b, 32, 8 * g + 2 * j + 2)
                if j == 0:
                    upto(pe, oT_ok, b, 4, g)
                for n in range(4):
                    last = pe.matmul(o_bank[32 * n:32 * n + 32, :], v_ext[:, j, 4 * g + n, :],
                                     prob[:, j % 2, n, :], start=(j == 0), stop=(j == TPB - 1),
                                     skip_group_check=True)
                last.then_inc(o_mm, 1)

            def turn_back(b, g):
                upto(pe, oT_ok, b, 4, g + 1)
                upto(pe, mT_ok, b, 4, g + 1)
                for t in range(TPB):
                    last = pe.matmul(misc[:, t, :], oT[:, t * P:(t + 1) * P], ident[:], start=True, stop=True,
                                     is_transpose=True)
                last.then_inc(back_mm, 1)

            def batch(b):
                upto(pe, xin_ok, b, 1, 1)
                upto(pe, xw_ok, b, 1, 0)
                for t in range(TPB):
                    last = pe.matmul(misc[:, t, :], x_in[:, t, :], ident[:], start=True, stop=True, is_transpose=True)
                last.then_inc(xT_mm, 1)
                upto(pe, xT_ok, b, 1, 1)
                upto(pe, exp_ok, b, 32, 0)
                for t in range(TPB):
                    last = pe.matmul(sT_bank[:, t, 0:3 * C], xT[:, t, :], w_sb[:], start=True, stop=True)
                last.then_inc(qkv_mm, 1)
                for n in range(8):
                    src = q_tok if n < 4 else k_tok
                    if n == 0:
                        upto(pe, split_ok, b, 2, 2)
                        upto(pe, v_ok, b, 1, 1)
                    if n >= 4:
                        upto(pe, qT_ok, b, 4, n - 3)
                    for k in range(2):
                        p = 2 * (n % 4) + k
                        for t in range(TPB):
                            last = pe.matmul(sT_bank[:, n % 4, :].bitcast(BF16)[:, (4 * k + t) * P:(4 * k + t + 1) * P],
                                             src[:, t, 2 * p:2 * p + 2, :].rearrange("p h n -> p (h n)"), identb[:],
                                             start=True, stop=True, is_transpose=True)
                    last.then_inc(turn_mm, 1)
                upto(pe, qT_ok, b, 4, 4)
                upto(pe, kT_ok, b, 4, 4)
                for i in range(TPB):
                    first_pass(b, 0, i)
                for g in range(4):
                    if g < 3:
                        first_pass(b, g + 1, 0)
                    if g:
                        turn_back(b, g - 1)
                    turn_maxima(b, g)
                    if g < 3:
                        first_pass(b, g + 1, 1)
                    for j in range(TPB):
                        scores(b, g, j)
                        if g < 3 and j < 2:
                            first_pass(b, g + 1, j + 2)
                        weigh(b, g, j)
                turn_back(b, 3)
                upto(pe, o_ok, b, 4, 4)
                for t in range(TPB):
                    last = pe.matmul(misc[:, t, :], o_tok[:, t].rearrange("p h d -> p (h d)"), ident[:],
                                     start=True, stop=True, is_transpose=True)
                last.then_inc(oc_mm, 1)
                upto(pe, oc_ok, b, 1, 1)
                for t in range(TPB):
                    last = pe.matmul(misc[:, t, :], ocT[:, t, :], wo_sb[:], start=True, stop=True)
                last.then_inc(y_mm, 1)
                upto(pe, x1_ok, b, 1, 1)
                upto(pe, sum_ok, b, 1, 1)
                for t in range(TPB):
                    last = pe.matmul(misc[:, t, :], x1[:, t, :], ident[:], start=True, stop=True, is_transpose=True)
                last.then_inc(x1T_mm, 1)

            pe.wait_ge(loaded, 16 * 9)
            pe.wait_ge(boot, 4)
            run(pe, batch)

        @block.scalar
        def _(act):
            def copy(out, in_):
                return act.activation(out, in_, ACT.Copy)

            def batch(b):
                upto(act, xT_mm, b, 1, 0)
                copy(x_in[:], rows(b)).then_inc(xin_ok, 1)
                upto(act, xT_mm, b, 1, 1)
                upto(act, qkv_mm, b, 1, 0)
                copy(xT[:], misc[:]).then_inc(xT_ok, 1)
                upto(act, qkv_mm, b, 1, 1)
                upto(act, o_mm, b, 16, 0)
                for t in range(TPB):
                    last = copy(v_ext[:, t, :, 0:AD], sT_bank[:, t, 2 * C:3 * C].rearrange("p (h d) -> p h d", d=AD))
                last.then_inc(v_ok, 1)
                for n in range(4):
                    upto(act, turn_mm, b, 8, n + 1)
                    for a in range(2):
                        src = sT_bank[64 * a:64 * a + 64, n, :].bitcast(BF16).rearrange("p (k l) -> p k l", k=2)
                        last = copy(qT[0:64, 4 * n + a:4 * n + a + 3:2, :], src)
                    last.then_inc(qT_ok, 1)
                for g in range(4):
                    upto(act, m_mm, b, 4, g + 1)
                    copy(mT[:], misc[0:12, 0:2, :].bitcast(BF16).rearrange("p a n -> p (a n)")).then_inc(mT_ok, 1)
                    for j in range(TPB):
                        for half in range(2):
                            u = 8 * g + 2 * j + half
                            upto(act, sT_mm, b, 32, u + 1)
                            upto(act, o_mm, b, 16, 4 * g + j - 1)
                            act.activation(prob[:, j % 2, 2 * half:2 * half + 2, :],
                                           sT_bank[:, 2 * half:2 * half + 2, :], ACT.Exp).then_inc(exp_ok, 1)
                    upto(act, o_mm, b, 16, 4 * g + 4)
                    upto(act, back_mm, b, 4, g)
                    copy(oT[:], o_bank[:]).then_inc(oT_ok, 1)
                upto(act, oc_mm, b, 1, 1)
                copy(ocT[:], misc[:]).then_inc(oc_ok, 1)

            act.wait_ge(loaded, 16 * 9)
            act.wait_ge(boot, 4)
            run(act, batch)

        @block.gpsimd
        def _(pool):
            pool.memset(x_shift[:], 0.0)
            pool.memset(halfneg[:], -0.5)
            pool.memset(eps[:], LN_EPS)
            pool.memset(v_ext[:].rearrange("p t h n -> p (t h n)"), 0.0).then_inc(chain, 1)
            pool.wait_ge(chain, 1)
            pool.memset(v_ext[:, :, :, AD:AD + 1], 1.0).then_inc(boot, 1)

            def batch(b):
                upto(pool, mv_ok, b, 1, 1)
                upto(pool, x1_ok, b, 1, 0)
                pool.tensor_tensor(rstd[:], mv[:, :, 1], eps[:, 0:TPB], ALU.add).then_inc(eps_ok, 1)
                upto(pool, eps_ok, b, 1, 1)
                pool.tensor_tensor(rstd[:], rstd[:], halfneg[:, 0:TPB], ALU.pow).then_inc(rstd_ok, 1)

            run(pool, batch)

        @block.vector
        def _(dve):
            def split(b, part, tok, slots, scale):
                src = sT_bank[:, :, part * C:(part + 1) * C].rearrange("p t (h d) -> p t h d", d=AD)

                def place(n):
                    return tok[:, :, :, n * AD:(n + 1) * AD]

                high, mid, low = slots
                r = rest[:, part].rearrange("p t (h d) -> p t h d", d=AD)
                for t in range(TPB):
                    last = dve.tensor_scalar(place(high[0])[:, t], src[:, t], scale, None, ALU.mult)
                last.then_inc(step_ok, 1)
                upto(dve, step_ok, b, STEPS, 3 * part + 1)
                for t in range(TPB):
                    last = dve.scalar_tensor_tensor(r[:, t], src[:, t], scale, place(high[0])[:, t], ALU.mult,
                                                    ALU.subtract)
                last.then_inc(step_ok, 1)
                upto(dve, step_ok, b, STEPS, 3 * part + 2)
                for t in range(TPB):
                    last = dve.tensor_copy(place(mid[0])[:, t], r[:, t])
                last.then_inc(step_ok, 1)
                upto(dve, step_ok, b, STEPS, 3 * part + 3)
                for t in range(TPB):
                    last = dve.tensor_tensor(place(low[0])[:, t], r[:, t], place(mid[0])[:, t], ALU.subtract)
                for again in high[1:]:
                    for t in range(TPB):
                        last = dve.tensor_copy(place(again)[:, t], place(high[0])[:, t])
                for again in mid[1:]:
                    for t in range(TPB):
                        last = dve.tensor_copy(place(again)[:, t], place(mid[0])[:, t])
                last.then_inc(split_ok, 1)

            def maxima(b, g, i):
                for n in range(4):
                    u = 16 * g + 4 * i + n
                    upto(dve, p1_mm, b, 64, u + 1)
                    if i == 0 and n == 0:
                        upto(dve, m_ok, b, 4, g)
                    dve.tensor_reduce(negmax[:, i, n:n + 1], max_bank[u % 2][:], AX.X, ALU.max,
                                      negate=True).then_inc(max_ok, 1)

            def split_maxima(b, g):
                upto(dve, max_ok, b, 64, 16 * g + 16)
                upto(dve, m_mm, b, 4, g)
                n = 6 + 3 * g
                dve.tensor_copy(m_tok[:, :, 0, :], negmax[:]).then_inc(step_ok, 1)
                upto(dve, step_ok, b, STEPS, n + 1)
                dve.tensor_tensor(m_rest[:], negmax[:], m_tok[:, :, 0, :], ALU.subtract).then_inc(step_ok, 1)
                upto(dve, step_ok, b, STEPS, n + 2)
                dve.tensor_copy(m_tok[:, :, 1, :], m_rest[:]).then_inc(step_ok, 1)
                upto(dve, step_ok, b, STEPS, n + 3)
                dve.tensor_tensor(m_tok[:, :, 2, :], m_rest[:], m_tok[:, :, 1, :], ALU.subtract).then_inc(m_ok, 1)

            def divide(b, g):
                upto(dve, back_mm, b, 4, g + 1)
                upto(dve, o_ok, b, 4, g)
                src = misc[:].rearrange("p t (h n) -> p t h n", n=32)
                dve.reciprocal(rden[:], src[:, :, :, AD]).then_inc(rden_ok, 1)
                upto(dve, rden_ok, b, 4, g + 1)
                if g == 0:
                    upto(dve, oc_mm, b, 1, 0)
                dve.tensor_tensor(o_tok[:, :, 4 * g:4 * g + 4, :], src[:, :, :, 0:AD],
                                  rden[:].unsqueeze(3).broadcast_to([P, TPB, 4, AD]), ALU.mult).then_inc(o_ok, 1)

            def batch(b):
                upto(dve, qkv_mm, b, 1, 1)
                upto(dve, turn_mm, b, 8, 0)
                upto(dve, v_ok, b, 1, 1)
                split(b, 0, q_tok, ((0, 1, 4), (2, 3), (5,)), float(AD) ** -0.5)
                split(b, 1, k_tok, ((0, 2, 5), (1, 3), (4,)), 1.0)
                for n in range(4):
                    upto(dve, turn_mm, b, 8, n + 5)
                    for a in range(2):
                        src = sT_bank[64 * a:64 * a + 64, n, :].bitcast(BF16).rearrange("p (k l) -> p k l", k=2)
                        last = dve.tensor_copy(kT[0:64, 4 * n + a:4 * n + a + 3:2, :], src)
                    last.then_inc(kT_ok, 1)
                for i in range(TPB):
                    maxima(b, 0, i)
                split_maxima(b, 0)
                for g in range(4):
                    if g < 3:
                        maxima(b, g + 1, 0)
                    if g:
                        divide(b, g - 1)
                    if g < 3:
                        for i in range(1, TPB):
                            maxima(b, g + 1, i)
                        split_maxima(b, g + 1)
                divide(b, 3)
                upto(dve, y_mm, b, 1, 1)
                dve.tensor_tensor(total[:], misc[:], rows(b), ALU.add).then_inc(sum_ok, 1)
                upto(dve, sum_ok, b, 1, 1)
                dve.tensor_tensor(total[:], total[:], bo_sb[:].unsqueeze(1).broadcast_to([P, TPB, C]),
                                  ALU.add).then_inc(res_ok, 1)
                upto(dve, res_ok, b, 1, 1)
                upto(dve, rstd_ok, b, 1, 0)
                for t in range(TPB):
                    last = dve.bn_stats(stats[:, t, :], total[:, t, :])
                last.then_inc(bn_ok, 1)
                dve.wait_ge(boot, 4)
                upto(dve, bn_ok, b, 1, 1)
                for t in range(TPB):
                    last = dve.bn_aggr(mv[:, t, :], stats[:, t, :])
                last.then_inc(mv_ok, 1)
                upto(dve, rstd_ok, b, 1, 1)
                upto(dve, x1T_mm, b, 1, 0)
                for t in range(TPB):
                    last = dve.tensor_scalar(x1[:, t, :], total[:, t, :], mv[:, t, 0:1], rstd[:, t:t + 1],
                                             ALU.subtract, ALU.mult)
                last.then_inc(x1_ok, 1)
                upto(dve, x1_ok, b, 1, 1)
                dve.tensor_scalar(rows(b), x1[:], 1.0, None, ALU.mult)
                upto(dve, x1T_mm, b, 1, 1)
                flat = misc[:].rearrange("p t n -> p (t n)")
                dve.tensor_copy(x_shift[0:64, bass.ds(b * XW, L)], flat[0:64])
                dve.tensor_copy(x_shift[64:P, bass.ds(b * XW + 1, L)], flat[64:P]).then_inc(xw_ok, 1)

            dve.memset(q_tok[:].rearrange("p t h n -> p (t h n)"), 0.0).then_inc(boot, 1)
            dve.memset(k_tok[:].rearrange("p t h n -> p (t h n)"), 0.0).then_inc(k_zero, 1)
            dve.wait_ge(k_zero, 1)
            dve.memset(k_tok[:, :, :, 48:51], 1.0).then_inc(boot, 1)
            dve.wait_ge(loaded, 16 * 9)
            dve.tensor_copy(identb[:], ident[:]).then_inc(boot, 1)
            run(dve, batch)


def local_layers(nc, args, state):
    (wqkv, wo, w1, w2, b1, b2, ln_gb, qk_scales, rot_base, masks) = args
    x_shift, ident, identb, halfneg, eps = state
    with ExitStack() as ctx:
        def sb(name, shape, dt=F32):
            return ctx.enter_context(nc.sbuf_tensor(name, shape, dt))

        def sem(name):
            return ctx.enter_context(nc.semaphore(name))

        wqkv_sb = sb("wqkv_sb", [P, 2, 3 * INNER])
        wo_sb = sb("wo_sb", [P, 2, PAIRS * P])
        w1_sb = sb("w1_sb", [P, 2, 2 * FF])
        w2_sb = sb("w2_sb", [P, 2, 3 * P])
        b1_sb = sb("b1_sb", [P, 2, 2 * FF])
        b2_sb = sb("b2_sb", [P, 2, P])
        gb_sb = sb("gb_sb", [P, 2, 2])
        scales_sb = sb("scales_sb", [P, DEPTH, 4 * DH])
        base_sb = sb("base_sb", [P, TPB, 4 * DH])
        mask_sb = sb("mask_sb", [P, 2, 512], BF16)
        tiny = sb("tiny", [P, HEADS])
        xs = sb("xs", [P, 2, P])
        sq = sb("sq", [P, INNER])
        ssum = sb("ssum", [P, 2, 2, HEADS])
        rnorm = sb("rnorm", [P, 2, 2, HEADS])
        tab = sb("tab", [P, 2, 4 * DH])
        qkn = sb("qkn", [P, 2, INNER])
        t_cos = sb("t_cos", [P, 2, INNER])
        t_sin = sb("t_sin", [P, 2, INNER])
        v_tok = sb("v_tok", [P, 2, INNER])
        v_pad = sb("v_pad", [P, 2, WPT, PAIRS * P])
        qT = sb("qT", [P, PAIRS, P])
        kT = sb("kT", [P, 2, PAIRS, 2, WIN + P])
        s_max = sb("s_max", [P, HEADS])
        s_sub = sb("s_sub", [P, HEADS * 2 * WIN])
        prob = sb("prob", [P, 2, HEADS * 2 * WIN])
        den = sb("den", [P, 2, HEADS])
        rden = sb("rden", [P, 2, HEADS])
        probT = sb("probT", [P, PAIRS, P])
        o_tok = sb("o_tok", [P, INNER])
        oT = sb("oT", [P, PAIRS, P])
        y_tok = sb("y_tok", [P, P])
        xs2 = sb("xs2", [P, 2, P])
        stats = sb("stats", [P, 6])
        mv = sb("mv", [P, 2])
        rstd = sb("rstd", [P, 1])
        xn = sb("xn", [P, P])
        xnT = sb("xnT", [P, P])
        gate = sb("gate", [P, FF])
        gelu = sb("gelu", [P, FF])
        lin = sb("lin", [P, FF])
        hid = sb("hid", [P, FF])
        hidT = sb("hidT", [P, 3, P])
        z_tok = sb("z_tok", [P, P])
        bank = [ctx.enter_context(nc.psum_tensor(f"bank{i}", [P, 2, 512], F32)) for i in range(4)]
        b01, b23, b45, b67 = bank

        w_loaded, c_loaded = sem("w_loaded"), sem("c_loaded")
        q_mm, k_mm, v_mm, qT_mm, kT_mm, s_mm = map(sem, ["q_mm", "k_mm", "v_mm", "qT_mm", "kT_mm", "s_mm"])
        pT_mm, o_mm, oT_mm, y_mm, yT_mm = map(sem, ["pT_mm", "o_mm", "oT_mm", "y_mm", "yT_mm"])
        ln_mm, xnT_mm, h_mm, hT_mm, z_mm, zT_mm = map(sem, ["ln_mm", "xnT_mm", "h_mm", "hT_mm", "z_mm", "zT_mm"])
        xs_ok, sqq_ok, sqk_ok, v_ok, qT_ok, kT_ok = map(sem, ["xs_ok", "sqq_ok", "sqk_ok", "v_ok", "qT_ok", "kT_ok"])
        exp_ok, pT_ok, oT_ok, y_ok, gelu_ok, hT_ok = map(sem, ["exp_ok", "pT_ok", "oT_ok", "y_ok", "gelu_ok", "hT_ok"])
        ssq_ok, ssk_ok, qn_ok, kn_ok, cosq_ok, cosk_ok = map(sem, ["ssq_ok", "ssk_ok", "qn_ok", "kn_ok", "cosq_ok", "cosk_ok"])
        max_ok, sub_ok, den_ok, rden_ok, o_ok, xa_ok, xs2_ok = map(sem, ["max_ok", "sub_ok", "den_ok", "rden_ok", "o_ok", "xa_ok", "xs2_ok"])
        bn_ok, mv_ok, xn_ok, xnT_ok, gate_ok, lin_ok, hid_ok, z_ok = map(sem, ["bn_ok", "mv_ok", "xn_ok", "xnT_ok", "gate_ok", "lin_ok", "hid_ok", "z_ok"])
        xf_ok = sem("xf_ok")
        tab_ok, aboveq_ok, rq_ok, abovek_ok, rk_ok, sinq_ok, sink_ok, eps_ok, rstd_ok = map(
            sem, ["tab_ok", "aboveq_ok", "rq_ok", "abovek_ok", "rk_ok", "sinq_ok", "sink_ok", "eps_ok", "rstd_ok"])
        vpad_ok, init_ok = [sem("vpad0_ok"), sem("vpad1_ok")], sem("init_ok")

        def done(eng, s, t, back=0, credit=0):
            count = t + 1 - back
            if isinstance(count, int):
                if count <= 0:
                    return
                count = min(count, TILES)
            eng.wait_ge(s, count + credit)

        def behind_constant(eng, s, t):
            eng.wait_ge(c_loaded, 48)
            eng.wait_ge(s, t + 1)

        def spread(eng, t, s):
            if isinstance(t, int) and t < 0:
                return
            eng.wait_ge(vpad_ok[s], (t // 2 + 1) * (16 * 4 * WPT))

        def weights(eng, t):
            eng.wait_ge(w_loaded, (t // TPL + 1) * (16 * LOADS))

        def par(t):
            return bass.ds((t // TPL) % 2, 1)

        def run(eng, step):
            for x in range(FIRST):
                step(x, x % 2)
            with eng.Fori(FIRST // 2, TILES // 2) as two:
                step(2 * two, 0)
                step(2 * two + 1, 1)
            for x in range(TILES, TILES + LAG):
                step(x, x % 2)

        def live(t):
            return not isinstance(t, int) or 0 <= t < TILES

        def state_cols(t, lo, hi, shift=0):
            return x_shift[lo:hi, bass.ds(((t // TPB) % B) * XW + (t % TPB) * P + shift, P)]

        block = ctx.enter_context(nc.Block())

        @block.sync
        def _(sp):
            def load_weights(layer, half):
                one = bass.ds(layer, 1)
                h = bass.ds(half, 1)
                def src(a):
                    return a[one].rearrange("l p n -> (l p) n")
                def dst(a, k=P):
                    return a[0:k, h].rearrange("p l n -> p (l n)")
                sp.dma_start(dst(wqkv_sb), src(wqkv)).then_inc(w_loaded, 16)
                sp.dma_start(dst(wo_sb), src(wo)).then_inc(w_loaded, 16)
                sp.dma_start(dst(w1_sb), src(w1)).then_inc(w_loaded, 16)
                sp.dma_start(dst(w2_sb), src(w2)).then_inc(w_loaded, 16)
                sp.dma_start(dst(b1_sb), b1[one].broadcast_to([P, 2 * FF])).then_inc(w_loaded, 16)
                sp.dma_start(dst(b2_sb), b2[one].broadcast_to([P, P])).then_inc(w_loaded, 16)
                sp.dma_start(dst(gb_sb), src(ln_gb)).then_inc(w_loaded, 16)

            def spread_v(t, s):
                sp.wait_ge(v_ok, t + 1)
                sp.wait_ge(o_mm, t + 1)
                for a in range(2):
                    for w in range(WPT):
                        for c in range(2):
                            src_w = w + c - 1
                            slot = s if src_w >= 0 else 1 - s
                            lo = (src_w % WPT) * WIN
                            dst = v_pad[64 * a + WIN * c:64 * a + WIN * c + WIN, s, w].rearrange(
                                "p (q n) -> p q n", n=P)[:, :, a * DH:(a + 1) * DH]
                            src = v_tok[lo:lo + WIN, slot, a * 512:(a + 1) * 512].rearrange(
                                "p (q n) -> p q n", n=DH)
                            sp.dma_start(dst, src).then_inc(vpad_ok[s], 16)

            sp.dma_start(scales_sb[:], qk_scales.rearrange("a (l n) -> a l n", l=DEPTH).broadcast_to(
                [P, DEPTH, 4 * DH])).then_inc(c_loaded, 16)
            sp.dma_start(base_sb[:], rot_base).then_inc(c_loaded, 16)
            sp.dma_start(mask_sb[:].bitcast(U16), masks).then_inc(c_loaded, 16)
            load_weights(0, 0)
            sp.wait_ge(w_loaded, 16 * LOADS)
            load_weights(1, 1)
            sp.wait_ge(init_ok, 2)
            for t in range(2):
                spread_v(t, t % 2)
            with sp.Fori(1, TPL // 2 + 2) as two:
                spread_v(2 * two, 0)
                spread_v(2 * two + 1, 1)
            with sp.Fori(2, DEPTH) as layer:
                sp.wait_ge(xf_ok, layer * TPL + 1)
                load_weights(layer, layer % 2)
                with sp.Fori(0, TPL // 2) as two:
                    t = (layer - 1) * TPL + 2 * two + 4
                    spread_v(t, 0)
                    spread_v(t + 1, 1)
            with sp.Fori((DEPTH - 1) * TPL // 2 + 2, TILES // 2) as two:
                spread_v(2 * two, 0)
                spread_v(2 * two + 1, 1)

        @block.tensor
        def _(pe):
            def project(t, s, part, out, mm):
                for j in range(2):
                    c = part * INNER + j * 512
                    last = pe.matmul(out[:, j, :], xs[:, s, :],
                                     wqkv_sb[:, par(t), c:c + 512].rearrange("p l n -> p (l n)"),
                                     start=True, stop=True)
                last.then_inc(mm, 1)

            def turn_pairs(out, terms, mm):
                for p in range(PAIRS):
                    for n, a in enumerate(terms):
                        last = pe.matmul(out[:, p // 4, (p % 4) * P:(p % 4 + 1) * P], a[:, p * P:(p + 1) * P],
                                         ident[:], start=(n == 0), stop=(n == len(terms) - 1), is_transpose=True)
                last.then_inc(mm, 1)

            def step(x, s):
                a, b, c, d = x, x - 1, x - 2, x - 3
                r = 1 - s
                if live(a):
                    weights(pe, a)
                    done(pe, xs_ok, a)
                    done(pe, o_ok, a, 3)
                    if isinstance(a, int):
                        done(pe, v_ok, a, 1)
                    project(a, s, 0, b01, q_mm)
                if live(b):
                    done(pe, cosq_ok, b)
                    done(pe, sinq_ok, b)
                    pe.wait_ge(xf_ok, b - 2 + TPL)
                    done(pe, y_ok, b, 2)
                    if isinstance(b, int):
                        done(pe, sub_ok, b, 1)
                    turn_pairs(b45, [t_cos[:, 0], t_sin[:, 0]], qT_mm)
                if live(a):
                    done(pe, oT_ok, a, 3)
                    if isinstance(a, int):
                        done(pe, kn_ok, a, 1)
                    project(a, s, 1, b23, k_mm)
                if live(b):
                    done(pe, cosk_ok, b)
                    done(pe, sink_ok, b)
                    done(pe, z_ok, b, 3)
                    done(pe, xa_ok, b, 2)
                    if isinstance(b, int):
                        done(pe, kT_ok, b, 1)
                    turn_pairs(b67, [t_cos[:, 1], t_sin[:, 1]], kT_mm)
                if live(a):
                    done(pe, sqq_ok, a)
                    done(pe, qn_ok, a)
                    project(a, s, 2, b01, v_mm)
                if live(b):
                    done(pe, qT_ok, b)
                    done(pe, kT_ok, b)
                    which = (b % TPB) // 2 if r == 0 else 1
                    for j in range(2):
                        pe.matmul(b45[:, j, :], identb[:],
                                  mask_sb[:, bass.ds(which, 1), :].rearrange("p l n -> p (l n)"),
                                  start=True, stop=False, skip_group_check=True)
                    for p in range(PAIRS):
                        for w in range(WPT):
                            last = pe.matmul(b45[WIN * w:WIN * w + WIN, p // 4, (p % 4) * P:(p % 4 + 1) * P],
                                             qT[:, p, WIN * w:WIN * w + WIN],
                                             kT[:, r, p, :, WIN * w:WIN * w + 2 * WIN],
                                             start=False, stop=True, skip_group_check=True)
                    last.then_inc(s_mm, 1)
                if live(d):
                    done(pe, xs2_ok, d)
                    done(pe, kT_ok, d + 2)
                    pe.matmul(b67[:, 0, 0:P], xs2[:, r, :], ident[:], start=True, stop=True,
                              is_transpose=True).then_inc(ln_mm, 1)
                if live(c):
                    done(pe, exp_ok, c)
                    done(pe, sqk_ok, c + 2)
                    done(pe, kn_ok, c + 2)
                    turn_pairs(b23, [prob[:, s]], pT_mm)
                if live(d):
                    done(pe, xn_ok, d)
                    pe.matmul(b67[:, 1, 0:P], xn[:], ident[:], start=True, stop=True,
                              is_transpose=True).then_inc(xnT_mm, 1)
                if live(c):
                    done(pe, pT_ok, c)
                    done(pe, v_ok, c + 2)
                    spread(pe, c, s)
                    for p in range(PAIRS):
                        for w in range(WPT):
                            last = pe.matmul(b01[WIN * w:WIN * w + WIN, p // 4, (p % 4) * P:(p % 4 + 1) * P],
                                             probT[:, p, WIN * w:WIN * w + WIN],
                                             v_pad[:, s, w, p * P:(p + 1) * P],
                                             start=True, stop=True, skip_group_check=True)
                    last.then_inc(o_mm, 1)
                if live(d):
                    done(pe, xnT_ok, d)
                    for j in range(2):
                        last = pe.matmul(b67[:, j, 0:FF], xnT[:],
                                         w1_sb[:, par(d), j * FF:(j + 1) * FF].rearrange("p l n -> p (l n)"),
                                         start=True, stop=True)
                    last.then_inc(h_mm, 1)
                if live(c):
                    done(pe, o_ok, c)
                    turn_pairs(b23, [o_tok[:]], oT_mm)
                if live(d):
                    done(pe, hid_ok, d)
                    done(pe, sub_ok, d + 2)
                    for j in range(3):
                        n = min(P, FF - j * P)
                        last = pe.matmul(b45[0:n, 0, j * P:(j + 1) * P], hid[:, j * P:j * P + n], ident[:],
                                         start=True, stop=True, is_transpose=True)
                    last.then_inc(hT_mm, 1)
                if live(c):
                    done(pe, oT_ok, c)
                    done(pe, sub_ok, c + 1)
                    for p in range(PAIRS):
                        last = pe.matmul(b45[:, 1, 0:P], oT[:, p, :],
                                         wo_sb[:, par(c), p * P:(p + 1) * P].rearrange("p l n -> p (l n)"),
                                         start=(p == 0), stop=(p == PAIRS - 1))
                    last.then_inc(y_mm, 1)
                if live(d):
                    done(pe, hT_ok, d)
                    for j in range(3):
                        n = min(P, FF - j * P)
                        last = pe.matmul(b67[:, 0, 0:P], hidT[0:n, j, :],
                                         w2_sb[0:n, par(d), j * P:(j + 1) * P].rearrange("p l n -> p (l n)"),
                                         start=(j == 0), stop=(j == 2))
                    last.then_inc(z_mm, 1)
                if live(c):
                    done(pe, y_ok, c)
                    done(pe, kT_ok, c + 1)
                    done(pe, hid_ok, c, 1)
                    pe.matmul(b67[:, 1, 0:P], y_tok[:], ident[:], start=True, stop=True,
                              is_transpose=True).then_inc(yT_mm, 1)
                if live(d):
                    done(pe, z_ok, d)
                    pe.matmul(b45[:, 0, 0:P], z_tok[:], ident[:], start=True, stop=True,
                              is_transpose=True).then_inc(zT_mm, 1)

            pe.sem_inc(o_mm, 2)
            pe.wait_ge(c_loaded, 48)
            run(pe, step)

        @block.scalar
        def _(act):
            def copy(out, in_):
                return act.activation(out, in_, ACT.Copy)

            def flat(bank):
                return bank[:].rearrange("p j n -> p (j n)")

            def load_xs(t, s):
                done(act, v_mm, t, 2)
                act.wait_ge(xf_ok, t + 1)
                copy(xs[:, s, :], state_cols(t, 0, P)).then_inc(xs_ok, 1)

            def step(x, s):
                a, b, c, d = x, x - 1, x - 2, x - 3
                r = 1 - s
                if live(a):
                    done(act, q_mm, a)
                    done(act, ssk_ok, a, 1)
                    act.activation(sq[:], flat(b01), ACT.Square).then_inc(sqq_ok, 1)
                if live(b):
                    done(act, qT_mm, b)
                    done(act, s_mm, b, 1)
                    copy(qT[:].rearrange("p q n -> p (q n)"), flat(b45)).then_inc(qT_ok, 1)
                if live(a):
                    done(act, k_mm, a)
                    done(act, ssq_ok, a)
                    act.activation(sq[:], flat(b23), ACT.Square).then_inc(sqk_ok, 1)
                if live(b):
                    done(act, kT_mm, b)
                    done(act, s_mm, b, 1)
                    for h in range(2):
                        src = flat(b67)[64 * h:64 * h + 64].rearrange("p (q n) -> p q n", n=P)
                        copy(kT[64 * h:64 * h + 64, r, :, h, WIN:WIN + P], src)
                        last = copy(kT[64 * h:64 * h + 64, s, :, h, 0:WIN], src[:, :, P - WIN:P])
                    last.then_inc(kT_ok, 1)
                if live(a):
                    done(act, v_mm, a)
                    spread(act, a - 1, r)
                    spread(act, a - 2, s)
                    copy(v_tok[:, s, :], flat(b01)).then_inc(v_ok, 1)
                if live(c):
                    done(act, pT_mm, c)
                    done(act, o_mm, c, 1, credit=2)
                    copy(probT[:].rearrange("p q n -> p (q n)"), flat(b23)).then_inc(pT_ok, 1)
                if live(b):
                    done(act, sub_ok, b)
                    done(act, pT_mm, b, 2)
                    done(act, den_ok, b, 2)
                    act.activation(prob[:, r, :], s_sub[:], ACT.Exp, scale=8.0).then_inc(exp_ok, 1)
                if isinstance(a, int) and a + 1 < TILES or not isinstance(a, int):
                    load_xs(a + 1, r)
                if live(d):
                    done(act, gate_ok, d)
                    done(act, hid_ok, d, 1)
                    act.activation(gelu[:], gate[:], ACT.Gelu).then_inc(gelu_ok, 1)
                if live(c):
                    done(act, oT_mm, c)
                    done(act, y_mm, c, 1)
                    copy(oT[:].rearrange("p q n -> p (q n)"), flat(b23)).then_inc(oT_ok, 1)
                if live(d):
                    done(act, hT_mm, d)
                    done(act, z_mm, d, 1)
                    copy(hidT[:, 0:2, :].rearrange("p q n -> p (q n)"), b45[:, 0, 0:2 * P])
                    copy(hidT[0:FF - 2 * P, 2, :], b45[0:FF - 2 * P, 0, 2 * P:3 * P]).then_inc(hT_ok, 1)
                if live(c):
                    done(act, y_mm, c)
                    done(act, yT_mm, c, 1)
                    copy(y_tok[:], b45[:, 1, 0:P]).then_inc(y_ok, 1)

            act.wait_ge(init_ok, 3)
            load_xs(0, 0)
            run(act, lambda x, s: step(x, s))

        @block.gpsimd
        def _(pool):
            def inv_root(t, s, i, ssum_ok, above_ok, root_ok):
                done(pool, ssum_ok, t)
                pool.tensor_tensor(ssum[:, s, i, :], ssum[:, s, i, :], tiny[:], ALU.add).then_inc(above_ok, 1)
                done(pool, above_ok, t)
                pool.tensor_tensor(rnorm[:, s, i, :], ssum[:, s, i, :], halfneg[:, 0:HEADS], ALU.pow).then_inc(root_ok, 1)

            def rotate(t, s, i, n_ok, mm, sin_ok):
                done(pool, n_ok, t)
                done(pool, mm, t, 1)
                src = qkn[:, i, :].rearrange("p (h g n) -> p h g n", g=2, n=DH // 2)
                dst = t_sin[:, i, :].rearrange("p (h g n) -> p h g n", g=2, n=DH // 2)
                for g in range(2):
                    c = (2 * i + 1) * DH + g * (DH // 2)
                    w = tab[:, s, c:c + DH // 2].unsqueeze(1).broadcast_to([P, HEADS, DH // 2])
                    last = pool.tensor_tensor(dst[:, :, g, :], src[:, :, 1 - g, :], w, ALU.mult)
                last.then_inc(sin_ok, 1)

            def step(x, s):
                a, d = x, x - 3
                if live(a):
                    done(pool, cosk_ok, a, 2)
                    pool.tensor_tensor(tab[:, s, :], base_sb[:, bass.ds(a % TPB, 1), :].rearrange("p l n -> p (l n)"),
                                       scales_sb[:, bass.ds(a // TPL, 1), :].rearrange("p l n -> p (l n)"),
                                       ALU.mult).then_inc(tab_ok, 1)
                    inv_root(a, s, 0, ssq_ok, aboveq_ok, rq_ok)
                    inv_root(a, s, 1, ssk_ok, abovek_ok, rk_ok)
                    rotate(a, s, 0, qn_ok, qT_mm, sinq_ok)
                    rotate(a, s, 1, kn_ok, kT_mm, sink_ok)
                if live(d):
                    done(pool, mv_ok, d)
                    done(pool, xn_ok, d, 1)
                    pool.tensor_tensor(rstd[:], mv[:, 1:2], eps[:, 0:1], ALU.add).then_inc(eps_ok, 1)
                    done(pool, eps_ok, d)
                    pool.tensor_tensor(rstd[:], rstd[:], halfneg[:, 0:1], ALU.pow).then_inc(rstd_ok, 1)

            pool.memset(tiny[:], 1e-37)
            pool.memset(v_pad[:].rearrange("p a b c -> p (a b c)"), 0.0).then_inc(init_ok, 1)
            pool.wait_ge(c_loaded, 48)
            run(pool, step)

        @block.vector
        def _(dve):
            def heads(ap, n=DH):
                return ap.rearrange("p (h n) -> p h n", n=n)

            def wide(ap, n=DH):
                return ap.unsqueeze(2).broadcast_to([P, HEADS, n])

            def flat(bank):
                return bank[:].rearrange("p j n -> p (j n)")

            def sum_squares(t, s, i, sq_ok, out_ok):
                done(dve, sq_ok, t)
                dve.tensor_reduce(ssum[:, s, i, :], heads(sq[:]), AX.X, ALU.add).then_inc(out_ok, 1)

            def normalize(t, s, i, bank, root_ok, n_ok, sin_ok, cos_ok):
                done(dve, root_ok, t)
                done(dve, sin_ok, t, 1)
                done(dve, cos_ok, t, 1)
                dve.scalar_tensor_tensor(heads(qkn[:, i, :]), wide(rnorm[:, s, i, :]), 1e12, heads(flat(bank)),
                                         ALU.min, ALU.mult).then_inc(n_ok, 1)

            def cosine(t, s, i, n_ok, mm, cos_ok):
                done(dve, n_ok, t)
                done(dve, mm, t, 1)
                w = tab[:, s, 2 * i * DH:(2 * i + 1) * DH].unsqueeze(1).broadcast_to([P, HEADS, DH])
                dve.tensor_tensor(heads(t_cos[:, i, :]), heads(qkn[:, i, :]), w, ALU.mult).then_inc(cos_ok, 1)

            def step(x, s):
                a, b, c, d = x, x - 1, x - 2, x - 3
                r = 1 - s
                if live(a):
                    sum_squares(a, s, 0, sqq_ok, ssq_ok)
                    normalize(a, s, 0, b01, rq_ok, qn_ok, sinq_ok, cosq_ok)
                    sum_squares(a, s, 1, sqk_ok, ssk_ok)
                    done(dve, tab_ok, a)
                    cosine(a, s, 0, qn_ok, qT_mm, cosq_ok)
                    normalize(a, s, 1, b23, rk_ok, kn_ok, sink_ok, cosk_ok)
                    cosine(a, s, 1, kn_ok, kT_mm, cosk_ok)
                if live(d):
                    done(dve, ln_mm, d)
                    done(dve, rstd_ok, d, 1)
                    dve.bn_stats(stats[:], b67[:, 0, 0:P]).then_inc(bn_ok, 1)
                    behind_constant(dve, bn_ok, d)
                    dve.bn_aggr(mv[:], stats[:]).then_inc(mv_ok, 1)
                if live(b):
                    done(dve, s_mm, b)
                    dve.tensor_reduce(s_max[:], heads(flat(b45)), AX.X, ALU.max).then_inc(max_ok, 1)
                if live(d):
                    done(dve, rstd_ok, d)
                    done(dve, xnT_mm, d, 1)
                    dve.tensor_scalar(xn[:], b67[:, 0, 0:P], mv[:, 0:1], rstd[:], ALU.subtract,
                                      ALU.mult).then_inc(xn_ok, 1)
                if live(b):
                    done(dve, max_ok, b)
                    done(dve, exp_ok, b, 1)
                    dve.tensor_tensor(heads(s_sub[:]), heads(flat(b45)), wide(s_max[:]),
                                      ALU.subtract).then_inc(sub_ok, 1)
                if live(d):
                    done(dve, xnT_mm, d)
                    done(dve, h_mm, d, 1)
                    dve.tensor_scalar(xnT[:], b67[:, 1, 0:P],
                                      gb_sb[:, par(d), 0:1].rearrange("p l n -> p (l n)"),
                                      gb_sb[:, par(d), 1:2].rearrange("p l n -> p (l n)"),
                                      ALU.mult, ALU.add).then_inc(xnT_ok, 1)
                if live(c):
                    done(dve, o_mm, c, credit=2)
                    done(dve, rden_ok, c)
                    done(dve, oT_mm, c, 1)
                    dve.tensor_tensor(heads(o_tok[:]), heads(flat(b01)), wide(rden[:, s, :]),
                                      ALU.mult).then_inc(o_ok, 1)
                if live(d):
                    done(dve, h_mm, d)
                    done(dve, gelu_ok, d, 1)
                    dve.tensor_tensor(gate[:], b67[:, 1, 0:FF],
                                      b1_sb[:, par(d), FF:2 * FF].rearrange("p l n -> p (l n)"),
                                      ALU.add).then_inc(gate_ok, 1)
                    dve.tensor_tensor(lin[:], b67[:, 0, 0:FF],
                                      b1_sb[:, par(d), 0:FF].rearrange("p l n -> p (l n)"),
                                      ALU.add).then_inc(lin_ok, 1)
                if live(b):
                    done(dve, exp_ok, b)
                    dve.tensor_reduce(den[:, r, :], heads(prob[:, r, :]), AX.X, ALU.add).then_inc(den_ok, 1)
                    done(dve, den_ok, b)
                    dve.reciprocal(rden[:, r, :], den[:, r, :]).then_inc(rden_ok, 1)
                if live(d):
                    done(dve, lin_ok, d)
                    done(dve, gelu_ok, d)
                    done(dve, hT_mm, d, 1)
                    dve.tensor_tensor(hid[:], lin[:], gelu[:], ALU.mult).then_inc(hid_ok, 1)
                    done(dve, z_mm, d)
                    done(dve, zT_mm, d, 1)
                    dve.tensor_tensor(z_tok[:], b67[:, 0, 0:P], b2_sb[:, par(d), :].rearrange("p l n -> p (l n)"),
                                      ALU.add).then_inc(z_ok, 1)
                if live(c):
                    done(dve, yT_mm, c)
                    if not isinstance(c, int) or c + 1 < TILES:
                        done(dve, xs_ok, c + 1)
                    done(dve, xs2_ok, c, 1)
                    lo, hi = state_cols(c, 0, 64), state_cols(c, 64, P, 1)
                    dve.tensor_tensor(lo, b67[0:64, 1, 0:P], lo, ALU.add)
                    dve.tensor_tensor(hi, b67[64:P, 1, 0:P], hi, ALU.add).then_inc(xa_ok, 1)
                    done(dve, xa_ok, c)
                    done(dve, ln_mm, c, 2)
                    dve.tensor_scalar(xs2[:, s, :], state_cols(c, 0, P), 1.0, None, ALU.mult).then_inc(xs2_ok, 1)
                if live(d):
                    done(dve, zT_mm, d)
                    if not isinstance(d, int) or d + 1 < TILES:
                        done(dve, xs2_ok, d + 1)
                    lo, hi = state_cols(d, 0, 64), state_cols(d, 64, P, 1)
                    dve.tensor_tensor(lo, b45[0:64, 0, 0:P], lo, ALU.add)
                    dve.tensor_tensor(hi, b45[64:P, 0, 0:P], hi, ALU.add).then_inc(xf_ok, 1)

            dve.sem_inc(xf_ok, TPL)
            dve.memset(kT[:].rearrange("p a b c d -> p (a b c d)"), 0.0).then_inc(init_ok, 1)
            dve.memset(v_tok[:].rearrange("p a b -> p (a b)"), 0.0).then_inc(init_ok, 1)
            dve.wait_ge(c_loaded, 48)
            dve.wait_ge(w_loaded, 16 * LOADS)
            run(dve, step)


def last_norm(nc, out, x_shift, x1_tok, ident, halfneg, eps):
    out_v = out.rearrange("b (t p) c -> b p t c", p=P)
    with ExitStack() as ctx:
        def sb(name, shape, dt=F32):
            return ctx.enter_context(nc.sbuf_tensor(name, shape, dt))

        def sem(name):
            return ctx.enter_context(nc.semaphore(name))

        feat = sb("feat", [P, TPB, P])
        total = sb("total", [P, TPB, P])
        stats = sb("f_stats", [P, TPB, 6])
        mv = sb("f_mv", [P, TPB, 2])
        rstd = sb("f_rstd", [P, TPB])
        y = sb("f_y", [P, B, TPB, P])
        turned = ctx.enter_context(nc.psum_tensor("f_turned", [P, TPB, P], F32))
        feat_ok, turn_mm, sum_ok, bn_ok, mv_ok, eps_ok, rstd_ok, y_ok, stored = map(
            sem, ["feat_ok", "turn_mm", "sum_ok", "f_bn_ok", "f_mv_ok", "f_eps_ok", "f_rstd_ok", "f_y_ok", "stored"])
        block = ctx.enter_context(nc.Block())

        @block.scalar
        def _(act):
            for b in range(B):
                if b:
                    act.wait_ge(turn_mm, b)
                act.activation(feat[0:64].rearrange("p t n -> p (t n)"), x_shift[0:64, b * XW:b * XW + L], ACT.Copy)
                act.activation(feat[64:P].rearrange("p t n -> p (t n)"), x_shift[64:P, b * XW + 1:b * XW + 1 + L],
                               ACT.Copy).then_inc(feat_ok, 1)

        @block.tensor
        def _(pe):
            for b in range(B):
                pe.wait_ge(feat_ok, b + 1)
                if b:
                    pe.wait_ge(sum_ok, b)
                for t in range(TPB):
                    last = pe.matmul(turned[:, t, :], feat[:, t, :], ident[:], start=True, stop=True,
                                     is_transpose=True)
                last.then_inc(turn_mm, 1)

        @block.vector
        def _(dve):
            for b in range(B):
                dve.wait_ge(turn_mm, b + 1)
                if b:
                    dve.wait_ge(y_ok, b)
                dve.tensor_tensor(total[:], turned[:], x1_tok[:, b * TPB:(b + 1) * TPB, :], ALU.add).then_inc(sum_ok, 1)
                dve.wait_ge(sum_ok, b + 1)
                for t in range(TPB):
                    last = dve.bn_stats(stats[:, t, :], total[:, t, :])
                last.then_inc(bn_ok, 1)
                dve.wait_ge(bn_ok, b + 1)
                for t in range(TPB):
                    last = dve.bn_aggr(mv[:, t, :], stats[:, t, :])
                last.then_inc(mv_ok, 1)
                dve.wait_ge(rstd_ok, b + 1)
                for t in range(TPB):
                    last = dve.tensor_scalar(y[:, b, t, :], total[:, t, :], mv[:, t, 0:1], rstd[:, t:t + 1],
                                             ALU.subtract, ALU.mult)
                last.then_inc(y_ok, 1)

        @block.gpsimd
        def _(pool):
            for b in range(B):
                pool.wait_ge(mv_ok, b + 1)
                if b:
                    pool.wait_ge(y_ok, b)
                pool.tensor_tensor(rstd[:], mv[:, :, 1], eps[:], ALU.add).then_inc(eps_ok, 1)
                pool.wait_ge(eps_ok, b + 1)
                pool.tensor_tensor(rstd[:], rstd[:], halfneg[:, 0:TPB], ALU.pow).then_inc(rstd_ok, 1)

        @block.sync
        def _(sp):
            for b in range(B):
                sp.wait_ge(y_ok, b + 1)
                sp.dma_start(out_v[b], y[:, b]).then_inc(stored, 16)
            sp.wait_ge(stored, 16 * B)


def bf16_bits(a):
    return (np.ascontiguousarray(a, dtype=np.float32).view(np.uint32) >> 16).astype(np.uint16)


def rotary_base():
    half = np.arange(0, DH, 2, dtype=np.float32)
    inv_freq = (np.float32(1.0) / np.power(np.float32(10000.0), half / np.float32(DH))).astype(np.float32)
    t = np.arange(L, dtype=np.float32)
    freqs = t[:, None] * inv_freq[None, :]
    freqs = np.concatenate([freqs, freqs], -1)
    base = (half + np.float32(0.4 * DH)) / np.float32(1.4 * DH)
    power = (t - L // 2) / np.float32(WIN // 2)
    scale = np.power(base[None, :], power[:, None]).astype(np.float32)
    scale = np.concatenate([scale, scale], -1)
    sign = np.concatenate([-np.ones(DH // 2), np.ones(DH // 2)]).astype(np.float32)
    cos, sin = np.cos(freqs), np.sin(freqs) * sign
    inv = np.float32(1.0) / scale
    rows = np.concatenate([cos * scale, sin * scale, cos * inv, sin * inv], -1).astype(np.float32)
    return np.ascontiguousarray(rows.reshape(TPB, P, 4 * DH).transpose(1, 0, 2))


def window_masks():
    i = np.arange(P)[:, None] % WIN
    j = np.arange(2 * WIN)[None, :]
    ok = (j >= i) & (j <= i + WIN)
    first = ok & ~((np.arange(P)[:, None] < WIN) & (j < WIN))
    low = np.float32(-(2.0 ** 100))
    rows = np.stack([np.tile(np.where(m, np.float32(0), low), (1, 8)) for m in (first, ok)], 1)
    return bf16_bits(rows)


def three_parts(a):
    out, a = [], np.asarray(a, dtype=np.float64)
    for _ in range(3):
        part = (a.astype(np.float32).view(np.uint32) & np.uint32(0xFFFF0000)).view(np.float32)
        out.append(part)
        a = a - part
    return out


def alibi_slopes():
    start = 2.0 ** (-2.0 ** (-(np.log2(AH) - 3)))
    return np.array([start * start ** i for i in range(AH)], dtype=np.float32)


def alibi_rows():
    slope = alibi_slopes().astype(np.float64)[:, None]
    pos = np.arange(L)
    tile, inside = pos // P, pos % P
    q_rows, k_rows = [], []
    for i in range(TPB):
        here = (tile == i)[None, :]
        sign = np.where(i > tile, -1.0, 1.0)
        back = np.where(tile > i, -1.0, 1.0)
        for part in three_parts(slope * inside):
            q_rows.append(part * here)
            k_rows.append(np.broadcast_to(sign, (AH, L)))
            q_rows.append(np.broadcast_to(-back, (AH, L)))
            k_rows.append(part * here)
        for part in three_parts(np.broadcast_to(slope, (AH, L))):
            q_rows.append(part * here)
            k_rows.append(np.broadcast_to(-float(P) * np.abs(i - tile), (AH, L)))
    return bf16_bits(np.stack(q_rows)), bf16_bits(np.stack(k_rows))


def alibi_inside():
    k, m = np.arange(P)[:, None], np.arange(P)[None, :]
    relu = np.stack([np.maximum(m - k, 0), np.maximum(k - m, 0)], 1).astype(np.float16).view(np.uint16)
    value = -2.0 * alibi_slopes().astype(np.float64)
    high = value.astype(np.float16)
    low = (value - high).astype(np.float16)
    diag = np.eye(P)[:, None, None, :] * np.stack([high, low], 1)[None, :, :, None]
    return relu, diag.astype(np.float16).view(np.uint16)




def attention_then_local_layers(nc, A, out):
    with ExitStack() as ctx:
        def sb(name, shape, dt=F32):
            return ctx.enter_context(nc.sbuf_tensor(name, shape, dt))

        ident = sb("ident", [P, P])
        identb = sb("identb", [P, P], BF16)
        halfneg = sb("halfneg", [P, HEADS])
        eps = sb("eps", [P, TPB])
        x_shift = sb("x_shift", [P, B * XW])
        x1_tok = sb("x1_tok", [P, TPL, P])
        alibi_attention(nc, (A["x"], A["eye"], A["a_wqkv"], A["a_wo"], A["a_bo"], A["q_const"], A["k_const"],
                             A["relu_const"], A["slope_const"]), (x_shift, x1_tok, ident, identb, halfneg, eps))
        local_layers(nc, (A["wqkv"], A["wo"], A["w1"], A["w2"], A["b1"], A["b2"], A["gb"], A["scales"], A["rot"],
                          A["masks"]), (x_shift, ident, identb, halfneg, eps))
        last_norm(nc, out, x_shift, x1_tok, ident, halfneg, eps)


def laid_out(i):
    def swapped(a):
        return np.concatenate([a[:, DH // 2:], a[:, :DH // 2]], -1)

    a = {"x": i["L0_attn_q"]}
    a["a_wqkv"] = np.concatenate([i[n].T for n in ("L0_attn_Wq", "L0_attn_Wk", "L0_attn_Wv")], 1)
    a["a_wo"] = i["L0_attn_Wo"].T
    a["a_bo"] = i["L0_attn_bo"].reshape(1, C)
    wqkv = i["L0_ffn_Wqkv"]
    v = wqkv[:, :, 2 * INNER:].reshape(DEPTH, C, PAIRS, 2, DH).transpose(0, 1, 3, 2, 4).reshape(DEPTH, C, INNER)
    a["wqkv"] = np.concatenate([wqkv[:, :, :2 * INNER], v], -1)
    a["wo"] = i["L0_ffn_Wo"].reshape(DEPTH, PAIRS, P, C).transpose(0, 2, 1, 3).reshape(DEPTH, P, PAIRS * C)
    a["w1"] = i["L0_ffn_W1"]
    w2 = np.concatenate([i["L0_ffn_W2"], np.zeros((DEPTH, 3 * P - FF, C), np.float32)], 1)
    a["w2"] = w2.reshape(DEPTH, 3, P, C).transpose(0, 2, 1, 3).reshape(DEPTH, P, 3 * C)
    a["b1"], a["b2"] = i["L0_ffn_b1"], i["L0_ffn_b2"]
    a["gb"] = np.stack([i["L0_ffn_ln_g"], i["L0_ffn_ln_b"]], -1)
    q, k = i["L0_ffn_q_scale"], i["L0_ffn_k_scale"]
    a["scales"] = np.concatenate([q, swapped(q), k, swapped(k)], -1).reshape(1, -1)
    a["eye"] = np.eye(P, dtype=np.float32)
    a["rot"], a["masks"] = rotary_base(), window_masks()
    a["q_const"], a["k_const"] = alibi_rows()
    a["relu_const"], a["slope_const"] = alibi_inside()
    return {n: np.ascontiguousarray(v) for n, v in a.items()}


def kernel(**inputs):
    import concourse.bacc as bacc
    from concourse.bass_utils import run_bass_kernel_spmd

    nc = bacc.Bacc("TRN2", target_bir_lowering=False, num_devices=1)
    arrays = {f"in_{n}": v for n, v in laid_out({n: np.asarray(v) for n, v in inputs.items()}).items()}
    A = {n[3:]: nc.dram_tensor(n, v.shape, mybir.dt.from_np(v.dtype), kind="ExternalInput").ap()
         for n, v in arrays.items()}
    out = nc.dram_tensor("out_0", (B, L, C), F32, kind="ExternalOutput").ap()
    attention_then_local_layers(nc, A, out)
    r = run_bass_kernel_spmd(nc, [arrays], core_ids=[0])
    return r.results[0]["out_0"]
```

```python
from contextlib import ExitStack

import numpy as np

import concourse.bass as bass
from concourse import mybir

F32 = mybir.dt.float32
BF16 = mybir.dt.bfloat16
F16 = mybir.dt.float16
U16 = mybir.dt.uint16
ALU = mybir.AluOpType
ACT = mybir.ActivationFunctionType
AX = mybir.AxisListType

P = 128
B, L, C = 4, 512, 128
TPB = L // P
TPL = B * TPB
LN_EPS = 1e-5
XW = L + 8

AH, AD = 16, 8
AROWS = 64 + 36
STEPS = 2 * 3 + 4 * 3

DEPTH = 6
TILES = DEPTH * TPL
HEADS, DH = 16, 64
INNER = HEADS * DH
PAIRS = HEADS // 2
WIN = 32
WPT = P // WIN
FF = int(C * 4 * 2 / 3)
FCH = -(-FF // P)
BIAS = 2 * FF + FCH * P
FFN_COLS = BIAS + 2 * FCH + 3
FIRST, LAG = 6, 4



def alibi_attention(nc, args, state):
    x, eye, wqkvT, woT, bo, q_const, k_const, relu_const, slope_const = args
    x_shift, x1_tok, ident, identb, halfneg, eps = state
    with ExitStack() as ctx:
        def sb(name, shape, dt=F32):
            return ctx.enter_context(nc.sbuf_tensor(name, shape, dt))

        def sem(name):
            return ctx.enter_context(nc.semaphore(name))

        w_sb = sb("a_w", [P, 3 * C])
        wo_sb = sb("a_wo", [P, C])
        bo_sb = sb("a_bo", [P, C])
        relu_sb = sb("a_relu", [P, 2, P], F16)
        slope_sb = sb("a_slope", [P, AH, 2, P], F16)
        qT = sb("a_qT", [AROWS, AH, L], BF16)
        kT = sb("a_kT", [AROWS, AH, L], BF16)
        q_tok = sb("a_q_tok", [P, TPB, AH, 64], BF16)
        k_tok = sb("a_k_tok", [P, TPB, AH, 64], BF16)
        rest = sb("a_rest", [P, 2, TPB, C])
        v_ext = sb("a_v_ext", [P, TPB, AH, 32])
        x_in = sb("a_x_in", [P, TPB, P])
        xT = sb("a_xT", [P, TPB, P])
        negmax = sb("a_negmax", [P, TPB, 4])
        m_rest = sb("a_m_rest", [P, TPB, 4])
        m_tok = sb("a_m_tok", [P, TPB, 3, 4], BF16)
        mT = sb("a_mT", [12, L], BF16)
        prob = sb("a_prob", [P, 2, 4, L])
        oT = sb("a_oT", [P, L])
        rden = sb("a_rden", [P, TPB, 4])
        o_tok = sb("a_o_tok", [P, TPB, AH, AD])
        ocT = sb("a_ocT", [P, TPB, P])
        total = sb("a_total", [P, TPB, P])
        stats = sb("a_stats", [P, TPB, 6])
        mv = sb("a_mv", [P, TPB, 2])
        rstd = sb("a_rstd", [P, TPB])
        x1 = sb("a_x1", [P, TPB, P])
        max_bank = [ctx.enter_context(nc.psum_tensor(f"a_max{i}", [P, L], F32)) for i in range(2)]
        sT_bank = ctx.enter_context(nc.psum_tensor("a_sT", [P, 4, L], F32))
        o_bank = ctx.enter_context(nc.psum_tensor("a_o", [P, L], F32))
        misc = ctx.enter_context(nc.psum_tensor("a_misc", [P, TPB, P], F32))

        loaded, boot, k_zero, step_ok = sem("a_loaded"), sem("a_boot"), sem("a_k_zero"), sem("a_step_ok")
        xin_ok, xT_mm, xT_ok, qkv_mm, v_ok, split_ok, chain = map(
            sem, ["a_xin_ok", "a_xT_mm", "a_xT_ok", "a_qkv_mm", "a_v_ok", "a_split_ok", "a_chain"])
        turn_mm, qT_ok, kT_ok, p1_mm, max_ok, m_ok, m_mm, mT_ok, mrow_ok = map(
            sem, ["a_turn_mm", "a_qT_ok", "a_kT_ok", "a_p1_mm", "a_max_ok", "a_m_ok", "a_m_mm", "a_mT_ok", "a_mrow_ok"])
        sT_mm, exp_ok, o_mm, oT_ok, back_mm, rden_ok, o_ok, oc_mm, oc_ok, y_mm = map(
            sem, ["a_sT_mm", "a_exp_ok", "a_o_mm", "a_oT_ok", "a_back_mm", "a_rden_ok", "a_o_ok", "a_oc_mm", "a_oc_ok", "a_y_mm"])
        sum_ok, res_ok, bn_ok, mv_ok, eps_ok, rstd_ok, x1_ok, x1T_mm, xw_ok = map(
            sem, ["a_sum_ok", "a_res_ok", "a_bn_ok", "a_mv_ok", "a_eps_ok", "a_rstd_ok", "a_x1_ok", "a_x1T_mm", "a_xw_ok"])

        def upto(eng, s, b, per_batch, count):
            n = b * per_batch + count
            if isinstance(n, int) and n <= 0:
                return
            eng.wait_ge(s, n)

        def run(eng, batch):
            batch(0)
            with eng.Fori(1, B) as b:
                batch(b)

        def rows(b):
            return x1_tok[:, bass.ds(b * TPB, TPB), :]

        block = ctx.enter_context(nc.Block())

        @block.sync
        def _(sp):
            sp.dma_start(ident[:], eye).then_inc(loaded, 16)
            sp.dma_start(x1_tok[:], x.rearrange("b (t p) c -> p (b t) c", p=P)).then_inc(loaded, 16)
            sp.dma_start(w_sb[:], wqkvT).then_inc(loaded, 16)
            sp.dma_start(wo_sb[:], woT).then_inc(loaded, 16)
            sp.dma_start(bo_sb[:], bo.broadcast_to([P, C])).then_inc(loaded, 16)
            sp.dma_start(qT[64:AROWS].bitcast(U16), q_const).then_inc(loaded, 16)
            sp.dma_start(kT[64:AROWS].bitcast(U16), k_const).then_inc(loaded, 16)
            sp.dma_start(relu_sb[:].bitcast(U16), relu_const).then_inc(loaded, 16)
            sp.dma_start(slope_sb[:].bitcast(U16), slope_const).then_inc(loaded, 16)

            def batch(b):
                for g in range(4):
                    upto(sp, mT_ok, b, 4, g + 1)
                    for piece in range(3):
                        sp.dma_start(qT[48 + piece:49 + piece, 4 * g:4 * g + 4, :], mT[4 * piece:4 * piece + 4, :]
                                     ).then_inc(mrow_ok, 16)

            run(sp, batch)
            sp.wait_ge(mrow_ok, B * 4 * 3 * 16)

        @block.tensor
        def _(pe):
            def first_pass(b, g, i):
                for n in range(4):
                    h, u = 4 * g + n, 16 * g + 4 * i + n
                    upto(pe, max_ok, b, 64, u - 1)
                    out = max_bank[u % 2]
                    pe.matmul(out[:], qT[:, h, i * P:(i + 1) * P], kT[:, h, :], start=True, stop=True)
                    for piece in range(2):
                        last = pe.matmul(out[:, i * P:(i + 1) * P], relu_sb[:, 0, :], slope_sb[:, h, piece, :],
                                         start=False, stop=True, skip_group_check=True)
                    last.then_inc(p1_mm, 1)

            def turn_maxima(b, g):
                upto(pe, m_ok, b, 4, g + 1)
                if g:
                    upto(pe, o_ok, b, 4, g)
                for t in range(TPB):
                    last = pe.matmul(misc[0:12, 0:2, :].bitcast(BF16).rearrange("p a n -> p (a n)")[
                        :, t * P:(t + 1) * P],
                        m_tok[:, t].rearrange("p a h -> p (a h)"), identb[:], start=True, stop=True,
                        is_transpose=True)
                last.then_inc(m_mm, 1)

            def scores(b, g, j):
                if j == 0:
                    pe.wait_ge(mrow_ok, (b * 4 + g + 1) * 48)
                for half in range(2):
                    u = 8 * g + 2 * j + half
                    upto(pe, exp_ok, b, 32, u - 1)
                    for n in range(2):
                        h = 4 * g + 2 * half + n
                        out = sT_bank[:, 2 * half + n, :]
                        pe.matmul(out, kT[:, h, j * P:(j + 1) * P], qT[:, h, :], start=True, stop=True)
                        for piece in range(2):
                            last = pe.matmul(out[:, j * P:(j + 1) * P], relu_sb[:, 1, :], slope_sb[:, h, piece, :],
                                             start=False, stop=True, skip_group_check=True)
                    last.then_inc(sT_mm, 1)

            def weigh(b, g, j):
                upto(pe, exp_ok, b, 32, 8 * g + 2 * j + 2)
                if j == 0:
                    upto(pe, oT_ok, b, 4, g)
                for n in range(4):
                    last = pe.matmul(o_bank[32 * n:32 * n + 32, :], v_ext[:, j, 4 * g + n, :],
                                     prob[:, j % 2, n, :], start=(j == 0), stop=(j == TPB - 1),
                                     skip_group_check=True)
                last.then_inc(o_mm, 1)

            def turn_back(b, g):
                upto(pe, oT_ok, b, 4, g + 1)
                upto(pe, mT_ok, b, 4, g + 1)
                for t in range(TPB):
                    last = pe.matmul(misc[:, t, :], oT[:, t * P:(t + 1) * P], ident[:], start=True, stop=True,
                                     is_transpose=True)
                last.then_inc(back_mm, 1)

            def batch(b):
                upto(pe, xin_ok, b, 1, 1)
                upto(pe, xw_ok, b, 1, 0)
                for t in range(TPB):
                    last = pe.matmul(misc[:, t, :], x_in[:, t, :], ident[:], start=True, stop=True, is_transpose=True)
                last.then_inc(xT_mm, 1)
                upto(pe, xT_ok, b, 1, 1)
                upto(pe, exp_ok, b, 32, 0)
                for t in range(TPB):
                    last = pe.matmul(sT_bank[:, t, 0:3 * C], xT[:, t, :], w_sb[:], start=True, stop=True)
                last.then_inc(qkv_mm, 1)
                for n in range(8):
                    src = q_tok if n < 4 else k_tok
                    if n == 0:
                        upto(pe, split_ok, b, 2, 2)
                        upto(pe, v_ok, b, 1, 1)
                    if n >= 4:
                        upto(pe, qT_ok, b, 4, n - 3)
                    for k in range(2):
                        p = 2 * (n % 4) + k
                        for t in range(TPB):
                            last = pe.matmul(sT_bank[:, n % 4, :].bitcast(BF16)[:, (4 * k + t) * P:(4 * k + t + 1) * P],
                                             src[:, t, 2 * p:2 * p + 2, :].rearrange("p h n -> p (h n)"), identb[:],
                                             start=True, stop=True, is_transpose=True)
                    last.then_inc(turn_mm, 1)
                upto(pe, qT_ok, b, 4, 4)
                upto(pe, kT_ok, b, 4, 4)
                for i in range(TPB):
                    first_pass(b, 0, i)
                for g in range(4):
                    if g < 3:
                        first_pass(b, g + 1, 0)
                    if g:
                        turn_back(b, g - 1)
                    turn_maxima(b, g)
                    if g < 3:
                        first_pass(b, g + 1, 1)
                    for j in range(TPB):
                        scores(b, g, j)
                        if g < 3 and j < 2:
                            first_pass(b, g + 1, j + 2)
                        weigh(b, g, j)
                turn_back(b, 3)
                upto(pe, o_ok, b, 4, 4)
                for t in range(TPB):
                    last = pe.matmul(misc[:, t, :], o_tok[:, t].rearrange("p h d -> p (h d)"), ident[:],
                                     start=True, stop=True, is_transpose=True)
                last.then_inc(oc_mm, 1)
                upto(pe, oc_ok, b, 1, 1)
                for t in range(TPB):
                    last = pe.matmul(misc[:, t, :], ocT[:, t, :], wo_sb[:], start=True, stop=True)
                last.then_inc(y_mm, 1)
                upto(pe, x1_ok, b, 1, 1)
                upto(pe, sum_ok, b, 1, 1)
                for t in range(TPB):
                    last = pe.matmul(misc[:, t, :], x1[:, t, :], ident[:], start=True, stop=True, is_transpose=True)
                last.then_inc(x1T_mm, 1)

            pe.wait_ge(loaded, 16 * 9)
            pe.wait_ge(boot, 4)
            run(pe, batch)

        @block.scalar
        def _(act):
            def copy(out, in_):
                return act.activation(out, in_, ACT.Copy)

            def batch(b):
                upto(act, xT_mm, b, 1, 0)
                copy(x_in[:], rows(b)).then_inc(xin_ok, 1)
                upto(act, xT_mm, b, 1, 1)
                upto(act, qkv_mm, b, 1, 0)
                copy(xT[:], misc[:]).then_inc(xT_ok, 1)
                upto(act, qkv_mm, b, 1, 1)
                upto(act, o_mm, b, 16, 0)
                for t in range(TPB):
                    last = copy(v_ext[:, t, :, 0:AD], sT_bank[:, t, 2 * C:3 * C].rearrange("p (h d) -> p h d", d=AD))
                last.then_inc(v_ok, 1)
                for n in range(4):
                    upto(act, turn_mm, b, 8, n + 1)
                    for a in range(2):
                        src = sT_bank[64 * a:64 * a + 64, n, :].bitcast(BF16).rearrange("p (k l) -> p k l", k=2)
                        last = copy(qT[0:64, 4 * n + a:4 * n + a + 3:2, :], src)
                    last.then_inc(qT_ok, 1)
                for g in range(4):
                    upto(act, m_mm, b, 4, g + 1)
                    copy(mT[:], misc[0:12, 0:2, :].bitcast(BF16).rearrange("p a n -> p (a n)")).then_inc(mT_ok, 1)
                    for j in range(TPB):
                        for half in range(2):
                            u = 8 * g + 2 * j + half
                            upto(act, sT_mm, b, 32, u + 1)
                            upto(act, o_mm, b, 16, 4 * g + j - 1)
                            act.activation(prob[:, j % 2, 2 * half:2 * half + 2, :],
                                           sT_bank[:, 2 * half:2 * half + 2, :], ACT.Exp).then_inc(exp_ok, 1)
                    upto(act, o_mm, b, 16, 4 * g + 4)
                    upto(act, back_mm, b, 4, g)
                    copy(oT[:], o_bank[:]).then_inc(oT_ok, 1)
                upto(act, oc_mm, b, 1, 1)
                copy(ocT[:], misc[:]).then_inc(oc_ok, 1)

            act.wait_ge(loaded, 16 * 9)
            act.wait_ge(boot, 4)
            run(act, batch)

        @block.gpsimd
        def _(pool):
            pool.memset(x_shift[:], 0.0)
            pool.memset(halfneg[:], -0.5)
            pool.memset(eps[:], LN_EPS)
            pool.memset(v_ext[:].rearrange("p t h n -> p (t h n)"), 0.0).then_inc(chain, 1)
            pool.wait_ge(chain, 1)
            pool.memset(v_ext[:, :, :, AD:AD + 1], 1.0).then_inc(boot, 1)

            def batch(b):
                upto(pool, mv_ok, b, 1, 1)
                upto(pool, x1_ok, b, 1, 0)
                pool.tensor_tensor(rstd[:], mv[:, :, 1], eps[:, 0:TPB], ALU.add).then_inc(eps_ok, 1)
                upto(pool, eps_ok, b, 1, 1)
                pool.tensor_tensor(rstd[:], rstd[:], halfneg[:, 0:TPB], ALU.pow).then_inc(rstd_ok, 1)

            run(pool, batch)

        @block.vector
        def _(dve):
            def split(b, part, tok, slots, scale):
                src = sT_bank[:, :, part * C:(part + 1) * C].rearrange("p t (h d) -> p t h d", d=AD)

                def place(n):
                    return tok[:, :, :, n * AD:(n + 1) * AD]

                high, mid, low = slots
                r = rest[:, part].rearrange("p t (h d) -> p t h d", d=AD)
                for t in range(TPB):
                    last = dve.tensor_scalar(place(high[0])[:, t], src[:, t], scale, None, ALU.mult)
                last.then_inc(step_ok, 1)
                upto(dve, step_ok, b, STEPS, 3 * part + 1)
                for t in range(TPB):
                    last = dve.scalar_tensor_tensor(r[:, t], src[:, t], scale, place(high[0])[:, t], ALU.mult,
                                                    ALU.subtract)
                last.then_inc(step_ok, 1)
                upto(dve, step_ok, b, STEPS, 3 * part + 2)
                for t in range(TPB):
                    last = dve.tensor_copy(place(mid[0])[:, t], r[:, t])
                last.then_inc(step_ok, 1)
                upto(dve, step_ok, b, STEPS, 3 * part + 3)
                for t in range(TPB):
                    last = dve.tensor_tensor(place(low[0])[:, t], r[:, t], place(mid[0])[:, t], ALU.subtract)
                for again in high[1:]:
                    for t in range(TPB):
                        last = dve.tensor_copy(place(again)[:, t], place(high[0])[:, t])
                for again in mid[1:]:
                    for t in range(TPB):
                        last = dve.tensor_copy(place(again)[:, t], place(mid[0])[:, t])
                last.then_inc(split_ok, 1)

            def maxima(b, g, i):
                for n in range(4):
                    u = 16 * g + 4 * i + n
                    upto(dve, p1_mm, b, 64, u + 1)
                    if i == 0 and n == 0:
                        upto(dve, m_ok, b, 4, g)
                    dve.tensor_reduce(negmax[:, i, n:n + 1], max_bank[u % 2][:], AX.X, ALU.max,
                                      negate=True).then_inc(max_ok, 1)

            def split_maxima(b, g):
                upto(dve, max_ok, b, 64, 16 * g + 16)
                upto(dve, m_mm, b, 4, g)
                n = 6 + 3 * g
                dve.tensor_copy(m_tok[:, :, 0, :], negmax[:]).then_inc(step_ok, 1)
                upto(dve, step_ok, b, STEPS, n + 1)
                dve.tensor_tensor(m_rest[:], negmax[:], m_tok[:, :, 0, :], ALU.subtract).then_inc(step_ok, 1)
                upto(dve, step_ok, b, STEPS, n + 2)
                dve.tensor_copy(m_tok[:, :, 1, :], m_rest[:]).then_inc(step_ok, 1)
                upto(dve, step_ok, b, STEPS, n + 3)
                dve.tensor_tensor(m_tok[:, :, 2, :], m_rest[:], m_tok[:, :, 1, :], ALU.subtract).then_inc(m_ok, 1)

            def divide(b, g):
                upto(dve, back_mm, b, 4, g + 1)
                upto(dve, o_ok, b, 4, g)
                src = misc[:].rearrange("p t (h n) -> p t h n", n=32)
                dve.reciprocal(rden[:], src[:, :, :, AD]).then_inc(rden_ok, 1)
                upto(dve, rden_ok, b, 4, g + 1)
                if g == 0:
                    upto(dve, oc_mm, b, 1, 0)
                dve.tensor_tensor(o_tok[:, :, 4 * g:4 * g + 4, :], src[:, :, :, 0:AD],
                                  rden[:].unsqueeze(3).broadcast_to([P, TPB, 4, AD]), ALU.mult).then_inc(o_ok, 1)

            def batch(b):
                upto(dve, qkv_mm, b, 1, 1)
                upto(dve, turn_mm, b, 8, 0)
                upto(dve, v_ok, b, 1, 1)
                split(b, 0, q_tok, ((0, 1, 4), (2, 3), (5,)), float(AD) ** -0.5)
                split(b, 1, k_tok, ((0, 2, 5), (1, 3), (4,)), 1.0)
                for n in range(4):
                    upto(dve, turn_mm, b, 8, n + 5)
                    for a in range(2):
                        src = sT_bank[64 * a:64 * a + 64, n, :].bitcast(BF16).rearrange("p (k l) -> p k l", k=2)
                        last = dve.tensor_copy(kT[0:64, 4 * n + a:4 * n + a + 3:2, :], src)
                    last.then_inc(kT_ok, 1)
                for i in range(TPB):
                    maxima(b, 0, i)
                split_maxima(b, 0)
                for g in range(4):
                    if g < 3:
                        maxima(b, g + 1, 0)
                    if g:
                        divide(b, g - 1)
                    if g < 3:
                        for i in range(1, TPB):
                            maxima(b, g + 1, i)
                        split_maxima(b, g + 1)
                divide(b, 3)
                upto(dve, y_mm, b, 1, 1)
                dve.tensor_tensor(total[:], misc[:], rows(b), ALU.add).then_inc(sum_ok, 1)
                upto(dve, sum_ok, b, 1, 1)
                dve.tensor_tensor(total[:], total[:], bo_sb[:].unsqueeze(1).broadcast_to([P, TPB, C]),
                                  ALU.add).then_inc(res_ok, 1)
                upto(dve, res_ok, b, 1, 1)
                upto(dve, rstd_ok, b, 1, 0)
                for t in range(TPB):
                    last = dve.bn_stats(stats[:, t, :], total[:, t, :])
                last.then_inc(bn_ok, 1)
                dve.wait_ge(boot, 4)
                upto(dve, bn_ok, b, 1, 1)
                for t in range(TPB):
                    last = dve.bn_aggr(mv[:, t, :], stats[:, t, :])
                last.then_inc(mv_ok, 1)
                upto(dve, rstd_ok, b, 1, 1)
                upto(dve, x1T_mm, b, 1, 0)
                for t in range(TPB):
                    last = dve.tensor_scalar(x1[:, t, :], total[:, t, :], mv[:, t, 0:1], rstd[:, t:t + 1],
                                             ALU.subtract, ALU.mult)
                last.then_inc(x1_ok, 1)
                upto(dve, x1_ok, b, 1, 1)
                dve.tensor_scalar(rows(b), x1[:], 1.0, None, ALU.mult)
                upto(dve, x1T_mm, b, 1, 1)
                flat = misc[:].rearrange("p t n -> p (t n)")
                dve.tensor_copy(x_shift[0:64, bass.ds(b * XW, L)], flat[0:64])
                dve.tensor_copy(x_shift[64:P, bass.ds(b * XW + 1, L)], flat[64:P]).then_inc(xw_ok, 1)

            dve.memset(q_tok[:].rearrange("p t h n -> p (t h n)"), 0.0).then_inc(boot, 1)
            dve.memset(k_tok[:].rearrange("p t h n -> p (t h n)"), 0.0).then_inc(k_zero, 1)
            dve.wait_ge(k_zero, 1)
            dve.memset(k_tok[:, :, :, 48:51], 1.0).then_inc(boot, 1)
            dve.wait_ge(loaded, 16 * 9)
            dve.tensor_copy(identb[:], ident[:]).then_inc(boot, 1)
            run(dve, batch)


def local_layers(nc, args, state):
    (wqkv, wo, ffn, qk_scales, rot_base, masks) = args
    x_shift, ident, identb, halfneg, eps = state
    with ExitStack() as ctx:
        def sb(name, shape, dt=F32):
            return ctx.enter_context(nc.sbuf_tensor(name, shape, dt))

        def sem(name):
            return ctx.enter_context(nc.semaphore(name))

        wqkv_sb = sb("wqkv_sb", [P, 2, 3 * INNER])
        wo_sb = sb("wo_sb", [P, PAIRS * P])
        ffn_sb = sb("ffn_sb", [P, FFN_COLS])
        w1_sb, w2_sb = ffn_sb[:, 0:2 * FF], ffn_sb[:, 2 * FF:2 * FF + FCH * P]
        b_lin, b_gate = (ffn_sb[:, BIAS + FCH * k:BIAS + FCH * (k + 1)] for k in range(2))
        b2_sb, ln_g, ln_b = (ffn_sb[:, BIAS + 2 * FCH + k:BIAS + 2 * FCH + k + 1] for k in range(3))
        scales_sb = sb("scales_sb", [P, DEPTH, 4 * DH])
        base_sb = sb("base_sb", [P, TPB, 4 * DH])
        mask_sb = sb("mask_sb", [P, 2, 512], BF16)
        tiny = sb("tiny", [P, 1])
        xs = sb("xs", [P, 2, P])
        sq = sb("sq", [P, 2, INNER])
        ssum = sb("ssum", [P, 2, 2, HEADS])
        rlog = sb("rlog", [P, 2, HEADS])
        rnorm = sb("rnorm", [P, 2, 2, HEADS])
        tab = sb("tab", [P, 2, 4 * DH])
        qkn = sb("qkn", [P, 2, INNER])
        t_cos = sb("t_cos", [P, 2, INNER])
        rot = sb("rot", [P, 2, INNER])
        t_sin = sb("t_sin", [P, 2, INNER])
        v_tok = sb("v_tok", [P, 2, INNER])
        v_pad = sb("v_pad", [P, 2, WPT, PAIRS * P])
        qT = sb("qT", [P, PAIRS, P])
        kT = sb("kT", [P, 2, PAIRS, 2, WIN + P])
        s_max = sb("s_max", [P, HEADS])
        s_sub = sb("s_sub", [P, HEADS * 2 * WIN])
        prob = sb("prob", [P, 2, HEADS * 2 * WIN])
        den = sb("den", [P, 2, HEADS])
        rden = sb("rden", [P, 2, HEADS])
        probT = sb("probT", [P, PAIRS, P])
        o_tok = sb("o_tok", [P, INNER])
        oT = sb("oT", [P, PAIRS, P])
        xs2 = sb("xs2", [P, 2, P])
        stats = sb("stats", [P, 6])
        mv = sb("mv", [P, 2])
        rstd = sb("rstd", [P, 1])
        xn = sb("xn", [P, P])
        xnT = sb("xnT", [P, P])
        gelu = sb("gelu", [P, FCH, P])
        hid = sb("hid", [P, FCH, P])
        bank = [ctx.enter_context(nc.psum_tensor(f"bank{i}", [P, 2, 512], F32)) for i in range(4)]
        b01, b23, b45, b67 = bank

        qkv_loaded, wo_loaded, ffn_loaded, c_loaded = map(sem, ["qkv_loaded", "wo_loaded", "ffn_loaded", "c_loaded"])
        q_mm, k_mm, v_mm, qT_mm, kT_mm, s1_mm, s_mm = map(sem, ["q_mm", "k_mm", "v_mm", "qT_mm", "kT_mm", "s1_mm", "s_mm"])
        pT_mm, o_mm, oT_mm, y_mm = map(sem, ["pT_mm", "o_mm", "oT_mm", "y_mm"])
        ln_mm, xnT_mm, h_mm, z_mm = map(sem, ["ln_mm", "xnT_mm", "h_mm", "z_mm"])
        xs_ok, sqq_ok, sqk_ok, v_ok, qT_ok, kT_ok = map(sem, ["xs_ok", "sqq_ok", "sqk_ok", "v_ok", "qT_ok", "kT_ok"])
        exp_ok, pT_ok, oT_ok, gelu_ok = map(sem, ["exp_ok", "pT_ok", "oT_ok", "gelu_ok"])
        ssq_ok, ssk_ok, qn_ok, kn_ok, cosq_ok, cosk_ok = map(sem, ["ssq_ok", "ssk_ok", "qn_ok", "kn_ok", "cosq_ok", "cosk_ok"])
        max1_ok, max2_ok, sub_ok, den_ok, rden_ok, o_ok, xa_ok, xs2_ok = map(sem, ["max1_ok", "max2_ok", "sub_ok", "den_ok", "rden_ok", "o_ok", "xa_ok", "xs2_ok"])
        bn_ok, mv_ok, xn_ok, xnT_ok, hid_ok = map(sem, ["bn_ok", "mv_ok", "xn_ok", "xnT_ok", "hid_ok"])
        xf_ok = sem("xf_ok")
        tab_ok, lnq_ok, rq_ok, lnk_ok, rk_ok, sinq_ok, sink_ok, rotq_ok, rotk_ok, eps_ok, rstd_ok = map(
            sem, ["tab_ok", "lnq_ok", "rq_ok", "lnk_ok", "rk_ok", "sinq_ok", "sink_ok", "rotq_ok", "rotk_ok", "eps_ok", "rstd_ok"])
        vpad_ok, init_ok = [sem("vpad0_ok"), sem("vpad1_ok")], sem("init_ok")

        def done(eng, s, t, back=0, credit=0):
            count = t + 1 - back
            if isinstance(count, int):
                if count <= 0:
                    return
                count = min(count, TILES)
            eng.wait_ge(s, count + credit)

        def behind_constant(eng, s, t):
            eng.wait_ge(c_loaded, 48)
            eng.wait_ge(s, t + 1)

        def spread(eng, t, s):
            if isinstance(t, int) and t < 0:
                return
            eng.wait_ge(vpad_ok[s], (t // 2 + 1) * (16 * 4 * WPT))

        def weights(eng, loaded, t):
            eng.wait_ge(loaded, (t // TPL + 1) * 16)

        def par(t):
            return bass.ds((t // TPL) % 2, 1)

        def run(eng, step):
            for x in range(FIRST):
                step(x, x % 2)
            with eng.Fori(FIRST // 2, TILES // 2) as two:
                step(2 * two, 0)
                step(2 * two + 1, 1)
            for x in range(TILES, TILES + LAG):
                step(x, x % 2)

        def live(t):
            return not isinstance(t, int) or 0 <= t < TILES

        def state_cols(t, lo, hi, shift=0):
            return x_shift[lo:hi, bass.ds(((t // TPB) % B) * XW + (t % TPB) * P + shift, P)]

        block = ctx.enter_context(nc.Block())

        @block.sync
        def _(sp):
            def of(a, layer):
                return a[bass.ds(layer, 1)].rearrange("l p n -> (l p) n")

            def load_qkv(layer):
                sp.dma_start(wqkv_sb[:, bass.ds(layer % 2, 1)].rearrange("p l n -> p (l n)"),
                             of(wqkv, layer)).then_inc(qkv_loaded, 16)

            def load_wo(layer):
                sp.dma_start(wo_sb[:], of(wo, layer)).then_inc(wo_loaded, 16)

            def load_ffn(layer):
                sp.dma_start(ffn_sb[:], of(ffn, layer)).then_inc(ffn_loaded, 16)

            def spread_two(two):
                spread_v(2 * two, 0)
                spread_v(2 * two + 1, 1)

            def layer_of_values(layer, next_qkv):
                first = layer * TPL
                spread_v(first, 0)
                spread_v(first + 1, 1)
                sp.wait_ge(y_mm, first)
                load_wo(layer)
                spread_v(first + 2, 0)
                sp.wait_ge(xf_ok, first + TPL)
                load_ffn(layer)
                if next_qkv:
                    load_qkv(layer + 1)
                spread_v(first + 3, 1)
                with sp.Fori(layer * (TPL // 2) + 2, (layer + 1) * (TPL // 2)) as two:
                    spread_two(two)

            def spread_v(t, s):
                sp.wait_ge(v_ok, t + 1)
                sp.wait_ge(o_mm, t + 1)
                for a in range(2):
                    for w in range(WPT):
                        for c in range(2):
                            src_w = w + c - 1
                            slot = s if src_w >= 0 else 1 - s
                            lo = (src_w % WPT) * WIN
                            dst = v_pad[64 * a + WIN * c:64 * a + WIN * c + WIN, s, w].rearrange(
                                "p (q n) -> p q n", n=P)[:, :, a * DH:(a + 1) * DH]
                            src = v_tok[lo:lo + WIN, slot, a * 512:(a + 1) * 512].rearrange(
                                "p (q n) -> p q n", n=DH)
                            sp.dma_start(dst, src).then_inc(vpad_ok[s], 16)

            sp.dma_start(scales_sb[:], qk_scales.rearrange("a (l n) -> a l n", l=DEPTH).broadcast_to(
                [P, DEPTH, 4 * DH])).then_inc(c_loaded, 16)
            sp.dma_start(base_sb[:], rot_base).then_inc(c_loaded, 16)
            sp.dma_start(mask_sb[:].bitcast(U16), masks).then_inc(c_loaded, 16)
            load_qkv(0)
            load_wo(0)
            load_ffn(0)
            sp.wait_ge(qkv_loaded, 16)
            load_qkv(1)
            sp.wait_ge(init_ok, 4)
            spread_two(0)
            with sp.Fori(1, TPL // 2) as two:
                spread_two(two)
            with sp.Fori(1, DEPTH - 1) as layer:
                layer_of_values(layer, True)
            layer_of_values(DEPTH - 1, False)

        @block.tensor
        def _(pe):
            def project(t, s, part, out, mm):
                for j in range(2):
                    c = part * INNER + j * 512
                    last = pe.matmul(out[:, j, :], xs[:, s, :],
                                     wqkv_sb[:, par(t), c:c + 512].rearrange("p l n -> p (l n)"),
                                     start=True, stop=True)
                last.then_inc(mm, 1)

            def turn_pairs(out, a, mm):
                for p in range(PAIRS):
                    last = pe.matmul(out[:, p // 4, (p % 4) * P:(p % 4 + 1) * P], a[:, p * P:(p + 1) * P],
                                     ident[:], start=True, stop=True, is_transpose=True)
                last.then_inc(mm, 1)

            def scores(b, r, j):
                which = (b % TPB) // 2 if r == 0 else 1
                pe.matmul(b45[:, j, :], identb[:], mask_sb[:, bass.ds(which, 1), :].rearrange("p l n -> p (l n)"),
                          start=True, stop=False, skip_group_check=True)
                for p in range(4):
                    for w in range(WPT):
                        last = pe.matmul(b45[WIN * w:WIN * w + WIN, j, p * P:(p + 1) * P],
                                         qT[:, 4 * j + p, WIN * w:WIN * w + WIN],
                                         kT[:, r, 4 * j + p, :, WIN * w:WIN * w + 2 * WIN],
                                         start=False, stop=True, skip_group_check=True)
                return last

            def step(x, s):
                a, b, c, e, g = x, x - 1, x - 2, x - 3, x - 4
                r = 1 - s
                if live(a):
                    weights(pe, qkv_loaded, a)
                    done(pe, xs_ok, a)
                    done(pe, o_ok, a, 3)
                    if isinstance(a, int):
                        done(pe, v_ok, a, 1)
                    project(a, s, 0, b01, q_mm)
                if live(a):
                    done(pe, oT_ok, a, 3)
                    if isinstance(a, int):
                        done(pe, kn_ok, a, 1)
                    project(a, s, 1, b23, k_mm)
                if live(e):
                    weights(pe, wo_loaded, e)
                    done(pe, oT_ok, e)
                    done(pe, sub_ok, e + 1)
                    for p in range(PAIRS):
                        last = pe.matmul(b45[:, 1, 0:P], wo_sb[:, p * P:(p + 1) * P], oT[:, p, :],
                                         start=(p == 0), stop=(p == PAIRS - 1))
                    last.then_inc(y_mm, 1)
                if live(g):
                    done(pe, hid_ok, g)
                    done(pe, sub_ok, g + 2)
                    for j in range(FCH):
                        n = min(P, FF - j * P)
                        last = pe.matmul(b45[:, 0, 0:P], w2_sb[0:n, j * P:(j + 1) * P], hid[0:n, j, :],
                                         start=(j == 0), stop=(j == FCH - 1))
                    last.then_inc(z_mm, 1)
                if live(b):
                    done(pe, rotk_ok, b)
                    done(pe, hid_ok, b, 3)
                    if isinstance(b, int):
                        done(pe, kT_ok, b, 1)
                    turn_pairs(b67, rot[:, 1], kT_mm)
                    done(pe, rotq_ok, b)
                    done(pe, xa_ok, b, 2)
                    pe.wait_ge(xf_ok, b - 2 + TPL)
                    if isinstance(b, int):
                        done(pe, sub_ok, b, 1)
                    turn_pairs(b45, rot[:, 0], qT_mm)
                if live(a):
                    done(pe, sqq_ok, a)
                    done(pe, qn_ok, a)
                    project(a, s, 2, b01, v_mm)
                if live(e):
                    done(pe, xs2_ok, e)
                    done(pe, kT_ok, e + 2)
                    pe.matmul(b67[:, 0, 0:P], xs2[:, r, :], ident[:], start=True, stop=True,
                              is_transpose=True).then_inc(ln_mm, 1)
                if live(b):
                    done(pe, qT_ok, b)
                    done(pe, kT_ok, b)
                    scores(b, r, 0).then_inc(s1_mm, 1)
                if live(c):
                    done(pe, exp_ok, c)
                    done(pe, sqk_ok, c + 2)
                    done(pe, kn_ok, c + 2)
                    turn_pairs(b23, prob[:, s], pT_mm)
                if live(b):
                    scores(b, r, 1).then_inc(s_mm, 1)
                if live(e):
                    done(pe, xn_ok, e)
                    pe.matmul(b67[:, 1, 0:P], xn[:], ident[:], start=True, stop=True,
                              is_transpose=True).then_inc(xnT_mm, 1)
                if live(c):
                    done(pe, pT_ok, c)
                    done(pe, v_ok, c + 2)
                    spread(pe, c, s)
                    for p in range(PAIRS):
                        for w in range(WPT):
                            last = pe.matmul(b01[WIN * w:WIN * w + WIN, p // 4, (p % 4) * P:(p % 4 + 1) * P],
                                             probT[:, p, WIN * w:WIN * w + WIN],
                                             v_pad[:, s, w, p * P:(p + 1) * P],
                                             start=True, stop=True, skip_group_check=True)
                    last.then_inc(o_mm, 1)
                if live(e):
                    weights(pe, ffn_loaded, e)
                    done(pe, xnT_ok, e)
                    for half in (1, 0):
                        for j in range(FCH):
                            n = min(P, FF - j * P)
                            last = pe.matmul(b67[0:n, half, j * P:(j + 1) * P],
                                             w1_sb[:, half * FF + j * P:half * FF + j * P + n], xnT[:],
                                             start=True, stop=True)
                    last.then_inc(h_mm, 1)
                if live(c):
                    done(pe, o_ok, c)
                    turn_pairs(b23, o_tok[:], oT_mm)

            pe.sem_inc(o_mm, 2)
            pe.wait_ge(c_loaded, 48)
            run(pe, step)

        @block.scalar
        def _(act):
            def copy(out, in_):
                return act.activation(out, in_, ACT.Copy)

            def flat(bank):
                return bank[:].rearrange("p j n -> p (j n)")

            def load_xs(t, s):
                done(act, v_mm, t, 2)
                act.wait_ge(xf_ok, t + 1)
                copy(xs[:, s, :], state_cols(t, 0, P)).then_inc(xs_ok, 1)

            def inv_root(t, s, i, ssum_ok, ln_ok, root_ok):
                done(act, ssum_ok, t)
                act.activation(rlog[:, i, :], ssum[:, s, i, :], ACT.Ln, bias=tiny[:]).then_inc(ln_ok, 1)
                done(act, ln_ok, t)
                act.activation(rnorm[:, s, i, :], rlog[:, i, :], ACT.Exp, scale=-0.5).then_inc(root_ok, 1)

            def step(x, s):
                a, b, c, e = x, x - 1, x - 2, x - 3
                r = 1 - s
                if live(a):
                    done(act, q_mm, a)
                    done(act, ssq_ok, a, 1)
                    act.activation(sq[:, 0, :], flat(b01), ACT.Square).then_inc(sqq_ok, 1)
                    done(act, k_mm, a)
                    done(act, ssk_ok, a, 1)
                    act.activation(sq[:, 1, :], flat(b23), ACT.Square).then_inc(sqk_ok, 1)
                act.preload_act_table_set("natural_log_exp_and_others")
                if live(a):
                    inv_root(a, s, 0, ssq_ok, lnq_ok, rq_ok)
                    inv_root(a, s, 1, ssk_ok, lnk_ok, rk_ok)
                if live(b):
                    done(act, kT_mm, b)
                    done(act, s_mm, b, 1)
                    for h in range(2):
                        src = flat(b67)[64 * h:64 * h + 64].rearrange("p (q n) -> p q n", n=P)
                        copy(kT[64 * h:64 * h + 64, r, :, h, WIN:WIN + P], src)
                        last = copy(kT[64 * h:64 * h + 64, s, :, h, 0:WIN], src[:, :, P - WIN:P])
                    last.then_inc(kT_ok, 1)
                    done(act, qT_mm, b)
                    done(act, s_mm, b, 1)
                    copy(qT[:].rearrange("p q n -> p (q n)"), flat(b45)).then_inc(qT_ok, 1)
                if live(a):
                    done(act, v_mm, a)
                    spread(act, a - 1, r)
                    spread(act, a - 2, s)
                    copy(v_tok[:, s, :], flat(b01)).then_inc(v_ok, 1)
                if live(c):
                    done(act, pT_mm, c)
                    done(act, o_mm, c, 1, credit=2)
                    copy(probT[:].rearrange("p q n -> p (q n)"), flat(b23)).then_inc(pT_ok, 1)
                if not isinstance(a, int) or a + 1 < TILES:
                    load_xs(a + 1, r)
                if live(b):
                    done(act, sub_ok, b)
                    done(act, pT_mm, b, 2)
                    done(act, den_ok, b, 2)
                    act.activation(prob[:, r, :], s_sub[:], ACT.Exp, scale=8.0).then_inc(exp_ok, 1)
                act.preload_act_table(ACT.Gelu)
                if live(c):
                    done(act, oT_mm, c)
                    done(act, y_mm, c, 1)
                    copy(oT[:].rearrange("p q n -> p (q n)"), flat(b23)).then_inc(oT_ok, 1)
                if live(e):
                    weights(act, ffn_loaded, e)
                    done(act, h_mm, e)
                    done(act, hid_ok, e, 1)
                    for j in range(FCH):
                        n = min(P, FF - j * P)
                        last = act.activation(gelu[0:n, j, :], b67[0:n, 1, j * P:(j + 1) * P], ACT.Gelu,
                                              bias=b_gate[0:n, j:j + 1])
                    last.then_inc(gelu_ok, 1)

            act.wait_ge(init_ok, 4)
            load_xs(0, 0)
            run(act, lambda x, s: step(x, s))

        @block.gpsimd
        def _(pool):
            def add_halves(t, i, sin_ok, cos_ok, mm, rot_ok):
                done(pool, sin_ok, t)
                done(pool, cos_ok, t)
                done(pool, mm, t, 1)
                pool.tensor_tensor(rot[:, i, :], t_cos[:, i, :], t_sin[:, i, :], ALU.add).then_inc(rot_ok, 1)

            def table(t, s):
                done(pool, cosk_ok, t, 2)
                pool.tensor_tensor(tab[:, s, :], base_sb[:, bass.ds(t % TPB, 1), :].rearrange("p l n -> p (l n)"),
                                   scales_sb[:, bass.ds((t // TPL) % DEPTH, 1), :].rearrange("p l n -> p (l n)"),
                                   ALU.mult).then_inc(tab_ok, 1)

            def rotate(t, s, i, n_ok, rot_ok, sin_ok):
                done(pool, n_ok, t)
                src = qkn[:, i, :].rearrange("p (h g n) -> p h g n", g=2, n=DH // 2)
                dst = t_sin[:, i, :].rearrange("p (h g n) -> p h g n", g=2, n=DH // 2)
                for g in range(2):
                    c = (2 * i + 1) * DH + g * (DH // 2)
                    w = tab[:, s, c:c + DH // 2].unsqueeze(1).broadcast_to([P, HEADS, DH // 2])
                    last = pool.tensor_tensor(dst[:, :, g, :], src[:, :, 1 - g, :], w, ALU.mult)
                last.then_inc(sin_ok, 1)

            def step(x, s):
                a, e = x, x - 3
                if live(e):
                    done(pool, mv_ok, e)
                    done(pool, xn_ok, e, 1)
                    pool.tensor_tensor(rstd[:], mv[:, 1:2], eps[:, 0:1], ALU.add).then_inc(eps_ok, 1)
                    done(pool, eps_ok, e)
                    pool.tensor_tensor(rstd[:], rstd[:], halfneg[:, 0:1], ALU.pow).then_inc(rstd_ok, 1)
                if live(a):
                    done(pool, tab_ok, a)
                    rotate(a, s, 0, qn_ok, rotq_ok, sinq_ok)
                    rotate(a, s, 1, kn_ok, rotk_ok, sink_ok)
                    add_halves(a, 0, sinq_ok, cosq_ok, qT_mm, rotq_ok)
                    add_halves(a, 1, sink_ok, cosk_ok, kT_mm, rotk_ok)
                if not isinstance(a, int) or a + 1 < TILES:
                    table(a + 1, 1 - s)

            pool.memset(tiny[:], 1e-37).then_inc(init_ok, 1)
            pool.memset(v_pad[:].rearrange("p a b c -> p (a b c)"), 0.0).then_inc(init_ok, 1)
            pool.wait_ge(c_loaded, 48)
            table(0, 0)
            run(pool, step)

        @block.vector
        def _(dve):
            def heads(ap, n=DH):
                return ap.rearrange("p (h n) -> p h n", n=n)

            def wide(ap, n=DH):
                return ap.unsqueeze(2).broadcast_to([P, HEADS, n])

            def flat(bank):
                return bank[:].rearrange("p j n -> p (j n)")

            def sum_squares(t, s, i, sq_ok, out_ok):
                done(dve, sq_ok, t)
                dve.tensor_reduce(ssum[:, s, i, :], heads(sq[:, i, :]), AX.X, ALU.add).then_inc(out_ok, 1)

            def normalize(t, s, i, bank, root_ok, n_ok, sin_ok, cos_ok):
                done(dve, root_ok, t)
                done(dve, sin_ok, t, 1)
                done(dve, cos_ok, t, 1)
                dve.scalar_tensor_tensor(heads(qkn[:, i, :]), wide(rnorm[:, s, i, :]), 1e12, heads(flat(bank)),
                                         ALU.min, ALU.mult).then_inc(n_ok, 1)

            def cosine(t, s, i, n_ok, rot_ok, cos_ok):
                done(dve, n_ok, t)
                done(dve, rot_ok, t, 1)
                w = tab[:, s, 2 * i * DH:(2 * i + 1) * DH].unsqueeze(1).broadcast_to([P, HEADS, DH])
                dve.tensor_tensor(heads(t_cos[:, i, :]), heads(qkn[:, i, :]), w, ALU.mult).then_inc(cos_ok, 1)

            def row_maxima(t, j, mm, out_ok):
                done(dve, mm, t)
                dve.tensor_reduce(s_max[:, 8 * j:8 * j + 8], heads(b45[:, j, :]), AX.X, ALU.max).then_inc(out_ok, 1)

            def less_maxima(t, j, m_ok):
                done(dve, m_ok, t)
                done(dve, exp_ok, t, 1)
                return dve.tensor_tensor(heads(s_sub[:, 512 * j:512 * j + 512]), heads(b45[:, j, :]),
                                         s_max[:, 8 * j:8 * j + 8].unsqueeze(2).broadcast_to([P, 8, DH]), ALU.subtract)

            def step(x, s):
                a, b, c, e, g = x, x - 1, x - 2, x - 3, x - 4
                r = 1 - s
                if live(a):
                    sum_squares(a, s, 0, sqq_ok, ssq_ok)
                    sum_squares(a, s, 1, sqk_ok, ssk_ok)
                if live(e):
                    done(dve, y_mm, e)
                    if not isinstance(e, int) or e + 1 < TILES:
                        done(dve, xs_ok, e + 1)
                    done(dve, xs2_ok, e, 1)
                    lo, hi = state_cols(e, 0, 64), state_cols(e, 64, P, 1)
                    dve.tensor_tensor(lo, b45[0:64, 1, 0:P], lo, ALU.add)
                    dve.tensor_tensor(hi, b45[64:P, 1, 0:P], hi, ALU.add).then_inc(xa_ok, 1)
                    done(dve, xa_ok, e)
                    done(dve, ln_mm, e, 2)
                    dve.tensor_scalar(xs2[:, r, :], state_cols(e, 0, P), 1.0, None, ALU.mult).then_inc(xs2_ok, 1)
                if live(g):
                    done(dve, z_mm, g)
                    if not isinstance(g, int) or g + 1 < TILES:
                        done(dve, xs2_ok, g + 1)
                    lo, hi = state_cols(g, 0, 64), state_cols(g, 64, P, 1)
                    dve.scalar_tensor_tensor(lo, b45[0:64, 0, 0:P], b2_sb[0:64], lo, ALU.add, ALU.add)
                    dve.scalar_tensor_tensor(hi, b45[64:P, 0, 0:P], b2_sb[64:P], hi, ALU.add,
                                             ALU.add).then_inc(xf_ok, 1)
                if live(a):
                    normalize(a, s, 0, b01, rq_ok, qn_ok, sinq_ok, cosq_ok)
                    normalize(a, s, 1, b23, rk_ok, kn_ok, sink_ok, cosk_ok)
                if live(e):
                    done(dve, ln_mm, e)
                    done(dve, rstd_ok, e, 1)
                    dve.bn_stats(stats[:], b67[:, 0, 0:P]).then_inc(bn_ok, 1)
                    behind_constant(dve, bn_ok, e)
                    dve.bn_aggr(mv[:], stats[:]).then_inc(mv_ok, 1)
                if live(a):
                    done(dve, tab_ok, a)
                    cosine(a, s, 0, qn_ok, rotq_ok, cosq_ok)
                    cosine(a, s, 1, kn_ok, rotk_ok, cosk_ok)
                if live(e):
                    done(dve, rstd_ok, e)
                    done(dve, xnT_mm, e, 1)
                    dve.tensor_scalar(xn[:], b67[:, 0, 0:P], mv[:, 0:1], rstd[:], ALU.subtract,
                                      ALU.mult).then_inc(xn_ok, 1)
                if live(b):
                    row_maxima(b, 0, s1_mm, max1_ok)
                    less_maxima(b, 0, max1_ok)
                if live(b):
                    row_maxima(b, 1, s_mm, max2_ok)
                if live(e):
                    weights(dve, ffn_loaded, e)
                    done(dve, xnT_mm, e)
                    done(dve, h_mm, e, 1)
                    dve.tensor_scalar(xnT[:], b67[:, 1, 0:P], ln_g, ln_b, ALU.mult, ALU.add).then_inc(xnT_ok, 1)
                if live(b):
                    less_maxima(b, 1, max2_ok).then_inc(sub_ok, 1)
                if live(c):
                    done(dve, o_mm, c, credit=2)
                    done(dve, rden_ok, c)
                    done(dve, oT_mm, c, 1)
                    dve.tensor_tensor(heads(o_tok[:]), heads(flat(b01)), wide(rden[:, s, :]),
                                      ALU.mult).then_inc(o_ok, 1)
                if live(b):
                    done(dve, exp_ok, b)
                    dve.tensor_reduce(den[:, r, :], heads(prob[:, r, :]), AX.X, ALU.add).then_inc(den_ok, 1)
                    done(dve, den_ok, b)
                    dve.reciprocal(rden[:, r, :], den[:, r, :]).then_inc(rden_ok, 1)
                if live(e):
                    done(dve, gelu_ok, e)
                    done(dve, z_mm, e, 1)
                    for j in range(FCH):
                        n = min(P, FF - j * P)
                        last = dve.scalar_tensor_tensor(hid[0:n, j, :], b67[0:n, 0, j * P:(j + 1) * P],
                                                        b_lin[0:n, j:j + 1], gelu[0:n, j, :], ALU.add, ALU.mult)
                    last.then_inc(hid_ok, 1)

            dve.sem_inc(xf_ok, TPL)
            dve.memset(kT[:].rearrange("p a b c d -> p (a b c d)"), 0.0).then_inc(init_ok, 1)
            dve.memset(v_tok[:].rearrange("p a b -> p (a b)"), 0.0).then_inc(init_ok, 1)
            dve.wait_ge(c_loaded, 48)
            run(dve, step)


def last_norm(nc, out, x_shift, x1_tok, ident, halfneg, eps):
    out_v = out.rearrange("b (t p) c -> b p t c", p=P)
    with ExitStack() as ctx:
        def sb(name, shape, dt=F32):
            return ctx.enter_context(nc.sbuf_tensor(name, shape, dt))

        def sem(name):
            return ctx.enter_context(nc.semaphore(name))

        feat = sb("feat", [P, TPB, P])
        total = sb("total", [P, TPB, P])
        stats = sb("f_stats", [P, TPB, 6])
        mv = sb("f_mv", [P, TPB, 2])
        rstd = sb("f_rstd", [P, TPB])
        y = sb("f_y", [P, B, TPB, P])
        turned = ctx.enter_context(nc.psum_tensor("f_turned", [P, TPB, P], F32))
        feat_ok, turn_mm, sum_ok, bn_ok, mv_ok, eps_ok, rstd_ok, y_ok, stored = map(
            sem, ["feat_ok", "turn_mm", "sum_ok", "f_bn_ok", "f_mv_ok", "f_eps_ok", "f_rstd_ok", "f_y_ok", "stored"])
        block = ctx.enter_context(nc.Block())

        @block.scalar
        def _(act):
            for b in range(B):
                if b:
                    act.wait_ge(turn_mm, b)
                act.activation(feat[0:64].rearrange("p t n -> p (t n)"), x_shift[0:64, b * XW:b * XW + L], ACT.Copy)
                act.activation(feat[64:P].rearrange("p t n -> p (t n)"), x_shift[64:P, b * XW + 1:b * XW + 1 + L],
                               ACT.Copy).then_inc(feat_ok, 1)

        @block.tensor
        def _(pe):
            for b in range(B):
                pe.wait_ge(feat_ok, b + 1)
                if b:
                    pe.wait_ge(sum_ok, b)
                for t in range(TPB):
                    last = pe.matmul(turned[:, t, :], feat[:, t, :], ident[:], start=True, stop=True,
                                     is_transpose=True)
                last.then_inc(turn_mm, 1)

        @block.vector
        def _(dve):
            for b in range(B):
                dve.wait_ge(turn_mm, b + 1)
                if b:
                    dve.wait_ge(y_ok, b)
                dve.tensor_tensor(total[:], turned[:], x1_tok[:, b * TPB:(b + 1) * TPB, :], ALU.add).then_inc(sum_ok, 1)
                dve.wait_ge(sum_ok, b + 1)
                for t in range(TPB):
                    last = dve.bn_stats(stats[:, t, :], total[:, t, :])
                last.then_inc(bn_ok, 1)
                dve.wait_ge(bn_ok, b + 1)
                for t in range(TPB):
                    last = dve.bn_aggr(mv[:, t, :], stats[:, t, :])
                last.then_inc(mv_ok, 1)
                dve.wait_ge(rstd_ok, b + 1)
                for t in range(TPB):
                    last = dve.tensor_scalar(y[:, b, t, :], total[:, t, :], mv[:, t, 0:1], rstd[:, t:t + 1],
                                             ALU.subtract, ALU.mult)
                last.then_inc(y_ok, 1)

        @block.gpsimd
        def _(pool):
            for b in range(B):
                pool.wait_ge(mv_ok, b + 1)
                if b:
                    pool.wait_ge(y_ok, b)
                pool.tensor_tensor(rstd[:], mv[:, :, 1], eps[:], ALU.add).then_inc(eps_ok, 1)
                pool.wait_ge(eps_ok, b + 1)
                pool.tensor_tensor(rstd[:], rstd[:], halfneg[:, 0:TPB], ALU.pow).then_inc(rstd_ok, 1)

        @block.sync
        def _(sp):
            for b in range(B):
                sp.wait_ge(y_ok, b + 1)
                sp.dma_start(out_v[b], y[:, b]).then_inc(stored, 16)
            sp.wait_ge(stored, 16 * B)


def bf16_bits(a):
    return (np.ascontiguousarray(a, dtype=np.float32).view(np.uint32) >> 16).astype(np.uint16)


def rotary_base():
    half = np.arange(0, DH, 2, dtype=np.float32)
    inv_freq = (np.float32(1.0) / np.power(np.float32(10000.0), half / np.float32(DH))).astype(np.float32)
    t = np.arange(L, dtype=np.float32)
    freqs = t[:, None] * inv_freq[None, :]
    freqs = np.concatenate([freqs, freqs], -1)
    base = (half + np.float32(0.4 * DH)) / np.float32(1.4 * DH)
    power = (t - L // 2) / np.float32(WIN // 2)
    scale = np.power(base[None, :], power[:, None]).astype(np.float32)
    scale = np.concatenate([scale, scale], -1)
    sign = np.concatenate([-np.ones(DH // 2), np.ones(DH // 2)]).astype(np.float32)
    cos, sin = np.cos(freqs), np.sin(freqs) * sign
    inv = np.float32(1.0) / scale
    rows = np.concatenate([cos * scale, sin * scale, cos * inv, sin * inv], -1).astype(np.float32)
    return np.ascontiguousarray(rows.reshape(TPB, P, 4 * DH).transpose(1, 0, 2))


def window_masks():
    i = np.arange(P)[:, None] % WIN
    j = np.arange(2 * WIN)[None, :]
    ok = (j >= i) & (j <= i + WIN)
    first = ok & ~((np.arange(P)[:, None] < WIN) & (j < WIN))
    low = np.float32(-(2.0 ** 100))
    rows = np.stack([np.tile(np.where(m, np.float32(0), low), (1, 8)) for m in (first, ok)], 1)
    return bf16_bits(rows)


def three_parts(a):
    out, a = [], np.asarray(a, dtype=np.float64)
    for _ in range(3):
        part = (a.astype(np.float32).view(np.uint32) & np.uint32(0xFFFF0000)).view(np.float32)
        out.append(part)
        a = a - part
    return out


def alibi_slopes():
    start = 2.0 ** (-2.0 ** (-(np.log2(AH) - 3)))
    return np.array([start * start ** i for i in range(AH)], dtype=np.float32)


def alibi_rows():
    slope = alibi_slopes().astype(np.float64)[:, None]
    pos = np.arange(L)
    tile, inside = pos // P, pos % P
    q_rows, k_rows = [], []
    for i in range(TPB):
        here = (tile == i)[None, :]
        sign = np.where(i > tile, -1.0, 1.0)
        back = np.where(tile > i, -1.0, 1.0)
        for part in three_parts(slope * inside):
            q_rows.append(part * here)
            k_rows.append(np.broadcast_to(sign, (AH, L)))
            q_rows.append(np.broadcast_to(-back, (AH, L)))
            k_rows.append(part * here)
        for part in three_parts(np.broadcast_to(slope, (AH, L))):
            q_rows.append(part * here)
            k_rows.append(np.broadcast_to(-float(P) * np.abs(i - tile), (AH, L)))
    return bf16_bits(np.stack(q_rows)), bf16_bits(np.stack(k_rows))


def alibi_inside():
    k, m = np.arange(P)[:, None], np.arange(P)[None, :]
    relu = np.stack([np.maximum(m - k, 0), np.maximum(k - m, 0)], 1).astype(np.float16).view(np.uint16)
    value = -2.0 * alibi_slopes().astype(np.float64)
    high = value.astype(np.float16)
    low = (value - high).astype(np.float16)
    diag = np.eye(P)[:, None, None, :] * np.stack([high, low], 1)[None, :, :, None]
    return relu, diag.astype(np.float16).view(np.uint16)




def attention_then_local_layers(nc, A, out):
    with ExitStack() as ctx:
        def sb(name, shape, dt=F32):
            return ctx.enter_context(nc.sbuf_tensor(name, shape, dt))

        ident = sb("ident", [P, P])
        identb = sb("identb", [P, P], BF16)
        halfneg = sb("halfneg", [P, HEADS])
        eps = sb("eps", [P, TPB])
        x_shift = sb("x_shift", [P, B * XW])
        x1_tok = sb("x1_tok", [P, TPL, P])
        alibi_attention(nc, (A["x"], A["eye"], A["a_wqkv"], A["a_wo"], A["a_bo"], A["q_const"], A["k_const"],
                             A["relu_const"], A["slope_const"]), (x_shift, x1_tok, ident, identb, halfneg, eps))
        local_layers(nc, (A["wqkv"], A["wo"], A["ffn"], A["scales"], A["rot"], A["masks"]), (x_shift, ident, identb, halfneg, eps))
        last_norm(nc, out, x_shift, x1_tok, ident, halfneg, eps)


def laid_out(i):
    def swapped(a):
        return np.concatenate([a[:, DH // 2:], a[:, :DH // 2]], -1)

    a = {"x": i["L0_attn_q"]}
    a["a_wqkv"] = np.concatenate([i[n].T for n in ("L0_attn_Wq", "L0_attn_Wk", "L0_attn_Wv")], 1)
    a["a_wo"] = i["L0_attn_Wo"].T
    a["a_bo"] = i["L0_attn_bo"].reshape(1, C)
    wqkv = i["L0_ffn_Wqkv"]
    v = wqkv[:, :, 2 * INNER:].reshape(DEPTH, C, PAIRS, 2, DH).transpose(0, 1, 3, 2, 4).reshape(DEPTH, C, INNER)
    a["wqkv"] = np.concatenate([wqkv[:, :, :2 * INNER], v], -1)
    a["wo"] = i["L0_ffn_Wo"].reshape(DEPTH, PAIRS, P, C).transpose(0, 2, 1, 3).reshape(DEPTH, P, PAIRS * C)
    pad = FCH * P - FF
    w2 = np.concatenate([i["L0_ffn_W2"], np.zeros((DEPTH, pad, C), np.float32)], 1)
    w2 = w2.reshape(DEPTH, FCH, P, C).transpose(0, 2, 1, 3).reshape(DEPTH, P, FCH * C)
    b1 = np.concatenate([i["L0_ffn_b1"].reshape(DEPTH, 2, FF), np.zeros((DEPTH, 2, pad), np.float32)], -1)
    b1 = b1.reshape(DEPTH, 2 * FCH, P).transpose(0, 2, 1)
    columns = [i[n][:, :, None] for n in ("L0_ffn_b2", "L0_ffn_ln_g", "L0_ffn_ln_b")]
    a["ffn"] = np.concatenate([i["L0_ffn_W1"], w2, b1] + columns, -1)
    q, k = i["L0_ffn_q_scale"], i["L0_ffn_k_scale"]
    a["scales"] = np.concatenate([q, swapped(q), k, swapped(k)], -1).reshape(1, -1)
    a["eye"] = np.eye(P, dtype=np.float32)
    a["rot"], a["masks"] = rotary_base(), window_masks()
    a["q_const"], a["k_const"] = alibi_rows()
    a["relu_const"], a["slope_const"] = alibi_inside()
    return {n: np.ascontiguousarray(v) for n, v in a.items()}


def kernel(**inputs):
    import concourse.bacc as bacc
    from concourse.bass_utils import run_bass_kernel_spmd

    nc = bacc.Bacc("TRN2", target_bir_lowering=False, num_devices=1)
    arrays = {f"in_{n}": v for n, v in laid_out({n: np.asarray(v) for n, v in inputs.items()}).items()}
    A = {n[3:]: nc.dram_tensor(n, v.shape, mybir.dt.from_np(v.dtype), kind="ExternalInput").ap()
         for n, v in arrays.items()}
    out = nc.dram_tensor("out_0", (B, L, C), F32, kind="ExternalOutput").ap()
    attention_then_local_layers(nc, A, out)
    r = run_bass_kernel_spmd(nc, [arrays], core_ids=[0])
    return r.results[0]["out_0"]
```

```python
from contextlib import ExitStack

import numpy as np

import concourse.bass as bass
from concourse import mybir

F32 = mybir.dt.float32
BF16 = mybir.dt.bfloat16
F16 = mybir.dt.float16
U16 = mybir.dt.uint16
ALU = mybir.AluOpType
ACT = mybir.ActivationFunctionType
AX = mybir.AxisListType

P = 128
B, L, C = 4, 512, 128
TPB = L // P
TPL = B * TPB
LN_EPS = 1e-5
XW = L + 8

AH, AD = 16, 8
AROWS = 64 + 36
SLOPE_PARTS = [1 if (h + 1) * 8 % AH == 0 else 2 for h in range(AH)]
STEPS = 4 * 3

DEPTH = 6
TILES = DEPTH * TPL
HEADS, DH = 16, 64
INNER = HEADS * DH
PAIRS = HEADS // 2
WIN = 32
WPT = P // WIN
FF = int(C * 4 * 2 / 3)
FCH = -(-FF // P)
BIAS = 2 * FF + FCH * P
FFN_COLS = BIAS + 2 * FCH + 3
FIRST, LAG = 6, 4



def alibi_attention(nc, args, state, first_weights):
    x, eye, wqkvT, woT, bo, q_const, k_const, relu_const, slope_const = args
    x_shift, x1_tok, ident, identb, halfneg, eps = state
    with ExitStack() as ctx:
        def sb(name, shape, dt=F32):
            return ctx.enter_context(nc.sbuf_tensor(name, shape, dt))

        def sem(name):
            return ctx.enter_context(nc.semaphore(name))

        w_sb = sb("a_w", [P, 3 * C])
        wo_sb = sb("a_wo", [P, C])
        bo_sb = sb("a_bo", [P, C])
        relu_sb = sb("a_relu", [P, 2, P], F16)
        slope_sb = sb("a_slope", [P, AH, 2, P], F16)
        qT = sb("a_qT", [AROWS, AH, L], BF16)
        kT = sb("a_kT", [AROWS, AH, L], BF16)
        q_tok = sb("a_q_tok", [P, TPB, AH, 64], BF16)
        k_tok = sb("a_k_tok", [P, TPB, AH, 64], BF16)
        qkv = sb("a_qkv", [P, TPL, 3 * C])
        factor = sb("a_factor", [P, 3])
        scaled = sb("a_scaled", [P, 2, TPB, C])
        rest = sb("a_rest", [P, 2, TPB, C])
        v_ext = sb("a_v_ext", [P, TPB, AH, 32])
        xT = sb("a_xT", [P, 2, TPB, P])
        negmax = sb("a_negmax", [P, TPB, 4])
        m_rest = sb("a_m_rest", [P, TPB, 4])
        m_tok = sb("a_m_tok", [P, TPB, 3, 4], BF16)
        mT = sb("a_mT", [12, L], BF16)
        prob = sb("a_prob", [P, 2, 4, L])
        oT = sb("a_oT", [P, L])
        rden = sb("a_rden", [P, TPB, 4])
        o_tok = sb("a_o_tok", [P, TPB, AH, AD])
        ocT = sb("a_ocT", [P, TPB, P])
        total = sb("a_total", [P, TPB, P])
        stats = sb("a_stats", [P, TPB, 6])
        mv = sb("a_mv", [P, TPB, 2])
        rstd = sb("a_rstd", [P, TPB])
        x1 = sb("a_x1", [P, TPB, P])
        max_bank = [ctx.enter_context(nc.psum_tensor(f"a_max{i}", [P, L], F32)) for i in range(2)]
        sT_bank = ctx.enter_context(nc.psum_tensor("a_sT", [P, 4, L], F32))
        o_bank = ctx.enter_context(nc.psum_tensor("a_o", [P, L], F32))
        misc = ctx.enter_context(nc.psum_tensor("a_misc", [P, TPB, P], F32))

        loaded, boot, k_zero, step_ok = sem("a_loaded"), sem("a_boot"), sem("a_k_zero"), sem("a_step_ok")
        xT_mm, xT_ok, qkv_mm, qkv_ok, v_ok, split_ok, cut_ok, chain = map(
            sem, ["a_xT_mm", "a_xT_ok", "a_qkv_mm", "a_qkv_ok", "a_v_ok", "a_split_ok", "a_cut_ok", "a_chain"])
        turnq_mm, turnk_mm, qT_ok, kT_ok, p1_mm, max_ok, m_ok, m_mm, mT_ok, mrow_ok = map(
            sem, ["a_turnq_mm", "a_turnk_mm", "a_qT_ok", "a_kT_ok", "a_p1_mm", "a_max_ok", "a_m_ok", "a_m_mm",
                  "a_mT_ok", "a_mrow_ok"])
        sT_mm, exp_ok, o_mm, oT_ok, back_mm, rden_ok, o_ok, oc_mm, oc_ok, y_mm = map(
            sem, ["a_sT_mm", "a_exp_ok", "a_o_mm", "a_oT_ok", "a_back_mm", "a_rden_ok", "a_o_ok", "a_oc_mm", "a_oc_ok",
                  "a_y_mm"])
        sum_ok, res_ok, bn_ok, mv_ok, eps_ok, rstd_ok, x1_ok, x1T_mm, xw_ok = map(
            sem, ["a_sum_ok", "a_res_ok", "a_bn_ok", "a_mv_ok", "a_eps_ok", "a_rstd_ok", "a_x1_ok", "a_x1T_mm",
                  "a_xw_ok"])

        def upto(eng, s, b, per_batch, count):
            n = b * per_batch + count
            if isinstance(n, int) and n <= 0:
                return
            eng.wait_ge(s, n)

        def run(batch, eng, tail):
            batch(0, False, True)
            with eng.Fori(1, B - 1) as b:
                batch(b, True, True)
            batch(B - 1, True, False)
            if tail is not None:
                tail(B - 1)

        def rows(b):
            return x1_tok[:, bass.ds(b * TPB, TPB), :]

        block = ctx.enter_context(nc.Block())

        @block.sync
        def _(sp):
            sp.dma_start(ident[:], eye).then_inc(loaded, 16)
            sp.dma_start(x1_tok[:], x.rearrange("b (t p) c -> p (b t) c", p=P)).then_inc(loaded, 16)
            sp.dma_start(w_sb[:], wqkvT).then_inc(loaded, 16)
            sp.dma_start(wo_sb[:], woT).then_inc(loaded, 16)
            sp.dma_start(bo_sb[:], bo.broadcast_to([P, C])).then_inc(loaded, 16)
            sp.dma_start(qT[64:AROWS].bitcast(U16), q_const).then_inc(loaded, 16)
            sp.dma_start(kT[64:AROWS].bitcast(U16), k_const).then_inc(loaded, 16)
            sp.dma_start(relu_sb[:].bitcast(U16), relu_const).then_inc(loaded, 16)
            sp.dma_start(slope_sb[:].bitcast(U16), slope_const).then_inc(loaded, 16)

            for to, weights, arrived in first_weights:
                sp.dma_start(to, weights).then_inc(arrived, 16)

            def batch(b, behind, ahead):
                for g in range(4):
                    upto(sp, mT_ok, b, 4, g + 1)
                    for piece in range(3):
                        sp.dma_start(qT[48 + piece:49 + piece, 4 * g:4 * g + 4, :], mT[4 * piece:4 * piece + 4, :]
                                     ).then_inc(mrow_ok, 16)

            run(batch, sp, None)
            sp.wait_ge(mrow_ok, B * 4 * 3 * 16)

        @block.tensor
        def _(pe):
            def first_pass(b, g, units):
                for unit in units:
                    i, h, u = unit // 4, 4 * g + unit % 4, 16 * g + unit
                    upto(pe, max_ok, b, 64, u - 1)
                    out = max_bank[u % 2]
                    pe.matmul(out[:], qT[:, h, i * P:(i + 1) * P], kT[:, h, :], start=True, stop=True)
                    for piece in range(SLOPE_PARTS[h]):
                        last = pe.matmul(out[:, i * P:(i + 1) * P], relu_sb[:, 0, :], slope_sb[:, h, piece, :],
                                         start=False, stop=True, skip_group_check=True)
                    last.then_inc(p1_mm, 1)

            def turn_maxima(b, g):
                upto(pe, m_ok, b, 4, g + 1)
                if g == 0:
                    upto(pe, sum_ok, b, 1, 0)
                elif g == 1:
                    upto(pe, mT_ok, b, 4, 1)
                    upto(pe, xw_ok, b, 1, 0)
                else:
                    upto(pe, o_ok, b, 4, g - 1)
                for t in range(TPB):
                    last = pe.matmul(misc[0:12, 0:2, :].bitcast(BF16).rearrange("p a n -> p (a n)")[
                        :, t * P:(t + 1) * P],
                        m_tok[:, t].rearrange("p a h -> p (a h)"), identb[:], start=True, stop=True,
                        is_transpose=True)
                last.then_inc(m_mm, 1)

            def scores(b, g, j, half):
                if j == 0 and half == 0:
                    pe.wait_ge(mrow_ok, (b * 4 + g + 1) * 48)
                u = 8 * g + 2 * j + half
                upto(pe, exp_ok, b, 32, u - 1)
                for n in range(2):
                    h = 4 * g + 2 * half + n
                    out = sT_bank[:, 2 * half + n, :]
                    pe.matmul(out, kT[:, h, j * P:(j + 1) * P], qT[:, h, :], start=True, stop=True)
                    for piece in range(SLOPE_PARTS[h]):
                        last = pe.matmul(out[:, j * P:(j + 1) * P], relu_sb[:, 1, :], slope_sb[:, h, piece, :],
                                         start=False, stop=True, skip_group_check=True)
                last.then_inc(sT_mm, 1)

            def weigh(b, g, j):
                upto(pe, exp_ok, b, 32, 8 * g + 2 * j + 2)
                if j == 0:
                    upto(pe, oT_ok, b, 4, g)
                for n in range(4):
                    last = pe.matmul(o_bank[32 * n:32 * n + 32, :], v_ext[:, j, 4 * g + n, :],
                                     prob[:, j % 2, n, :], start=(j == 0), stop=(j == TPB - 1),
                                     skip_group_check=True)
                last.then_inc(o_mm, 1)

            def turn_back(b, g):
                upto(pe, oT_ok, b, 4, g + 1)
                upto(pe, mT_ok, b, 4, g + 2 if g < 3 else 4)
                if g == 3:
                    upto(pe, o_ok, b, 4, 3)
                for t in range(TPB):
                    last = pe.matmul(misc[:, t, :], oT[:, t * P:(t + 1) * P], ident[:], start=True, stop=True,
                                     is_transpose=True)
                last.then_inc(back_mm, 1)

            def project(b):
                if b:
                    pe.wait_ge(xT_ok, b)
                for t in range(TPB):
                    last = pe.matmul(misc[:, t, :], x1_tok[:, b * TPB + t, :], ident[:], start=True, stop=True,
                                     is_transpose=True)
                last.then_inc(xT_mm, 1)
                pe.wait_ge(xT_ok, b + 1)
                if b:
                    pe.wait_ge(qkv_ok, 2 * b)
                for t in range(TPB):
                    last = pe.matmul(sT_bank[:, t, 0:3 * C], xT[:, b % 2, t, :], w_sb[:], start=True, stop=True)
                last.then_inc(qkv_mm, 1)

            def turn(b, n):
                if n == 0:
                    upto(pe, split_ok, b, 2, 2)
                    upto(pe, max_ok, b, 64, 0)
                for tok, bank, mm, ok in ((q_tok, max_bank[0], turnq_mm, qT_ok), (k_tok, max_bank[1], turnk_mm, kT_ok)):
                    upto(pe, ok, b, 4, n)
                    for k in range(2):
                        p = 2 * n + k
                        for t in range(TPB):
                            last = pe.matmul(bank[:].bitcast(BF16)[:, (4 * k + t) * P:(4 * k + t + 1) * P],
                                             tok[:, t, 2 * p:2 * p + 2, :].rearrange("p h n -> p (h n)"), identb[:],
                                             start=True, stop=True, is_transpose=True)
                    last.then_inc(mm, 1)

            def turn_outputs(b):
                upto(pe, o_ok, b, 4, 4)
                for t in range(TPB):
                    last = pe.matmul(misc[:, t, :], o_tok[:, t].rearrange("p h d -> p (h d)"), ident[:],
                                     start=True, stop=True, is_transpose=True)
                last.then_inc(oc_mm, 1)

            def project_out(b):
                upto(pe, oc_ok, b, 1, 1)
                for t in range(TPB):
                    last = pe.matmul(misc[:, t, :], ocT[:, t, :], wo_sb[:], start=True, stop=True)
                last.then_inc(y_mm, 1)

            def turn_x1(b):
                upto(pe, x1_ok, b, 1, 1)
                upto(pe, sum_ok, b, 1, 1)
                for t in range(TPB):
                    last = pe.matmul(misc[:, t, :], x1[:, t, :], ident[:], start=True, stop=True, is_transpose=True)
                last.then_inc(x1T_mm, 1)

            def tail(b):
                turn_back(b, 3)
                turn_outputs(b)
                project_out(b)
                turn_x1(b)

            def batch(b, behind, ahead):
                if not behind:
                    pe.wait_ge(qkv_ok, 2 * B)
                    for n in range(4):
                        turn(b, n)
                upto(pe, qT_ok, b, 4, 4)
                upto(pe, kT_ok, b, 4, 4)
                first_pass(b, 0, range(4))
                if behind:
                    turn_back(b - 1, 3)
                first_pass(b, 0, range(4, 8))
                if behind:
                    turn_outputs(b - 1)
                first_pass(b, 0, range(8, 12))
                if behind:
                    project_out(b - 1)
                first_pass(b, 0, range(12, 16))
                turn_maxima(b, 0)
                first_pass(b, 1, range(4))
                for half in range(2):
                    scores(b, 0, 0, half)
                if behind:
                    upto(pe, mT_ok, b, 4, 1)
                    turn_x1(b - 1)
                for g in range(4):
                    for j in range(3):
                        for half in range(2):
                            if g < 3:
                                first_pass(b, g + 1, range(4 * j + 4 + 2 * half, 4 * j + 6 + 2 * half))
                            scores(b, g, j + 1, half)
                        if g == 3 and ahead:
                            turn(b + 1, j)
                        weigh(b, g, j)
                        if j == 0 and g:
                            turn_back(b, g - 1)
                    if g < 3:
                        turn_maxima(b, g + 1)
                    if g < 2:
                        first_pass(b, g + 2, range(4))
                    if g == 3 and ahead:
                        turn(b + 1, 3)
                    weigh(b, g, 3)
                    if g < 3:
                        for half in range(2):
                            scores(b, g + 1, 0, half)

            pe.wait_ge(loaded, 16 * 9)
            pe.wait_ge(boot, 4)
            for b in range(B):
                project(b)
            run(batch, pe, tail)

        @block.scalar
        def _(act):
            def copy(out, in_):
                return act.activation(out, in_, ACT.Copy)

            def turned_x(b):
                act.wait_ge(xT_mm, b + 1)
                if b > 1:
                    act.wait_ge(qkv_mm, b - 1)
                copy(xT[:, b % 2], misc[:]).then_inc(xT_ok, 1)

            def projections(b):
                act.wait_ge(qkv_mm, b + 1)
                copy(qkv[:, b * TPB:b * TPB + 2, :], sT_bank[:, 0:2, 0:3 * C]).then_inc(qkv_ok, 1)

            def tail(b):
                upto(act, oc_mm, b, 1, 1)
                upto(act, y_mm, b, 1, 0)
                copy(ocT[:], misc[:]).then_inc(oc_ok, 1)

            def batch(b, behind, ahead):
                if behind:
                    tail(b - 1)
                upto(act, o_mm, b, 16, 0)
                copy(v_ext[:, :, :, 0:AD], qkv[:, bass.ds(b * TPB, TPB), 2 * C:3 * C].rearrange(
                    "p t (h d) -> p t h d", d=AD)).then_inc(v_ok, 1)
                upto(act, m_mm, b, 4, 1)
                copy(mT[:], turned_maxima).then_inc(mT_ok, 1)
                for g in range(4):
                    for j in range(TPB):
                        for half in range(2):
                            u = 8 * g + 2 * j + half
                            upto(act, sT_mm, b, 32, u + 1)
                            upto(act, o_mm, b, 16, 4 * g + j - 1)
                            act.activation(prob[:, j % 2, 2 * half:2 * half + 2, :],
                                           sT_bank[:, 2 * half:2 * half + 2, :], ACT.Exp).then_inc(exp_ok, 1)
                    if g < 3:
                        upto(act, m_mm, b, 4, g + 2)
                        copy(mT[:], turned_maxima).then_inc(mT_ok, 1)
                    upto(act, o_mm, b, 16, 4 * g + 4)
                    upto(act, back_mm, b, 4, g)
                    copy(oT[:], o_bank[:]).then_inc(oT_ok, 1)

            turned_maxima = misc[0:12, 0:2, :].bitcast(BF16).rearrange("p a n -> p (a n)")
            act.wait_ge(loaded, 16 * 9)
            act.wait_ge(boot, 4)
            for b in range(B):
                turned_x(b)
                projections(b)
            act.wait_ge(qkv_ok, 2 * B)
            run(batch, act, tail)

        @block.gpsimd
        def _(pool):
            pool.memset(x_shift[:], 0.0)
            pool.memset(halfneg[:], -0.5)
            pool.memset(eps[:], LN_EPS)
            pool.memset(factor[:, 0:1], float(AD) ** -0.5)
            pool.memset(factor[:, 1:3], 1.0)
            pool.memset(v_ext[:].rearrange("p t h n -> p (t h n)"), 0.0).then_inc(chain, 1)
            pool.wait_ge(chain, 1)
            pool.memset(v_ext[:, :, :, AD:AD + 1], 1.0).then_inc(boot, 1)

            def times(out, in_, n):
                ones = factor[:, n:n + 1].unsqueeze(2).unsqueeze(3).broadcast_to([P, TPB, AH, AD])
                return pool.tensor_tensor(out, in_, ones, ALU.mult)

            def split(b, part, tok, slots):
                def heads(ap):
                    return ap.rearrange("p t (h d) -> p t h d", d=AD)

                def place(n):
                    return tok[:, :, :, n * AD:(n + 1) * AD]

                high, mid, low = slots
                whole, left = heads(scaled[:, part]), heads(rest[:, part])
                times(whole, heads(qkv[:, bass.ds(b * TPB, TPB), part * C:(part + 1) * C]), part).then_inc(cut_ok, 1)
                upto(pool, cut_ok, b, 8, 4 * part + 1)
                times(place(high[0]), whole, 2).then_inc(cut_ok, 1)
                upto(pool, cut_ok, b, 8, 4 * part + 2)
                pool.tensor_tensor(left, whole, place(high[0]), ALU.subtract).then_inc(cut_ok, 1)
                upto(pool, cut_ok, b, 8, 4 * part + 3)
                times(place(mid[0]), left, 2).then_inc(cut_ok, 1)
                for again in high[1:]:
                    times(place(again), whole, 2)
                for again in mid[1:]:
                    times(place(again), left, 2)
                upto(pool, cut_ok, b, 8, 4 * part + 4)
                pool.tensor_tensor(place(low[0]), left, place(mid[0]), ALU.subtract).then_inc(split_ok, 1)

            def tail(b):
                upto(pool, mv_ok, b, 1, 1)
                upto(pool, x1_ok, b, 1, 0)
                pool.tensor_tensor(rstd[:], mv[:, :, 1], eps[:, 0:TPB], ALU.add).then_inc(eps_ok, 1)
                upto(pool, eps_ok, b, 1, 1)
                pool.tensor_tensor(rstd[:], rstd[:], halfneg[:, 0:TPB], ALU.pow).then_inc(rstd_ok, 1)

            def batch(b, behind, ahead):
                upto(pool, qkv_ok, b, 0 if behind else 2, 2 * B if behind else 2)
                upto(pool, turnk_mm, b, 4, 0)
                split(b, 0, q_tok, ((0, 1, 4), (2, 3), (5,)))
                split(b, 1, k_tok, ((0, 2, 5), (1, 3), (4,)))
                if behind:
                    tail(b - 1)

            pool.wait_ge(boot, 4)
            run(batch, pool, tail)

        @block.vector
        def _(dve):
            def maxima(b, g, units):
                for unit in units:
                    u = 16 * g + unit
                    upto(dve, p1_mm, b, 64, u + 1)
                    if unit == 0:
                        upto(dve, m_ok, b, 4, g)
                    dve.tensor_reduce(negmax[:, unit // 4, unit % 4:unit % 4 + 1], max_bank[u % 2][:], AX.X, ALU.max,
                                      negate=True).then_inc(max_ok, 1)

            def split_maxima(b, g):
                upto(dve, max_ok, b, 64, 16 * g + 16)
                upto(dve, m_mm, b, 4, g)
                n = 3 * g
                dve.tensor_copy(m_tok[:, :, 0, :], negmax[:]).then_inc(step_ok, 1)
                upto(dve, step_ok, b, STEPS, n + 1)
                dve.tensor_tensor(m_rest[:], negmax[:], m_tok[:, :, 0, :], ALU.subtract).then_inc(step_ok, 1)
                upto(dve, step_ok, b, STEPS, n + 2)
                dve.tensor_copy(m_tok[:, :, 1, :], m_rest[:]).then_inc(step_ok, 1)
                upto(dve, step_ok, b, STEPS, n + 3)
                dve.tensor_tensor(m_tok[:, :, 2, :], m_rest[:], m_tok[:, :, 1, :], ALU.subtract).then_inc(m_ok, 1)

            def divide(b, g):
                upto(dve, back_mm, b, 4, g + 1)
                upto(dve, o_ok, b, 4, g)
                src = misc[:].rearrange("p t (h n) -> p t h n", n=32)
                dve.reciprocal(rden[:], src[:, :, :, AD]).then_inc(rden_ok, 1)
                upto(dve, rden_ok, b, 4, g + 1)
                if g == 0:
                    upto(dve, oc_mm, b, 1, 0)
                dve.tensor_tensor(o_tok[:, :, 4 * g:4 * g + 4, :], src[:, :, :, 0:AD],
                                  rden[:].unsqueeze(3).broadcast_to([P, TPB, 4, AD]), ALU.mult).then_inc(o_ok, 1)

            def projections(b):
                dve.wait_ge(qkv_mm, b + 1)
                dve.tensor_copy(qkv[:, b * TPB + 2:(b + 1) * TPB, :], sT_bank[:, 2:4, 0:3 * C]).then_inc(qkv_ok, 1)

            def turned(b, n):
                for turned_to, bank, mm, ok in ((qT, max_bank[0], turnq_mm, qT_ok), (kT, max_bank[1], turnk_mm, kT_ok)):
                    upto(dve, mm, b, 4, n + 1)
                    for a in range(2):
                        src = bank[64 * a:64 * a + 64, :].bitcast(BF16).rearrange("p (k l) -> p k l", k=2)
                        last = dve.tensor_copy(turned_to[0:64, 4 * n + a:4 * n + a + 3:2, :], src)
                    last.then_inc(ok, 1)

            def statistics(b):
                upto(dve, y_mm, b, 1, 1)
                dve.tensor_tensor(total[:], misc[:], rows(b), ALU.add).then_inc(sum_ok, 1)
                upto(dve, sum_ok, b, 1, 1)
                dve.tensor_tensor(total[:], total[:], bo_sb[:].unsqueeze(1).broadcast_to([P, TPB, C]),
                                  ALU.add).then_inc(res_ok, 1)
                upto(dve, res_ok, b, 1, 1)
                upto(dve, rstd_ok, b, 1, 0)
                for t in range(TPB):
                    last = dve.bn_stats(stats[:, t, :], total[:, t, :])
                last.then_inc(bn_ok, 1)
                dve.wait_ge(boot, 4)
                upto(dve, bn_ok, b, 1, 1)
                for t in range(TPB):
                    last = dve.bn_aggr(mv[:, t, :], stats[:, t, :])
                last.then_inc(mv_ok, 1)

            def normalize(b):
                upto(dve, rstd_ok, b, 1, 1)
                upto(dve, x1T_mm, b, 1, 0)
                for t in range(TPB):
                    last = dve.tensor_scalar(x1[:, t, :], total[:, t, :], mv[:, t, 0:1], rstd[:, t:t + 1],
                                             ALU.subtract, ALU.mult)
                last.then_inc(x1_ok, 1)
                upto(dve, x1_ok, b, 1, 1)
                dve.tensor_scalar(rows(b), x1[:], 1.0, None, ALU.mult)

            def shifted(b):
                upto(dve, x1T_mm, b, 1, 1)
                flat = misc[:].rearrange("p t n -> p (t n)")
                dve.tensor_copy(x_shift[0:64, bass.ds(b * XW, L)], flat[0:64])
                dve.tensor_copy(x_shift[64:P, bass.ds(b * XW + 1, L)], flat[64:P]).then_inc(xw_ok, 1)

            def tail(b):
                divide(b, 3)
                statistics(b)
                normalize(b)
                shifted(b)

            def batch(b, behind, ahead):
                if not behind:
                    for n in range(4):
                        turned(b, n)
                maxima(b, 0, range(4))
                if behind:
                    divide(b - 1, 3)
                maxima(b, 0, range(4, 12))
                if behind:
                    statistics(b - 1)
                maxima(b, 0, range(12, 16))
                split_maxima(b, 0)
                if behind:
                    normalize(b - 1)
                maxima(b, 1, range(4))
                if behind:
                    shifted(b - 1)
                for g in range(4):
                    for j in range(3):
                        if g < 3:
                            maxima(b, g + 1, range(4 * j + 4, 4 * j + 8))
                        if g == 3 and ahead:
                            turned(b + 1, j)
                        if j == 0 and g:
                            divide(b, g - 1)
                    if g < 3:
                        split_maxima(b, g + 1)
                    if g < 2:
                        maxima(b, g + 2, range(4))
                    if g == 3 and ahead:
                        turned(b + 1, 3)

            dve.memset(q_tok[:].rearrange("p t h n -> p (t h n)"), 0.0).then_inc(boot, 1)
            dve.memset(k_tok[:].rearrange("p t h n -> p (t h n)"), 0.0).then_inc(k_zero, 1)
            dve.wait_ge(k_zero, 1)
            dve.memset(k_tok[:, :, :, 48:51], 1.0).then_inc(boot, 1)
            dve.wait_ge(loaded, 16 * 9)
            dve.tensor_copy(identb[:], ident[:]).then_inc(boot, 1)
            for b in range(B):
                projections(b)
            run(batch, dve, tail)


def local_layers(nc, args, state, held):
    (wqkv, wo, ffn, qk_scales, rot_base, masks) = args
    x_shift, ident, identb, halfneg, eps = state
    (wqkv_sb, wo_sb, ffn_sb), (qkv_loaded, wo_loaded, ffn_loaded) = held
    with ExitStack() as ctx:
        def sb(name, shape, dt=F32):
            return ctx.enter_context(nc.sbuf_tensor(name, shape, dt))

        def sem(name):
            return ctx.enter_context(nc.semaphore(name))

        w1_sb, w2_sb = ffn_sb[:, 0:2 * FF], ffn_sb[:, 2 * FF:2 * FF + FCH * P]
        b_lin, b_gate = (ffn_sb[:, BIAS + FCH * k:BIAS + FCH * (k + 1)] for k in range(2))
        b2_sb, ln_g, ln_b = (ffn_sb[:, BIAS + 2 * FCH + k:BIAS + 2 * FCH + k + 1] for k in range(3))
        scales_sb = sb("scales_sb", [P, DEPTH, 4 * DH])
        base_sb = sb("base_sb", [P, TPB, 4 * DH])
        mask_sb = sb("mask_sb", [P, 2, 512], BF16)
        tiny = sb("tiny", [P, 1])
        xs = sb("xs", [P, 2, P])
        sq = sb("sq", [P, 2, INNER])
        ssum = sb("ssum", [P, 2, 2, HEADS])
        rlog = sb("rlog", [P, 2, HEADS])
        rnorm = sb("rnorm", [P, 2, 2, HEADS])
        tab = sb("tab", [P, 2, 4 * DH])
        qkn = sb("qkn", [P, 2, INNER])
        t_cos = sb("t_cos", [P, 2, INNER])
        rot = sb("rot", [P, 2, INNER])
        t_sin = sb("t_sin", [P, 2, INNER])
        v_tok = sb("v_tok", [P, 2, INNER])
        v_pad = sb("v_pad", [P, 2, WPT, PAIRS * P])
        qT = sb("qT", [P, PAIRS, P])
        kT = sb("kT", [P, 2, PAIRS, 2, WIN + P])
        s_max = sb("s_max", [P, HEADS])
        s_sub = sb("s_sub", [P, HEADS * 2 * WIN])
        prob = sb("prob", [P, 2, HEADS * 2 * WIN])
        den = sb("den", [P, 2, HEADS])
        rden = sb("rden", [P, 2, HEADS])
        probT = sb("probT", [P, PAIRS, P])
        o_tok = sb("o_tok", [P, INNER])
        oT = sb("oT", [P, PAIRS, P])
        xs2 = sb("xs2", [P, 2, P])
        stats = sb("stats", [P, 6])
        mv = sb("mv", [P, 2])
        rstd = sb("rstd", [P, 1])
        xn = sb("xn", [P, P])
        xnT = sb("xnT", [P, P])
        gelu = sb("gelu", [P, FCH, P])
        hid = sb("hid", [P, FCH, P])
        bank = [ctx.enter_context(nc.psum_tensor(f"bank{i}", [P, 2, 512], F32)) for i in range(4)]
        b01, b23, b45, b67 = bank

        c_loaded = sem("c_loaded")
        q_mm, k_mm, v_mm, qT_mm, kT_mm, s1_mm, s_mm = map(
            sem, ["q_mm", "k_mm", "v_mm", "qT_mm", "kT_mm", "s1_mm", "s_mm"])
        pT_mm, o_mm, oT_mm, y_mm = map(sem, ["pT_mm", "o_mm", "oT_mm", "y_mm"])
        ln_mm, xnT_mm, h_mm, z_mm = map(sem, ["ln_mm", "xnT_mm", "h_mm", "z_mm"])
        xs_ok, sqq_ok, sqk_ok, v_ok, qT_ok, kT_ok = map(sem, ["xs_ok", "sqq_ok", "sqk_ok", "v_ok", "qT_ok", "kT_ok"])
        exp_ok, pT_ok, oT_ok, gelu_ok = map(sem, ["exp_ok", "pT_ok", "oT_ok", "gelu_ok"])
        ssq_ok, ssk_ok, qn_ok, kn_ok, cosq_ok, cosk_ok = map(
            sem, ["ssq_ok", "ssk_ok", "qn_ok", "kn_ok", "cosq_ok", "cosk_ok"])
        max1_ok, max2_ok, sub_ok, den_ok, rden_ok, o_ok, xa_ok, xs2_ok = map(
            sem, ["max1_ok", "max2_ok", "sub_ok", "den_ok", "rden_ok", "o_ok", "xa_ok", "xs2_ok"])
        bn_ok, mv_ok, xn_ok, xnT_ok, hid_ok = map(sem, ["bn_ok", "mv_ok", "xn_ok", "xnT_ok", "hid_ok"])
        xf_ok = sem("xf_ok")
        tab_ok, lnq_ok, rq_ok, lnk_ok, rk_ok, sinq_ok, sink_ok, rotq_ok, rotk_ok, eps_ok, rstd_ok = map(
            sem, ["tab_ok", "lnq_ok", "rq_ok", "lnk_ok", "rk_ok", "sinq_ok", "sink_ok", "rotq_ok", "rotk_ok",
                  "eps_ok", "rstd_ok"])
        vpad_ok, init_ok = [sem("vpad0_ok"), sem("vpad1_ok")], sem("init_ok")

        def done(eng, s, t, back=0, credit=0):
            count = t + 1 - back
            if isinstance(count, int):
                if count <= 0:
                    return
                count = min(count, TILES)
            eng.wait_ge(s, count + credit)

        def behind_constant(eng, s, t):
            eng.wait_ge(c_loaded, 48)
            eng.wait_ge(s, t + 1)

        def spread(eng, t, s):
            if isinstance(t, int) and t < 0:
                return
            eng.wait_ge(vpad_ok[s], (t // 2 + 1) * (16 * 4 * WPT))

        def weights(eng, loaded, t):
            eng.wait_ge(loaded, (t // TPL + 1) * 16)

        def par(t):
            return bass.ds((t // TPL) % 2, 1)

        def run(eng, step):
            for x in range(FIRST):
                step(x, x % 2)
            with eng.Fori(FIRST // 2, TILES // 2) as two:
                step(2 * two, 0)
                step(2 * two + 1, 1)
            for x in range(TILES, TILES + LAG):
                step(x, x % 2)

        def live(t):
            return not isinstance(t, int) or 0 <= t < TILES

        def state_cols(t, lo, hi, shift=0):
            return x_shift[lo:hi, bass.ds(((t // TPB) % B) * XW + (t % TPB) * P + shift, P)]

        block = ctx.enter_context(nc.Block())

        @block.sync
        def _(sp):
            def of(a, layer):
                return a[bass.ds(layer, 1)].rearrange("l p n -> (l p) n")

            def load_qkv(layer):
                sp.dma_start(wqkv_sb[:, bass.ds(layer % 2, 1)].rearrange("p l n -> p (l n)"),
                             of(wqkv, layer)).then_inc(qkv_loaded, 16)

            def load_wo(layer):
                sp.dma_start(wo_sb[:], of(wo, layer)).then_inc(wo_loaded, 16)

            def load_ffn(layer):
                sp.dma_start(ffn_sb[:], of(ffn, layer)).then_inc(ffn_loaded, 16)

            def spread_two(two):
                spread_v(2 * two, 0)
                spread_v(2 * two + 1, 1)

            def layer_of_values(layer, next_qkv):
                first = layer * TPL
                spread_v(first, 0)
                spread_v(first + 1, 1)
                sp.wait_ge(y_mm, first)
                load_wo(layer)
                spread_v(first + 2, 0)
                sp.wait_ge(xf_ok, first + TPL)
                load_ffn(layer)
                if next_qkv:
                    load_qkv(layer + 1)
                spread_v(first + 3, 1)
                with sp.Fori(layer * (TPL // 2) + 2, (layer + 1) * (TPL // 2)) as two:
                    spread_two(two)

            def spread_v(t, s):
                sp.wait_ge(v_ok, t + 1)
                sp.wait_ge(o_mm, t + 1)
                for a in range(2):
                    for w in range(WPT):
                        for c in range(2):
                            src_w = w + c - 1
                            slot = s if src_w >= 0 else 1 - s
                            lo = (src_w % WPT) * WIN
                            dst = v_pad[64 * a + WIN * c:64 * a + WIN * c + WIN, s, w].rearrange(
                                "p (q n) -> p q n", n=P)[:, :, a * DH:(a + 1) * DH]
                            src = v_tok[lo:lo + WIN, slot, a * 512:(a + 1) * 512].rearrange(
                                "p (q n) -> p q n", n=DH)
                            sp.dma_start(dst, src).then_inc(vpad_ok[s], 16)

            sp.dma_start(scales_sb[:], qk_scales.rearrange("a (l n) -> a l n", l=DEPTH).broadcast_to(
                [P, DEPTH, 4 * DH])).then_inc(c_loaded, 16)
            sp.dma_start(base_sb[:], rot_base).then_inc(c_loaded, 16)
            sp.dma_start(mask_sb[:].bitcast(U16), masks).then_inc(c_loaded, 16)
            sp.wait_ge(qkv_loaded, 16)
            load_qkv(1)
            sp.wait_ge(init_ok, 4)
            spread_two(0)
            with sp.Fori(1, TPL // 2) as two:
                spread_two(two)
            with sp.Fori(1, DEPTH - 1) as layer:
                layer_of_values(layer, True)
            layer_of_values(DEPTH - 1, False)

        @block.tensor
        def _(pe):
            def project(t, s, part, out, mm):
                for j in range(2):
                    c = part * INNER + j * 512
                    last = pe.matmul(out[:, j, :], xs[:, s, :],
                                     wqkv_sb[:, par(t), c:c + 512].rearrange("p l n -> p (l n)"),
                                     start=True, stop=True)
                last.then_inc(mm, 1)

            def turn_pairs(out, a, mm):
                for p in range(PAIRS):
                    last = pe.matmul(out[:, p // 4, (p % 4) * P:(p % 4 + 1) * P], a[:, p * P:(p + 1) * P],
                                     ident[:], start=True, stop=True, is_transpose=True)
                last.then_inc(mm, 1)

            def scores(b, r, j):
                which = (b % TPB) // 2 if r == 0 else 1
                pe.matmul(b45[:, j, :], identb[:], mask_sb[:, bass.ds(which, 1), :].rearrange("p l n -> p (l n)"),
                          start=True, stop=False, skip_group_check=True)
                for p in range(4):
                    for w in range(WPT):
                        last = pe.matmul(b45[WIN * w:WIN * w + WIN, j, p * P:(p + 1) * P],
                                         qT[:, 4 * j + p, WIN * w:WIN * w + WIN],
                                         kT[:, r, 4 * j + p, :, WIN * w:WIN * w + 2 * WIN],
                                         start=False, stop=True, skip_group_check=True)
                return last

            def step(x, s):
                a, b, c, e, g = x, x - 1, x - 2, x - 3, x - 4
                r = 1 - s
                if live(a):
                    weights(pe, qkv_loaded, a)
                    done(pe, xs_ok, a)
                    done(pe, o_ok, a, 3)
                    if isinstance(a, int):
                        done(pe, v_ok, a, 1)
                    project(a, s, 0, b01, q_mm)
                    done(pe, oT_ok, a, 3)
                    if isinstance(a, int):
                        done(pe, kn_ok, a, 1)
                    project(a, s, 1, b23, k_mm)
                if live(e):
                    weights(pe, wo_loaded, e)
                    done(pe, oT_ok, e)
                    done(pe, sub_ok, e + 1)
                    for p in range(PAIRS):
                        last = pe.matmul(b45[:, 1, 0:P], wo_sb[:, p * P:(p + 1) * P], oT[:, p, :],
                                         start=(p == 0), stop=(p == PAIRS - 1))
                    last.then_inc(y_mm, 1)
                if live(g):
                    done(pe, hid_ok, g)
                    done(pe, sub_ok, g + 2)
                    for j in range(FCH):
                        n = min(P, FF - j * P)
                        last = pe.matmul(b45[:, 0, 0:P], w2_sb[0:n, j * P:(j + 1) * P], hid[0:n, j, :],
                                         start=(j == 0), stop=(j == FCH - 1))
                    last.then_inc(z_mm, 1)
                if live(b):
                    done(pe, rotk_ok, b)
                    done(pe, hid_ok, b, 3)
                    if isinstance(b, int):
                        done(pe, kT_ok, b, 1)
                    turn_pairs(b67, rot[:, 1], kT_mm)
                if live(a):
                    done(pe, sqq_ok, a)
                    done(pe, qn_ok, a)
                    project(a, s, 2, b01, v_mm)
                if live(b):
                    done(pe, rotq_ok, b)
                    done(pe, xa_ok, b, 2)
                    pe.wait_ge(xf_ok, b - 2 + TPL)
                    if isinstance(b, int):
                        done(pe, sub_ok, b, 1)
                    turn_pairs(b45, rot[:, 0], qT_mm)
                if live(e):
                    done(pe, xs2_ok, e)
                    done(pe, kT_ok, e + 2)
                    pe.matmul(b67[:, 0, 0:P], xs2[:, r, :], ident[:], start=True, stop=True,
                              is_transpose=True).then_inc(ln_mm, 1)
                if live(c):
                    done(pe, exp_ok, c)
                    done(pe, sqk_ok, c + 2)
                    done(pe, kn_ok, c + 2)
                    turn_pairs(b23, prob[:, s], pT_mm)
                if live(b):
                    done(pe, qT_ok, b)
                    done(pe, kT_ok, b)
                    scores(b, r, 0).then_inc(s1_mm, 1)
                    scores(b, r, 1).then_inc(s_mm, 1)
                if live(e):
                    done(pe, xn_ok, e)
                    pe.matmul(b67[:, 1, 0:P], xn[:], ident[:], start=True, stop=True,
                              is_transpose=True).then_inc(xnT_mm, 1)
                if live(c):
                    done(pe, pT_ok, c)
                    done(pe, v_ok, c + 2)
                    spread(pe, c, s)
                    for p in range(PAIRS):
                        for w in range(WPT):
                            last = pe.matmul(b01[WIN * w:WIN * w + WIN, p // 4, (p % 4) * P:(p % 4 + 1) * P],
                                             probT[:, p, WIN * w:WIN * w + WIN],
                                             v_pad[:, s, w, p * P:(p + 1) * P],
                                             start=True, stop=True, skip_group_check=True)
                    last.then_inc(o_mm, 1)
                if live(e):
                    weights(pe, ffn_loaded, e)
                    done(pe, xnT_ok, e)
                    for half in (1, 0):
                        for j in range(FCH):
                            n = min(P, FF - j * P)
                            last = pe.matmul(b67[0:n, half, j * P:(j + 1) * P],
                                             w1_sb[:, half * FF + j * P:half * FF + j * P + n], xnT[:],
                                             start=True, stop=True)
                    last.then_inc(h_mm, 1)
                if live(c):
                    done(pe, o_ok, c)
                    turn_pairs(b23, o_tok[:], oT_mm)

            pe.sem_inc(o_mm, 2)
            pe.wait_ge(c_loaded, 48)
            run(pe, step)

        @block.scalar
        def _(act):
            def copy(out, in_):
                return act.activation(out, in_, ACT.Copy)

            def flat(bank):
                return bank[:].rearrange("p j n -> p (j n)")

            def load_xs(t, s):
                done(act, v_mm, t, 2)
                act.wait_ge(xf_ok, t + 1)
                copy(xs[:, s, :], state_cols(t, 0, P)).then_inc(xs_ok, 1)

            def inv_root(t, s, i, ssum_ok, ln_ok, root_ok):
                done(act, ssum_ok, t)
                act.activation(rlog[:, i, :], ssum[:, s, i, :], ACT.Ln, bias=tiny[:]).then_inc(ln_ok, 1)
                done(act, ln_ok, t)
                act.activation(rnorm[:, s, i, :], rlog[:, i, :], ACT.Exp, scale=-0.5).then_inc(root_ok, 1)

            def turned_keys(r, s, h):
                src = flat(b67)[64 * h:64 * h + 64].rearrange("p (q n) -> p q n", n=P)
                copy(kT[64 * h:64 * h + 64, r, :, h, WIN:WIN + P], src)
                return copy(kT[64 * h:64 * h + 64, s, :, h, 0:WIN], src[:, :, P - WIN:P])

            def step(x, s):
                a, b, c, e = x, x - 1, x - 2, x - 3
                r = 1 - s
                if live(a):
                    done(act, q_mm, a)
                    done(act, ssq_ok, a, 1)
                    act.activation(sq[:, 0, :], flat(b01), ACT.Square).then_inc(sqq_ok, 1)
                act.preload_act_table_set("natural_log_exp_and_others")
                if live(a):
                    inv_root(a, s, 0, ssq_ok, lnq_ok, rq_ok)
                    done(act, k_mm, a)
                    done(act, ssk_ok, a, 1)
                    act.activation(sq[:, 1, :], flat(b23), ACT.Square).then_inc(sqk_ok, 1)
                if live(b):
                    done(act, kT_mm, b)
                    done(act, s_mm, b, 1)
                    turned_keys(r, s, 0)
                if live(a):
                    inv_root(a, s, 1, ssk_ok, lnk_ok, rk_ok)
                if live(b):
                    turned_keys(r, s, 1).then_inc(kT_ok, 1)
                    done(act, qT_mm, b)
                    done(act, s_mm, b, 1)
                    copy(qT[:].rearrange("p q n -> p (q n)"), flat(b45)).then_inc(qT_ok, 1)
                if live(a):
                    done(act, v_mm, a)
                    spread(act, a - 1, r)
                    spread(act, a - 2, s)
                    copy(v_tok[:, s, :], flat(b01)).then_inc(v_ok, 1)
                if live(c):
                    done(act, pT_mm, c)
                    done(act, o_mm, c, 1, credit=2)
                    copy(probT[:].rearrange("p q n -> p (q n)"), flat(b23)).then_inc(pT_ok, 1)
                if not isinstance(a, int) or a + 1 < TILES:
                    load_xs(a + 1, r)
                if live(b):
                    done(act, sub_ok, b)
                    done(act, pT_mm, b, 2)
                    done(act, den_ok, b, 2)
                    act.activation(prob[:, r, :], s_sub[:], ACT.Exp, scale=8.0).then_inc(exp_ok, 1)
                act.preload_act_table(ACT.Gelu)
                if live(c):
                    done(act, oT_mm, c)
                    done(act, y_mm, c, 1)
                    copy(oT[:].rearrange("p q n -> p (q n)"), flat(b23)).then_inc(oT_ok, 1)
                if live(e):
                    weights(act, ffn_loaded, e)
                    done(act, h_mm, e)
                    done(act, hid_ok, e, 1)
                    for j in range(FCH):
                        n = min(P, FF - j * P)
                        last = act.activation(gelu[0:n, j, :], b67[0:n, 1, j * P:(j + 1) * P], ACT.Gelu,
                                              bias=b_gate[0:n, j:j + 1])
                    last.then_inc(gelu_ok, 1)

            load_xs(0, 0)
            act.wait_ge(init_ok, 4)
            run(act, step)

        @block.gpsimd
        def _(pool):
            def add_halves(t, i, sin_ok, cos_ok, mm, rot_ok):
                done(pool, sin_ok, t)
                done(pool, cos_ok, t)
                done(pool, mm, t, 1)
                pool.tensor_tensor(rot[:, i, :], t_cos[:, i, :], t_sin[:, i, :], ALU.add).then_inc(rot_ok, 1)

            def table(t, s):
                done(pool, cosk_ok, t, 2)
                pool.tensor_tensor(tab[:, s, :], base_sb[:, bass.ds(t % TPB, 1), :].rearrange("p l n -> p (l n)"),
                                   scales_sb[:, bass.ds((t // TPL) % DEPTH, 1), :].rearrange("p l n -> p (l n)"),
                                   ALU.mult).then_inc(tab_ok, 1)

            def rotate(t, s, i, n_ok, rot_ok, sin_ok):
                done(pool, n_ok, t)
                src = qkn[:, i, :].rearrange("p (h g n) -> p h g n", g=2, n=DH // 2)
                dst = t_sin[:, i, :].rearrange("p (h g n) -> p h g n", g=2, n=DH // 2)
                for g in range(2):
                    c = (2 * i + 1) * DH + g * (DH // 2)
                    w = tab[:, s, c:c + DH // 2].unsqueeze(1).broadcast_to([P, HEADS, DH // 2])
                    last = pool.tensor_tensor(dst[:, :, g, :], src[:, :, 1 - g, :], w, ALU.mult)
                last.then_inc(sin_ok, 1)

            def step(x, s):
                a, e = x, x - 3
                if live(a):
                    done(pool, tab_ok, a)
                    rotate(a, s, 0, qn_ok, rotq_ok, sinq_ok)
                if live(e):
                    done(pool, mv_ok, e)
                    done(pool, xn_ok, e, 1)
                    pool.tensor_tensor(rstd[:], mv[:, 1:2], eps[:, 0:1], ALU.add).then_inc(eps_ok, 1)
                    done(pool, eps_ok, e)
                    pool.tensor_tensor(rstd[:], rstd[:], halfneg[:, 0:1], ALU.pow).then_inc(rstd_ok, 1)
                if live(a):
                    rotate(a, s, 1, kn_ok, rotk_ok, sink_ok)
                    add_halves(a, 0, sinq_ok, cosq_ok, qT_mm, rotq_ok)
                    add_halves(a, 1, sink_ok, cosk_ok, kT_mm, rotk_ok)
                if not isinstance(a, int) or a + 1 < TILES:
                    table(a + 1, 1 - s)

            pool.memset(tiny[:], 1e-37).then_inc(init_ok, 1)
            pool.memset(v_pad[:].rearrange("p a b c -> p (a b c)"), 0.0).then_inc(init_ok, 1)
            pool.wait_ge(c_loaded, 48)
            table(0, 0)
            run(pool, step)

        @block.vector
        def _(dve):
            def heads(ap, n=DH):
                return ap.rearrange("p (h n) -> p h n", n=n)

            def wide(ap, n=DH):
                return ap.unsqueeze(2).broadcast_to([P, HEADS, n])

            def flat(bank):
                return bank[:].rearrange("p j n -> p (j n)")

            def sum_squares(t, s, i, sq_ok, out_ok):
                done(dve, sq_ok, t)
                dve.tensor_reduce(ssum[:, s, i, :], heads(sq[:, i, :]), AX.X, ALU.add).then_inc(out_ok, 1)

            def normalize(t, s, i, bank, root_ok, n_ok, sin_ok, cos_ok):
                done(dve, root_ok, t)
                done(dve, sin_ok, t, 1)
                done(dve, cos_ok, t, 1)
                dve.scalar_tensor_tensor(heads(qkn[:, i, :]), wide(rnorm[:, s, i, :]), 1e12, heads(flat(bank)),
                                         ALU.min, ALU.mult).then_inc(n_ok, 1)

            def cosine(t, s, i, n_ok, rot_ok, cos_ok):
                done(dve, n_ok, t)
                done(dve, rot_ok, t, 1)
                w = tab[:, s, 2 * i * DH:(2 * i + 1) * DH].unsqueeze(1).broadcast_to([P, HEADS, DH])
                dve.tensor_tensor(heads(t_cos[:, i, :]), heads(qkn[:, i, :]), w, ALU.mult).then_inc(cos_ok, 1)

            def row_maxima(t, j, mm, out_ok):
                done(dve, mm, t)
                dve.tensor_reduce(s_max[:, 8 * j:8 * j + 8], heads(b45[:, j, :]), AX.X, ALU.max).then_inc(out_ok, 1)

            def less_maxima(t, j, m_ok):
                done(dve, m_ok, t)
                done(dve, exp_ok, t, 1)
                return dve.tensor_tensor(heads(s_sub[:, 512 * j:512 * j + 512]), heads(b45[:, j, :]),
                                         s_max[:, 8 * j:8 * j + 8].unsqueeze(2).broadcast_to([P, 8, DH]), ALU.subtract)

            def step(x, s):
                a, b, c, e, g = x, x - 1, x - 2, x - 3, x - 4
                r = 1 - s
                if live(a):
                    sum_squares(a, s, 0, sqq_ok, ssq_ok)
                    normalize(a, s, 0, b01, rq_ok, qn_ok, sinq_ok, cosq_ok)
                if live(e):
                    done(dve, y_mm, e)
                    if not isinstance(e, int) or e + 1 < TILES:
                        done(dve, xs_ok, e + 1)
                    done(dve, xs2_ok, e, 1)
                    lo, hi = state_cols(e, 0, 64), state_cols(e, 64, P, 1)
                    dve.tensor_tensor(lo, b45[0:64, 1, 0:P], lo, ALU.add)
                    dve.tensor_tensor(hi, b45[64:P, 1, 0:P], hi, ALU.add).then_inc(xa_ok, 1)
                if live(a):
                    sum_squares(a, s, 1, sqk_ok, ssk_ok)
                if live(e):
                    done(dve, xa_ok, e)
                    done(dve, ln_mm, e, 2)
                    dve.tensor_scalar(xs2[:, r, :], state_cols(e, 0, P), 1.0, None, ALU.mult).then_inc(xs2_ok, 1)
                if live(g):
                    done(dve, z_mm, g)
                    if not isinstance(g, int) or g + 1 < TILES:
                        done(dve, xs2_ok, g + 1)
                    lo, hi = state_cols(g, 0, 64), state_cols(g, 64, P, 1)
                    dve.scalar_tensor_tensor(lo, b45[0:64, 0, 0:P], b2_sb[0:64], lo, ALU.add, ALU.add)
                    dve.scalar_tensor_tensor(hi, b45[64:P, 0, 0:P], b2_sb[64:P], hi, ALU.add,
                                             ALU.add).then_inc(xf_ok, 1)
                if live(a):
                    normalize(a, s, 1, b23, rk_ok, kn_ok, sink_ok, cosk_ok)
                    done(dve, tab_ok, a)
                    cosine(a, s, 0, qn_ok, rotq_ok, cosq_ok)
                if live(e):
                    done(dve, ln_mm, e)
                    done(dve, rstd_ok, e, 1)
                    dve.bn_stats(stats[:], b67[:, 0, 0:P]).then_inc(bn_ok, 1)
                    behind_constant(dve, bn_ok, e)
                    dve.bn_aggr(mv[:], stats[:]).then_inc(mv_ok, 1)
                if live(a):
                    cosine(a, s, 1, kn_ok, rotk_ok, cosk_ok)
                if live(e):
                    done(dve, rstd_ok, e)
                    done(dve, xnT_mm, e, 1)
                    dve.tensor_scalar(xn[:], b67[:, 0, 0:P], mv[:, 0:1], rstd[:], ALU.subtract,
                                      ALU.mult).then_inc(xn_ok, 1)
                if live(b):
                    row_maxima(b, 0, s1_mm, max1_ok)
                    less_maxima(b, 0, max1_ok)
                if live(b):
                    row_maxima(b, 1, s_mm, max2_ok)
                if live(e):
                    weights(dve, ffn_loaded, e)
                    done(dve, xnT_mm, e)
                    done(dve, h_mm, e, 1)
                    dve.tensor_scalar(xnT[:], b67[:, 1, 0:P], ln_g, ln_b, ALU.mult, ALU.add).then_inc(xnT_ok, 1)
                if live(b):
                    less_maxima(b, 1, max2_ok).then_inc(sub_ok, 1)
                if live(c):
                    done(dve, o_mm, c, credit=2)
                    done(dve, rden_ok, c)
                    done(dve, oT_mm, c, 1)
                    dve.tensor_tensor(heads(o_tok[:]), heads(flat(b01)), wide(rden[:, s, :]),
                                      ALU.mult).then_inc(o_ok, 1)
                if live(b):
                    done(dve, exp_ok, b)
                    dve.tensor_reduce(den[:, r, :], heads(prob[:, r, :]), AX.X, ALU.add).then_inc(den_ok, 1)
                    done(dve, den_ok, b)
                    dve.reciprocal(rden[:, r, :], den[:, r, :]).then_inc(rden_ok, 1)
                if live(e):
                    done(dve, gelu_ok, e)
                    done(dve, z_mm, e, 1)
                    for j in range(FCH):
                        n = min(P, FF - j * P)
                        last = dve.scalar_tensor_tensor(hid[0:n, j, :], b67[0:n, 0, j * P:(j + 1) * P],
                                                        b_lin[0:n, j:j + 1], gelu[0:n, j, :], ALU.add, ALU.mult)
                    last.then_inc(hid_ok, 1)

            dve.sem_inc(xf_ok, TPL)
            dve.memset(kT[:].rearrange("p a b c d -> p (a b c d)"), 0.0).then_inc(init_ok, 1)
            dve.memset(v_tok[:].rearrange("p a b -> p (a b)"), 0.0).then_inc(init_ok, 1)
            dve.wait_ge(c_loaded, 48)
            run(dve, step)


def last_norm(nc, out, x_shift, x1_tok, ident, halfneg, eps):
    out_v = out.rearrange("b (t p) c -> b p t c", p=P)
    with ExitStack() as ctx:
        def sb(name, shape, dt=F32):
            return ctx.enter_context(nc.sbuf_tensor(name, shape, dt))

        def sem(name):
            return ctx.enter_context(nc.semaphore(name))

        feat = sb("feat", [P, TPB, P])
        total = sb("total", [P, TPB, P])
        stats = sb("f_stats", [P, TPB, 6])
        mv = sb("f_mv", [P, TPB, 2])
        rstd = sb("f_rstd", [P, TPB])
        y = sb("f_y", [P, B, TPB, P])
        turned = ctx.enter_context(nc.psum_tensor("f_turned", [P, TPB, P], F32))
        feat_ok, turn_mm, sum_ok, bn_ok, mv_ok, eps_ok, rstd_ok, y_ok, stored = map(
            sem, ["feat_ok", "turn_mm", "sum_ok", "f_bn_ok", "f_mv_ok", "f_eps_ok", "f_rstd_ok", "f_y_ok", "stored"])
        block = ctx.enter_context(nc.Block())

        @block.scalar
        def _(act):
            for b in range(B):
                if b:
                    act.wait_ge(turn_mm, b)
                act.activation(feat[0:64].rearrange("p t n -> p (t n)"), x_shift[0:64, b * XW:b * XW + L], ACT.Copy)
                act.activation(feat[64:P].rearrange("p t n -> p (t n)"), x_shift[64:P, b * XW + 1:b * XW + 1 + L],
                               ACT.Copy).then_inc(feat_ok, 1)

        @block.tensor
        def _(pe):
            for b in range(B):
                pe.wait_ge(feat_ok, b + 1)
                if b:
                    pe.wait_ge(sum_ok, b)
                for t in range(TPB):
                    last = pe.matmul(turned[:, t, :], feat[:, t, :], ident[:], start=True, stop=True,
                                     is_transpose=True)
                last.then_inc(turn_mm, 1)

        @block.vector
        def _(dve):
            for b in range(B):
                dve.wait_ge(turn_mm, b + 1)
                if b:
                    dve.wait_ge(y_ok, b)
                dve.tensor_tensor(total[:], turned[:], x1_tok[:, b * TPB:(b + 1) * TPB, :], ALU.add).then_inc(sum_ok, 1)
                dve.wait_ge(sum_ok, b + 1)
                for t in range(TPB):
                    last = dve.bn_stats(stats[:, t, :], total[:, t, :])
                last.then_inc(bn_ok, 1)
                dve.wait_ge(bn_ok, b + 1)
                for t in range(TPB):
                    last = dve.bn_aggr(mv[:, t, :], stats[:, t, :])
                last.then_inc(mv_ok, 1)
                dve.wait_ge(rstd_ok, b + 1)
                for t in range(TPB):
                    last = dve.tensor_scalar(y[:, b, t, :], total[:, t, :], mv[:, t, 0:1], rstd[:, t:t + 1],
                                             ALU.subtract, ALU.mult)
                last.then_inc(y_ok, 1)

        @block.gpsimd
        def _(pool):
            for b in range(B):
                pool.wait_ge(mv_ok, b + 1)
                if b:
                    pool.wait_ge(y_ok, b)
                pool.tensor_tensor(rstd[:], mv[:, :, 1], eps[:], ALU.add).then_inc(eps_ok, 1)
                pool.wait_ge(eps_ok, b + 1)
                pool.tensor_tensor(rstd[:], rstd[:], halfneg[:, 0:TPB], ALU.pow).then_inc(rstd_ok, 1)

        @block.sync
        def _(sp):
            for b in range(B):
                sp.wait_ge(y_ok, b + 1)
                sp.dma_start(out_v[b], y[:, b]).then_inc(stored, 16)
            sp.wait_ge(stored, 16 * B)


def bf16_bits(a):
    return (np.ascontiguousarray(a, dtype=np.float32).view(np.uint32) >> 16).astype(np.uint16)


def rotary_base():
    half = np.arange(0, DH, 2, dtype=np.float32)
    inv_freq = (np.float32(1.0) / np.power(np.float32(10000.0), half / np.float32(DH))).astype(np.float32)
    t = np.arange(L, dtype=np.float32)
    freqs = t[:, None] * inv_freq[None, :]
    freqs = np.concatenate([freqs, freqs], -1)
    base = (half + np.float32(0.4 * DH)) / np.float32(1.4 * DH)
    power = (t - L // 2) / np.float32(WIN // 2)
    scale = np.power(base[None, :], power[:, None]).astype(np.float32)
    scale = np.concatenate([scale, scale], -1)
    sign = np.concatenate([-np.ones(DH // 2), np.ones(DH // 2)]).astype(np.float32)
    cos, sin = np.cos(freqs), np.sin(freqs) * sign
    inv = np.float32(1.0) / scale
    rows = np.concatenate([cos * scale, sin * scale, cos * inv, sin * inv], -1).astype(np.float32)
    return np.ascontiguousarray(rows.reshape(TPB, P, 4 * DH).transpose(1, 0, 2))


def window_masks():
    i = np.arange(P)[:, None] % WIN
    j = np.arange(2 * WIN)[None, :]
    ok = (j >= i) & (j <= i + WIN)
    first = ok & ~((np.arange(P)[:, None] < WIN) & (j < WIN))
    low = np.float32(-(2.0 ** 100))
    rows = np.stack([np.tile(np.where(m, np.float32(0), low), (1, 8)) for m in (first, ok)], 1)
    return bf16_bits(rows)


def three_parts(a):
    out, a = [], np.asarray(a, dtype=np.float64)
    for _ in range(3):
        part = (a.astype(np.float32).view(np.uint32) & np.uint32(0xFFFF0000)).view(np.float32)
        out.append(part)
        a = a - part
    return out


def alibi_slopes():
    start = 2.0 ** (-2.0 ** (-(np.log2(AH) - 3)))
    return np.array([start * start ** i for i in range(AH)], dtype=np.float32)


def alibi_rows():
    slope = alibi_slopes().astype(np.float64)[:, None]
    pos = np.arange(L)
    tile, inside = pos // P, pos % P
    q_rows, k_rows = [], []
    for i in range(TPB):
        here = (tile == i)[None, :]
        sign = np.where(i > tile, -1.0, 1.0)
        back = np.where(tile > i, -1.0, 1.0)
        for part in three_parts(slope * inside):
            q_rows.append(part * here)
            k_rows.append(np.broadcast_to(sign, (AH, L)))
            q_rows.append(np.broadcast_to(-back, (AH, L)))
            k_rows.append(part * here)
        for part in three_parts(np.broadcast_to(slope, (AH, L))):
            q_rows.append(part * here)
            k_rows.append(np.broadcast_to(-float(P) * np.abs(i - tile), (AH, L)))
    return bf16_bits(np.stack(q_rows)), bf16_bits(np.stack(k_rows))


def alibi_inside():
    k, m = np.arange(P)[:, None], np.arange(P)[None, :]
    relu = np.stack([np.maximum(m - k, 0), np.maximum(k - m, 0)], 1).astype(np.float16).view(np.uint16)
    value = -2.0 * alibi_slopes().astype(np.float64)
    high = value.astype(np.float16)
    low = (value - high).astype(np.float16)
    diag = np.eye(P)[:, None, None, :] * np.stack([high, low], 1)[None, :, :, None]
    return relu, diag.astype(np.float16).view(np.uint16)




def attention_then_local_layers(nc, A, out):
    with ExitStack() as ctx:
        def sb(name, shape, dt=F32):
            return ctx.enter_context(nc.sbuf_tensor(name, shape, dt))

        ident = sb("ident", [P, P])
        identb = sb("identb", [P, P], BF16)
        halfneg = sb("halfneg", [P, HEADS])
        eps = sb("eps", [P, TPB])
        wqkv_sb = sb("wqkv_sb", [P, 2, 3 * INNER])
        wo_sb = sb("wo_sb", [P, PAIRS * P])
        ffn_sb = sb("ffn_sb", [P, FFN_COLS])
        loaded = [ctx.enter_context(nc.semaphore(n)) for n in ("qkv_loaded", "wo_loaded", "ffn_loaded")]
        first_weights = [(wqkv_sb[:, 0], A["wqkv"][0], loaded[0]), (wo_sb[:], A["wo"][0], loaded[1]),
                         (ffn_sb[:], A["ffn"][0], loaded[2])]
        x_shift = sb("x_shift", [P, B * XW])
        x1_tok = sb("x1_tok", [P, TPL, P])
        alibi_attention(nc, (A["x"], A["eye"], A["a_wqkv"], A["a_wo"], A["a_bo"], A["q_const"], A["k_const"],
                             A["relu_const"], A["slope_const"]), (x_shift, x1_tok, ident, identb, halfneg, eps),
                        first_weights)
        local_layers(nc, (A["wqkv"], A["wo"], A["ffn"], A["scales"], A["rot"], A["masks"]),
                     (x_shift, ident, identb, halfneg, eps), ((wqkv_sb, wo_sb, ffn_sb), loaded))
        last_norm(nc, out, x_shift, x1_tok, ident, halfneg, eps)


def laid_out(i):
    def swapped(a):
        return np.concatenate([a[:, DH // 2:], a[:, :DH // 2]], -1)

    a = {"x": i["L0_attn_q"]}
    a["a_wqkv"] = np.concatenate([i[n].T for n in ("L0_attn_Wq", "L0_attn_Wk", "L0_attn_Wv")], 1)
    a["a_wo"] = i["L0_attn_Wo"].T
    a["a_bo"] = i["L0_attn_bo"].reshape(1, C)
    wqkv = i["L0_ffn_Wqkv"]
    v = wqkv[:, :, 2 * INNER:].reshape(DEPTH, C, PAIRS, 2, DH).transpose(0, 1, 3, 2, 4).reshape(DEPTH, C, INNER)
    a["wqkv"] = np.concatenate([wqkv[:, :, :2 * INNER], v], -1)
    a["wo"] = i["L0_ffn_Wo"].reshape(DEPTH, PAIRS, P, C).transpose(0, 2, 1, 3).reshape(DEPTH, P, PAIRS * C)
    pad = FCH * P - FF
    w2 = np.concatenate([i["L0_ffn_W2"], np.zeros((DEPTH, pad, C), np.float32)], 1)
    w2 = w2.reshape(DEPTH, FCH, P, C).transpose(0, 2, 1, 3).reshape(DEPTH, P, FCH * C)
    b1 = np.concatenate([i["L0_ffn_b1"].reshape(DEPTH, 2, FF), np.zeros((DEPTH, 2, pad), np.float32)], -1)
    b1 = b1.reshape(DEPTH, 2 * FCH, P).transpose(0, 2, 1)
    columns = [i[n][:, :, None] for n in ("L0_ffn_b2", "L0_ffn_ln_g", "L0_ffn_ln_b")]
    a["ffn"] = np.concatenate([i["L0_ffn_W1"], w2, b1] + columns, -1)
    q, k = i["L0_ffn_q_scale"], i["L0_ffn_k_scale"]
    a["scales"] = np.concatenate([q, swapped(q), k, swapped(k)], -1).reshape(1, -1)
    a["eye"] = np.eye(P, dtype=np.float32)
    a["rot"], a["masks"] = rotary_base(), window_masks()
    a["q_const"], a["k_const"] = alibi_rows()
    a["relu_const"], a["slope_const"] = alibi_inside()
    return {n: np.ascontiguousarray(v) for n, v in a.items()}


def kernel(**inputs):
    import concourse.bacc as bacc
    from concourse.bass_utils import run_bass_kernel_spmd

    nc = bacc.Bacc("TRN2", target_bir_lowering=False, num_devices=1)
    arrays = {f"in_{n}": v for n, v in laid_out({n: np.asarray(v) for n, v in inputs.items()}).items()}
    A = {n[3:]: nc.dram_tensor(n, v.shape, mybir.dt.from_np(v.dtype), kind="ExternalInput").ap()
         for n, v in arrays.items()}
    out = nc.dram_tensor("out_0", (B, L, C), F32, kind="ExternalOutput").ap()
    attention_then_local_layers(nc, A, out)
    r = run_bass_kernel_spmd(nc, [arrays], core_ids=[0])
    return r.results[0]["out_0"]
```
